# Optimizing a Trainium2 kernel written in Bass

```python
import numpy as np
import jax
import jax.numpy as jnp

def _softmax(x, axis=-1):
    return jax.nn.softmax(x, axis=axis)
def _gelu(x):
    return jax.nn.gelu(x, approximate=True)
def _silu(x):
    return jax.nn.silu(x)
def _sigmoid(x):
    return jax.nn.sigmoid(x)
def _layernorm(x, axis=-1, eps=1e-5):
    m = jnp.mean(x, axis=axis, keepdims=True)
    v = jnp.var(x, axis=axis, keepdims=True)
    return (x - m) / jnp.sqrt(v + eps)
def _scatter_add(tgt, idx, src, axis=0):
    return tgt.at[idx].add(src)
def _segment_sum(src, seg, n):
    return jax.ops.segment_sum(src, seg, n)

kernel_name = 'mk_conv_seq_d2_conv_nchw512_c60adc'

def setup_inputs(seed: int = 0):
    np.random.seed(seed)
    _w = jnp.asarray
    def _rec_inputs():
        import jax
        import jax.numpy as jnp
        _gk = jax.random.key(seed)
        x = -0.000929 + 1 * jax.random.normal(jax.random.fold_in(_gk, 1), (2, 512, 32, 32), jnp.float32)
        return x
    x = _rec_inputs()
    def _L0_conv_setup():
        import jax, jax.numpy as jnp
        import numpy as np
        B, C, H, W = (2, 512, 32, 32)
        HEADS = 8
        GROUPS = 8
        DH = 64
        DF = 4
        OFF_SCALE = 4.0
        EPS = 1e-05

        def _bn(t, gamma, beta):
            s = gamma / jnp.sqrt(1.0 + EPS)
            return t * s[None, :, None, None] + beta[None, :, None, None]

        def _gconv1x1(t, w):
            b, c, h, ww = t.shape
            o = jnp.einsum('bgci,goc->bgoi', t.reshape(b, GROUPS, c // GROUPS, h * ww), w)
            return o.reshape(b, GROUPS * w.shape[1], h, ww)

        def _grid_sample(img, grid):
            N, Ci, Hi, Wi = img.shape
            gx = (grid[..., 0] + 1.0) * (Wi / 2.0) - 0.5
            gy = (grid[..., 1] + 1.0) * (Hi / 2.0) - 0.5
            x0 = jnp.floor(gx)
            y0 = jnp.floor(gy)
            wx = gx - x0
            wy = gy - y0

            def gather(im, ix, iy):
                valid = (ix >= 0) & (ix < Wi) & (iy >= 0) & (iy < Hi)
                ixc = jnp.clip(ix, 0, Wi - 1).astype(jnp.int32)
                iyc = jnp.clip(iy, 0, Hi - 1).astype(jnp.int32)
                return im[:, iyc, ixc] * valid[None].astype(im.dtype)

            def sample_one(im, x0, y0, wx, wy):
                v00 = gather(im, x0, y0)
                v01 = gather(im, x0 + 1, y0)
                v10 = gather(im, x0, y0 + 1)
                v11 = gather(im, x0 + 1, y0 + 1)
                wx = wx[None]
                wy = wy[None]
                return v00 * (1 - wx) * (1 - wy) + v01 * wx * (1 - wy) + v10 * (1 - wx) * wy + v11 * wx * wy
            return jax.vmap(sample_one)(img, x0, y0, wx, wy)

        def _forward(x, bn1_g, bn1_b, bn2_g, bn2_b, qw, kw, vw, out_w, out_b, off_dw_w, off_dw_b, off_pw_w, cpb_w1, cpb_b1, cpb_w2, cpb_b2, cpb_w3, cpb_b3, mlp_w1, mlp_b1, mlp_w2, mlp_b2):
            b = x.shape[0]
            xn = _bn(x, bn1_g, bn1_b)
            q = _gconv1x1(xn, qw)
            qg = q.reshape(b * GROUPS, DH, H, W)
            off = jax.lax.conv_general_dilated(qg, off_dw_w, (DF, DF), ((1, 1), (1, 1)), dimension_numbers=('NCHW', 'OIHW', 'NCHW'), feature_group_count=DH)
            off = jax.nn.gelu(off + off_dw_b[None, :, None, None], approximate=False)
            off = jnp.tanh(jnp.einsum('bchw,oc->bohw', off, off_pw_w)) * OFF_SCALE
            Hd, Wd = (off.shape[-2], off.shape[-1])
            gy, gx = jnp.meshgrid(jnp.arange(Hd, dtype=x.dtype), jnp.arange(Wd, dtype=x.dtype), indexing='ij')
            vx = gx[None] + off[:, 0]
            vy = gy[None] + off[:, 1]
            nx = 2.0 * vx / max(Hd - 1, 1) - 1.0
            ny = 2.0 * vy / max(Wd - 1, 1) - 1.0
            vgrid_scaled = jnp.stack((nx, ny), axis=-1)
            kv = _grid_sample(xn.reshape(b * GROUPS, DH, H, W), vgrid_scaled)
            kv = kv.reshape(b, GROUPS * DH, Hd, Wd)
            k = _gconv1x1(kv, kw)
            v = _gconv1x1(kv, vw)
            scale = DH ** (-0.5)
            qh = q.reshape(b, HEADS, DH, H * W).transpose(0, 1, 3, 2) * scale
            kh = k.reshape(b, HEADS, DH, Hd * Wd).transpose(0, 1, 3, 2)
            vh = v.reshape(b, HEADS, DH, Hd * Wd).transpose(0, 1, 3, 2)
            qgy, qgx = jnp.meshgrid(jnp.arange(H, dtype=x.dtype), jnp.arange(W, dtype=x.dtype), indexing='ij')
            grid_q = jnp.stack((2.0 * qgx / max(H - 1, 1) - 1.0, 2.0 * qgy / max(W - 1, 1) - 1.0), axis=-1).reshape(1, H * W, 2)
            grid_kv = vgrid_scaled.reshape(b * GROUPS, Hd * Wd, 2)
            pos = grid_q[:, :, None, :] - grid_kv[:, None, :, :]
            bias = jnp.sign(pos) * jnp.log1p(jnp.abs(pos))
            bias = jax.nn.relu(bias @ cpb_w1 + cpb_b1)
            bias = jax.nn.relu(bias @ cpb_w2 + cpb_b2)
            bias = (bias @ cpb_w3 + cpb_b3).reshape(b, GROUPS, H * W, Hd * Wd)
            sim = jnp.einsum('bhid,bhjd->bhij', qh, kh) + bias
            attn = jax.nn.softmax(sim, axis=-1)
            out = jnp.einsum('bhij,bhjd->bhid', attn, vh)
            out = out.transpose(0, 1, 3, 2).reshape(b, HEADS * DH, H, W)
            out = jnp.einsum('bchw,oc->bohw', out, out_w) + out_b[None, :, None, None]
            x = x + out
            xn2 = _bn(x, bn2_g, bn2_b)
            h1 = jax.nn.gelu(jnp.einsum('bchw,oc->bohw', xn2, mlp_w1) + mlp_b1[None, :, None, None], approximate=False)
            return x + jnp.einsum('bchw,oc->bohw', h1, mlp_w2) + mlp_b2[None, :, None, None]
        ks = jax.random.split(jax.random.key(seed), 16)
        w = lambda k, shape: jax.random.normal(k, shape, dtype=jnp.float32) * 0.02
        return {'x': jax.random.normal(ks[0], (B, C, H, W), dtype=jnp.float32), 'bn1_g': jnp.ones((C,), jnp.float32), 'bn1_b': jnp.zeros((C,), jnp.float32), 'bn2_g': jnp.ones((C,), jnp.float32), 'bn2_b': jnp.zeros((C,), jnp.float32), 'qw': w(ks[1], (GROUPS, DH, C // GROUPS)), 'kw': w(ks[2], (GROUPS, DH, C // GROUPS)), 'vw': w(ks[3], (GROUPS, DH, C // GROUPS)), 'out_w': w(ks[4], (C, HEADS * DH)), 'out_b': jnp.zeros((C,), jnp.float32), 'off_dw_w': w(ks[5], (DH, 1, 6, 6)), 'off_dw_b': jnp.zeros((DH,), jnp.float32), 'off_pw_w': w(ks[6], (2, DH)), 'cpb_w1': w(ks[7], (2, 128)), 'cpb_b1': jnp.zeros((128,), jnp.float32), 'cpb_w2': w(ks[8], (128, 128)), 'cpb_b2': jnp.zeros((128,), jnp.float32), 'cpb_w3': w(ks[9], (128, 1)), 'cpb_b3': jnp.zeros((1,), jnp.float32), 'mlp_w1': w(ks[10], (4 * C, C)), 'mlp_b1': jnp.zeros((4 * C,), jnp.float32), 'mlp_w2': w(ks[11], (C, 4 * C)), 'mlp_b2': jnp.zeros((C,), jnp.float32)}
    _L0_conv_all = _L0_conv_setup()
    _L0_conv_in = {k: v for k, v in _L0_conv_all.items() if k in ('bn1_g', 'bn1_b', 'bn2_g', 'bn2_b', 'qw', 'kw', 'vw', 'out_w', 'out_b', 'off_dw_w', 'off_dw_b', 'off_pw_w', 'cpb_w1', 'cpb_b1', 'cpb_w2', 'cpb_b2', 'cpb_w3', 'cpb_b3', 'mlp_w1', 'mlp_b1', 'mlp_w2', 'mlp_b2', )}
    del _L0_conv_all

    def _L1_conv_setup():
        import jax, jax.numpy as jnp
        import numpy as np
        import math
        C = 512
        N_HEADS = 8
        N_GROUPS = 32
        EPS = 1e-05
        key = jax.random.key(seed)
        k1, k2, k3 = jax.random.split(key, 3)
        B, H, W = (4, 48, 48)
        x = jax.random.normal(k1, (B, C, H, W), dtype=jnp.float32)
        gn_w = jnp.ones((C,), jnp.float32)
        gn_b = jnp.zeros((C,), jnp.float32)
        qkv_w = jax.random.normal(k2, (3 * C, C), jnp.float32) * (1.0 / math.sqrt(C))
        qkv_b = jnp.zeros((3 * C,), jnp.float32)
        proj_w = jax.random.normal(k3, (C, C), jnp.float32) * (1.0 / math.sqrt(C))
        proj_b = jnp.zeros((C,), jnp.float32)
        return {'x': x, 'gn_w': gn_w, 'gn_b': gn_b, 'qkv_w': qkv_w, 'qkv_b': qkv_b, 'proj_w': proj_w, 'proj_b': proj_b}
    _L1_conv_all = _L1_conv_setup()
    _L1_conv_in = {k: v for k, v in _L1_conv_all.items() if k in ('gn_w', 'gn_b', 'qkv_w', 'qkv_b', 'proj_w', 'proj_b', )}
    del _L1_conv_all

    return {
        "x": x,
        "L0_conv_bn1_g": _L0_conv_in["bn1_g"],
        "L0_conv_bn1_b": _L0_conv_in["bn1_b"],
        "L0_conv_bn2_g": _L0_conv_in["bn2_g"],
        "L0_conv_bn2_b": _L0_conv_in["bn2_b"],
        "L0_conv_qw": _L0_conv_in["qw"],
        "L0_conv_kw": _L0_conv_in["kw"],
        "L0_conv_vw": _L0_conv_in["vw"],
        "L0_conv_out_w": _L0_conv_in["out_w"],
        "L0_conv_out_b": _L0_conv_in["out_b"],
        "L0_conv_off_dw_w": _L0_conv_in["off_dw_w"],
        "L0_conv_off_dw_b": _L0_conv_in["off_dw_b"],
        "L0_conv_off_pw_w": _L0_conv_in["off_pw_w"],
        "L0_conv_cpb_w1": _L0_conv_in["cpb_w1"],
        "L0_conv_cpb_b1": _L0_conv_in["cpb_b1"],
        "L0_conv_cpb_w2": _L0_conv_in["cpb_w2"],
        "L0_conv_cpb_b2": _L0_conv_in["cpb_b2"],
        "L0_conv_cpb_w3": _L0_conv_in["cpb_w3"],
        "L0_conv_cpb_b3": _L0_conv_in["cpb_b3"],
        "L0_conv_mlp_w1": _L0_conv_in["mlp_w1"],
        "L0_conv_mlp_b1": _L0_conv_in["mlp_b1"],
        "L0_conv_mlp_w2": _L0_conv_in["mlp_w2"],
        "L0_conv_mlp_b2": _L0_conv_in["mlp_b2"],
        "L1_conv_gn_w": _L1_conv_in["gn_w"],
        "L1_conv_gn_b": _L1_conv_in["gn_b"],
        "L1_conv_qkv_w": _L1_conv_in["qkv_w"],
        "L1_conv_qkv_b": _L1_conv_in["qkv_b"],
        "L1_conv_proj_w": _L1_conv_in["proj_w"],
        "L1_conv_proj_b": _L1_conv_in["proj_b"],
    }

def reference(x, L0_conv_bn1_g, L0_conv_bn1_b, L0_conv_bn2_g, L0_conv_bn2_b, L0_conv_qw, L0_conv_kw, L0_conv_vw, L0_conv_out_w, L0_conv_out_b, L0_conv_off_dw_w, L0_conv_off_dw_b, L0_conv_off_pw_w, L0_conv_cpb_w1, L0_conv_cpb_b1, L0_conv_cpb_w2, L0_conv_cpb_b2, L0_conv_cpb_w3, L0_conv_cpb_b3, L0_conv_mlp_w1, L0_conv_mlp_b1, L0_conv_mlp_w2, L0_conv_mlp_b2, L1_conv_gn_w, L1_conv_gn_b, L1_conv_qkv_w, L1_conv_qkv_b, L1_conv_proj_w, L1_conv_proj_b):
    import jax
    import jax.numpy as jnp
    def _L0_conv_ref(x, bn1_g, bn1_b, bn2_g, bn2_b, qw, kw, vw, out_w, out_b, off_dw_w, off_dw_b, off_pw_w, cpb_w1, cpb_b1, cpb_w2, cpb_b2, cpb_w3, cpb_b3, mlp_w1, mlp_b1, mlp_w2, mlp_b2):
        import jax, jax.numpy as jnp
        import numpy as np
        B, C, H, W = (2, 512, 32, 32)
        HEADS = 8
        GROUPS = 8
        DH = 64
        DF = 4
        OFF_SCALE = 4.0
        EPS = 1e-05

        def _bn(t, gamma, beta):
            s = gamma / jnp.sqrt(1.0 + EPS)
            return t * s[None, :, None, None] + beta[None, :, None, None]

        def _gconv1x1(t, w):
            b, c, h, ww = t.shape
            o = jnp.einsum('bgci,goc->bgoi', t.reshape(b, GROUPS, c // GROUPS, h * ww), w)
            return o.reshape(b, GROUPS * w.shape[1], h, ww)

        def _grid_sample(img, grid):
            N, Ci, Hi, Wi = img.shape
            gx = (grid[..., 0] + 1.0) * (Wi / 2.0) - 0.5
            gy = (grid[..., 1] + 1.0) * (Hi / 2.0) - 0.5
            x0 = jnp.floor(gx)
            y0 = jnp.floor(gy)
            wx = gx - x0
            wy = gy - y0

            def gather(im, ix, iy):
                valid = (ix >= 0) & (ix < Wi) & (iy >= 0) & (iy < Hi)
                ixc = jnp.clip(ix, 0, Wi - 1).astype(jnp.int32)
                iyc = jnp.clip(iy, 0, Hi - 1).astype(jnp.int32)
                return im[:, iyc, ixc] * valid[None].astype(im.dtype)

            def sample_one(im, x0, y0, wx, wy):
                v00 = gather(im, x0, y0)
                v01 = gather(im, x0 + 1, y0)
                v10 = gather(im, x0, y0 + 1)
                v11 = gather(im, x0 + 1, y0 + 1)
                wx = wx[None]
                wy = wy[None]
                return v00 * (1 - wx) * (1 - wy) + v01 * wx * (1 - wy) + v10 * (1 - wx) * wy + v11 * wx * wy
            return jax.vmap(sample_one)(img, x0, y0, wx, wy)

        def _forward(x, bn1_g, bn1_b, bn2_g, bn2_b, qw, kw, vw, out_w, out_b, off_dw_w, off_dw_b, off_pw_w, cpb_w1, cpb_b1, cpb_w2, cpb_b2, cpb_w3, cpb_b3, mlp_w1, mlp_b1, mlp_w2, mlp_b2):
            b = x.shape[0]
            xn = _bn(x, bn1_g, bn1_b)
            q = _gconv1x1(xn, qw)
            qg = q.reshape(b * GROUPS, DH, H, W)
            off = jax.lax.conv_general_dilated(qg, off_dw_w, (DF, DF), ((1, 1), (1, 1)), dimension_numbers=('NCHW', 'OIHW', 'NCHW'), feature_group_count=DH)
            off = jax.nn.gelu(off + off_dw_b[None, :, None, None], approximate=False)
            off = jnp.tanh(jnp.einsum('bchw,oc->bohw', off, off_pw_w)) * OFF_SCALE
            Hd, Wd = (off.shape[-2], off.shape[-1])
            gy, gx = jnp.meshgrid(jnp.arange(Hd, dtype=x.dtype), jnp.arange(Wd, dtype=x.dtype), indexing='ij')
            vx = gx[None] + off[:, 0]
            vy = gy[None] + off[:, 1]
            nx = 2.0 * vx / max(Hd - 1, 1) - 1.0
            ny = 2.0 * vy / max(Wd - 1, 1) - 1.0
            vgrid_scaled = jnp.stack((nx, ny), axis=-1)
            kv = _grid_sample(xn.reshape(b * GROUPS, DH, H, W), vgrid_scaled)
            kv = kv.reshape(b, GROUPS * DH, Hd, Wd)
            k = _gconv1x1(kv, kw)
            v = _gconv1x1(kv, vw)
            scale = DH ** (-0.5)
            qh = q.reshape(b, HEADS, DH, H * W).transpose(0, 1, 3, 2) * scale
            kh = k.reshape(b, HEADS, DH, Hd * Wd).transpose(0, 1, 3, 2)
            vh = v.reshape(b, HEADS, DH, Hd * Wd).transpose(0, 1, 3, 2)
            qgy, qgx = jnp.meshgrid(jnp.arange(H, dtype=x.dtype), jnp.arange(W, dtype=x.dtype), indexing='ij')
            grid_q = jnp.stack((2.0 * qgx / max(H - 1, 1) - 1.0, 2.0 * qgy / max(W - 1, 1) - 1.0), axis=-1).reshape(1, H * W, 2)
            grid_kv = vgrid_scaled.reshape(b * GROUPS, Hd * Wd, 2)
            pos = grid_q[:, :, None, :] - grid_kv[:, None, :, :]
            bias = jnp.sign(pos) * jnp.log1p(jnp.abs(pos))
            bias = jax.nn.relu(bias @ cpb_w1 + cpb_b1)
            bias = jax.nn.relu(bias @ cpb_w2 + cpb_b2)
            bias = (bias @ cpb_w3 + cpb_b3).reshape(b, GROUPS, H * W, Hd * Wd)
            sim = jnp.einsum('bhid,bhjd->bhij', qh, kh) + bias
            attn = jax.nn.softmax(sim, axis=-1)
            out = jnp.einsum('bhij,bhjd->bhid', attn, vh)
            out = out.transpose(0, 1, 3, 2).reshape(b, HEADS * DH, H, W)
            out = jnp.einsum('bchw,oc->bohw', out, out_w) + out_b[None, :, None, None]
            x = x + out
            xn2 = _bn(x, bn2_g, bn2_b)
            h1 = jax.nn.gelu(jnp.einsum('bchw,oc->bohw', xn2, mlp_w1) + mlp_b1[None, :, None, None], approximate=False)
            return x + jnp.einsum('bchw,oc->bohw', h1, mlp_w2) + mlp_b2[None, :, None, None]
        return _forward(x, bn1_g, bn1_b, bn2_g, bn2_b, qw, kw, vw, out_w, out_b, off_dw_w, off_dw_b, off_pw_w, cpb_w1, cpb_b1, cpb_w2, cpb_b2, cpb_w3, cpb_b3, mlp_w1, mlp_b1, mlp_w2, mlp_b2)

    def _L1_conv_ref(x, gn_w, gn_b, qkv_w, qkv_b, proj_w, proj_b):
        import jax, jax.numpy as jnp
        import numpy as np
        import math
        C = 512
        N_HEADS = 8
        N_GROUPS = 32
        EPS = 1e-05
        b, c, h, w = x.shape
        T = h * w
        xf = x.reshape(b, c, T)
        xg = xf.reshape(b, N_GROUPS, c // N_GROUPS, T)
        mean = xg.mean(axis=(2, 3), keepdims=True)
        var = xg.var(axis=(2, 3), keepdims=True)
        xn = (xg - mean) * jax.lax.rsqrt(var + EPS)
        xn = xn.reshape(b, c, T) * gn_w[None, :, None] + gn_b[None, :, None]
        qkv = jnp.einsum('oc,bct->bot', qkv_w, xn) + qkv_b[None, :, None]
        ch = c // N_HEADS
        qkv = qkv.reshape(b * N_HEADS, 3 * ch, T)
        q, k, v = jnp.split(qkv, 3, axis=1)
        scale = 1.0 / math.sqrt(math.sqrt(ch))
        weight = jnp.einsum('bct,bcs->bts', q * scale, k * scale)
        weight = jax.nn.softmax(weight.astype(jnp.float32), axis=-1).astype(qkv.dtype)
        a = jnp.einsum('bts,bcs->bct', weight, v).reshape(b, c, T)
        hout = jnp.einsum('oc,bct->bot', proj_w, a) + proj_b[None, :, None]
        return (xn + hout).reshape(b, c, h, w)

    def _gn(v, G=32, eps=1e-5):
        B_, C_, H_, W_ = v.shape
        g = v.reshape(B_, G, C_ // G, H_, W_)
        m = jnp.mean(g, axis=(2, 3, 4), keepdims=True)
        s = jnp.var(g, axis=(2, 3, 4), keepdims=True)
        return ((g - m) / jnp.sqrt(s + eps)).reshape(v.shape)

    def _ln_c(v, eps=1e-6):
        m = jnp.mean(v, axis=1, keepdims=True)
        s = jnp.var(v, axis=1, keepdims=True)
        return (v - m) / jnp.sqrt(s + eps)

    def _ln_t(v, eps=1e-5):
        m = jnp.mean(v, axis=-1, keepdims=True)
        s = jnp.var(v, axis=-1, keepdims=True)
        return (v - m) / jnp.sqrt(s + eps)

    def _to_tokens(v):
        B_, C_, H_, W_ = v.shape
        return v.reshape(B_, C_, H_ * W_).transpose(0, 2, 1)
    def _from_tokens(t, like):
        B_, C_, H_, W_ = like.shape
        return t.transpose(0, 2, 1).reshape(B_, C_, H_, W_)

    x = _L0_conv_ref(x, L0_conv_bn1_g, L0_conv_bn1_b, L0_conv_bn2_g, L0_conv_bn2_b, L0_conv_qw, L0_conv_kw, L0_conv_vw, L0_conv_out_w, L0_conv_out_b, L0_conv_off_dw_w, L0_conv_off_dw_b, L0_conv_off_pw_w, L0_conv_cpb_w1, L0_conv_cpb_b1, L0_conv_cpb_w2, L0_conv_cpb_b2, L0_conv_cpb_w3, L0_conv_cpb_b3, L0_conv_mlp_w1, L0_conv_mlp_b1, L0_conv_mlp_w2, L0_conv_mlp_b2)
    x = _L1_conv_ref(x, L1_conv_gn_w, L1_conv_gn_b, L1_conv_qkv_w, L1_conv_qkv_b, L1_conv_proj_w, L1_conv_proj_b)
    return x


_drawn_inputs = setup_inputs


def setup_inputs(seed=0):
    import zlib

    import numpy as np

    out = dict(_drawn_inputs(seed))
    spreads = {'L0_conv_bn1_g': (1.0, 0.6),
     'L0_conv_bn1_b': (0.0, 0.8),
     'L0_conv_bn2_g': (1.0, 0.2),
     'L0_conv_bn2_b': (0.0, 0.499),
     'L0_conv_out_b': (0.0, 0.1),
     'L0_conv_off_dw_b': (0.0, 0.8),
     'L0_conv_cpb_b1': (0.0, 2.0),
     'L0_conv_cpb_b2': (0.0, 2.0),
     'L0_conv_mlp_b1': (0.0, 0.1),
     'L0_conv_mlp_b2': (0.0, 0.1),
     'L1_conv_gn_w': (1.0, 0.2),
     'L1_conv_gn_b': (0.0, 0.1),
     'L1_conv_qkv_b': (0.0, 0.1),
     'L1_conv_proj_b': (0.0, 0.1)}
    factors = {'L0_conv_qw': 8.0,
     'L0_conv_kw': 8.0,
     'L0_conv_vw': 4.908,
     'L0_conv_out_w': 5.018,
     'L0_conv_off_dw_w': 8.0,
     'L0_conv_off_pw_w': 8.0,
     'L0_conv_cpb_w1': 8.0,
     'L0_conv_cpb_w2': 32.924,
     'L0_conv_cpb_w3': 31.84}
    for name, (base, spread) in spreads.items():
        noise = np.random.default_rng([zlib.crc32(name.encode()), seed]).standard_normal(out[name].shape)
        drawn = base * np.exp(spread * noise) if base else spread * noise
        out[name] = jnp.asarray(drawn.astype(out[name].dtype))
    for name, factor in factors.items():
        out[name] = (out[name] * factor).astype(out[name].dtype)
    return out
```

```python
import math
from contextlib import ExitStack

import numpy as np

import concourse.bass as bass
from concourse import mybir

B, C, HH, WW = 2, 512, 32, 32
T = HH * WW
P = 128
CC = C // P
G, DH = 8, 64
NCH = B * CC
HD = WD = 8
J = HD * WD
HALF = T // 2
HID = 4 * C
HC = HID // P
EPS = 1e-5
STEPS = J // 2
NG = 32
GCH = C // NG

_COLS = {}


def _col(name, width):
    at = sum(w for _, w in _COLS.values())
    _COLS[name] = (at, width)


for _n, _w in (("bn1_g", CC), ("bn1_b", CC), ("bn2_g", CC), ("bn2_b", CC), ("out_b", CC), ("mlp_b2", CC),
               ("gn_w", CC), ("gn_b", CC), ("proj_b", CC), ("mlp_b1", HC), ("q_b", CC), ("k_b", CC),
               ("dw_w", 36), ("dw_b", 1), ("cpb_b2", 1), ("cpb_b3", 1),
               ("w3_window", 63), ("cpb_w2", P), ("w1_rows", P), ("b1_rows", P),
               ("pw_feat", P), ("pw_x", P), ("pw_y", P), ("v_b", C)):
    _col(_n, _w)
SMALL = sum(w for _, w in _COLS.values())

_CONST = {}
for _n, _w in (("ident", P), ("grid_feat", J), ("grid_x", J), ("grid_y", J), ("query_pos", 1), ("neg_ix", 1),
               ("neg_iy", 8), ("group_mean", P)):
    _CONST[_n] = (sum(w for _, w in _CONST.values()), _w)
NCONST = sum(w for _, w in _CONST.values())


def deformable_then_attention(nc, x_d, small_d, const_d, onehot_d, qw_d, kw_d, vw_d, ow_d, w1_d, w2_d, qkw_d, vpw_d,
                              pw_d, out_d):
    fp32 = mybir.dt.float32
    f32r = mybir.dt.float32r
    ACT = mybir.ActivationFunctionType
    ALU = mybir.AluOpType
    AX = mybir.AxisListType
    X = AX.X
    outer = ExitStack()
    with outer:
        def sb(ctx, name, shape, dt=fp32):
            return ctx.enter_context(nc.sbuf_tensor(name, shape, dt))

        def pb(ctx, name, shape):
            return ctx.enter_context(nc.psum_tensor(name, shape, fp32))

        def sem(ctx, name):
            return ctx.enter_context(nc.semaphore(name))

        xs = sb(outer, "xs", [P, CC, B, T])
        ao = sb(outer, "ao", [P, NCH, T])
        small = sb(outer, "small", [P, SMALL])
        const = sb(outer, "const", [P, NCONST])

        def sm(name, a=0, b=None):
            at, w = _COLS[name]
            return small[:, at + a:at + (w if b is None else b)]

        def co(name, a=0, b=None):
            at, w = _CONST[name]
            return const[:, at + a:at + (w if b is None else b)]

        ident = co("ident")
        pool_held, dve_held, act_held, pe_held = (sem(outer, x) for x in ("pool_held", "dve_held", "act_held", "pe_held"))

        with ExitStack() as l0:
            q = sb(l0, "q", [P, NCH, T])
            kall = sb(l0, "kall", [P, NCH, J])
            vall = sb(l0, "vall", [P, NCH, P])
            feat = sb(l0, "feat", [P, 2, NCH, J])

            with ExitStack() as a:
                xn = sb(a, "xn", [P, CC, B, T])
                xnt = sb(a, "xnt", [P, B, 8, C])
                qw = sb(a, "qw", [P, CC, P])
                kw = sb(a, "kw", [P, CC, P])
                vw = sb(a, "vw", [P, CC, P])
                bn_s = sb(a, "bn_s", [P, CC])
                dw = sb(a, "dw", [P, NCH, HD, WD])
                dwt = sb(a, "dwt", [P, NCH, HD, WD])
                kv = sb(a, "kv", [P, NCH, 2, J])
                pq = pb(a, "pq", [P, 4, HALF])
                pt = pb(a, "pt", [P, 4, C])
                wt = ao[:, :, :]
                flat = xn[:, :, :, :].rearrange("p a b c -> p (a b c)")
                th_f, th_x, th_y, s1, s2, hx = (flat[:, i * 1024:(i + 1) * 1024] for i in range(6))

                s_x = [sem(a, f"s_x{cc}") for cc in range(CC)]
                s_qw = sem(a, "s_qw")
                s_small = sem(a, "s_small")
                s_w = sem(a, "s_w")
                s_bn = sem(a, "s_bn")
                s_xn = sem(a, "s_xn")
                s_q = sem(a, "s_q")
                s_qc = sem(a, "s_qc")
                s_t = sem(a, "s_t")
                s_tc = sem(a, "s_tc")
                s_dw = sem(a, "s_dw")
                s_dwc = sem(a, "s_dwc")
                s_gelu = sem(a, "s_gelu")
                s_off = sem(a, "s_off")
                s_tanh = sem(a, "s_tanh")
                s_f = sem(a, "s_f")
                s_fa = sem(a, "s_fa")
                s_hy = sem(a, "s_hy")
                s_hv = sem(a, "s_hv")
                s_wt = sem(a, "s_wt")
                s_kv = sem(a, "s_kv")
                s_kvc = sem(a, "s_kvc")
                s_k = sem(a, "s_k")
                s_kc = sem(a, "s_kc")
                block = a.enter_context(nc.Block())

                @block.sync
                def _(sp):
                    sp.dma_start(small[:, :], small_d).then_inc(s_small, 16)
                    for cc in range(CC):
                        sp.dma_start(xs[:, cc, :, :], x_d[:, cc, :, :]).then_inc(s_x[cc], 16)
                        if cc == 0:
                            sp.dma_start(qw[:, :, :], qw_d).then_inc(s_qw, 16)
                            sp.dma_start(const[:, :], const_d).then_inc(s_w, 16)
                    sp.dma_start(kw[:, :, :], kw_d).then_inc(s_w, 16)
                    sp.dma_start(vw[:, :, :], vw_d).then_inc(s_w, 16)

                @block.tensor
                def _(pe):
                    pe.wait_ge(s_qw, 16)
                    pe.wait_ge(s_w, 48)
                    for i in range(NCH * 2):
                        n, h = i // 2, i % 2
                        b, cc = n % B, n // B
                        pe.wait_ge(s_xn, cc + 1)
                        if i >= 4:
                            pe.wait_ge(s_qc, i - 3)
                        nc.tensor.matmul(pq[:, i % 4, :], qw[:, cc, :], xn[:, cc, b, h * HALF:(h + 1) * HALF],
                                         start=True, stop=True).then_inc(s_q, 1)
                    for i in range(B * 8):
                        b, t = i // 8, i % 8
                        if i >= 4:
                            pe.wait_ge(s_tc, i - 3)
                        for cc in range(CC):
                            mm = nc.tensor.transpose(pt[:, i % 4, cc * P:(cc + 1) * P],
                                                     xn[:, cc, b, t * P:(t + 1) * P], ident)
                        mm.then_inc(s_t, 1)
                    pe.wait_ge(s_gelu, 1)
                    pe.wait_ge(s_qc, 2 * NCH)
                    dwf = dw[:, :, :, :].rearrange("p a b c -> p (a b c)")
                    pe.wait_ge(s_tc, B * 8)
                    for v, name in enumerate(("pw_feat", "pw_x", "pw_y")):
                        for par in range(2):
                            r = slice(par * DH, (par + 1) * DH)
                            o = pq[:, 2 * v + par, :] if v < 2 else pt[:, par, :]
                            at = _COLS[name][0]
                            nc.tensor.matmul(o, small[r, at:at + P], dwf[r, :], start=True, stop=True).then_inc(s_off, 1)
                    wtf = wt.rearrange("p t (a n j) -> p t a n j", a=2, n=NCH)
                    pe.wait_ge(s_wt, 8)
                    for n in range(NCH):
                        b, cc = n // CC, n % CC
                        for par in range(2):
                            r = slice(par * DH, (par + 1) * DH)
                            for t in range(8):
                                mm = nc.tensor.matmul(pt[r, 2, n * J:(n + 1) * J],
                                                      xnt[:, b, t, cc * P + par * DH:cc * P + (par + 1) * DH],
                                                      wtf[:, t, par, n, :], start=(t == 0), stop=(t == 7))
                    mm.then_inc(s_kv, 1)
                    pe.wait_ge(s_kvc, 2)
                    for n in range(NCH):
                        mm = nc.tensor.matmul(pt[:, 3, n * J:(n + 1) * J], kw[:, n % CC, :], kv[:, n, 0, :],
                                              start=True, stop=True)
                    mm.then_inc(s_k, 1)
                    pe.wait_ge(s_tanh, 6)
                    for n in range(NCH):
                        mm = nc.tensor.matmul(pq[:, n // 4, (n % 4) * P:(n % 4 + 1) * P],
                                              kv[:, n, :, :].rearrange("p a j -> p (a j)"), vw[:, n % CC, :],
                                              start=True, stop=True)
                    mm.then_inc(s_k, 1)

                @block.scalar
                def _(act):
                    for i in range(NCH * 2):
                        n, h = i // 2, i % 2
                        b, cc = n % B, n // B
                        act.wait_ge(s_q, i + 1)
                        nc.scalar.activation(q[:, b * CC + cc, h * HALF:(h + 1) * HALF], pq[:, i % 4, :],
                                             ACT.Copy).then_inc(s_qc, 1)
                    for i in range(B * 8):
                        act.wait_ge(s_t, i + 1)
                        nc.scalar.activation(xnt[:, i // 8, i % 8, :], pt[:, i % 4, :], ACT.Copy).then_inc(s_tc, 1)
                    dwf = dw[:, :, :, :].rearrange("p a b c -> p (a b c)")
                    act.wait_ge(s_dw, 1)
                    nc.scalar.activation(dwf, dwf, ACT.Gelu, bias=sm("dw_b")).then_inc(s_gelu, 1)
                    for v, dst in enumerate((th_f, th_x, th_y)):
                        for par in range(2):
                            act.wait_ge(s_off, 2 * v + par + 1)
                            o = pq[:, 2 * v + par, :] if v < 2 else pt[:, par, :]
                            nc.scalar.activation(dst[:, par * 512:(par + 1) * 512], o, ACT.Tanh).then_inc(s_tanh, 1)
                    act.wait_ge(s_f, 1)
                    nc.scalar.activation(s1, th_f, ACT.Abs).then_inc(s_fa, 1)
                    act.wait_ge(s_fa, 1)
                    nc.scalar.activation(s1, s1, ACT.Ln, bias=1.0).then_inc(s_fa, 1)
                    nc.scalar.activation(s2, th_f, ACT.Sign).then_inc(s_fa, 1)
                    act.wait_ge(s_f, 3)
                    act.wait_ge(s_fa, 3)
                    nc.scalar.activation(hx, th_x, ACT.Abs, bias=co("neg_ix")).then_inc(s_hy, 1)
                    for t in range(8):
                        if t == 0:
                            act.wait_ge(s_f, 4)
                            act.wait_ge(s_hy, 1)
                        if t >= 2:
                            act.wait_ge(s_hv, t)
                        nc.scalar.activation((th_x, s1)[t % 2], th_y, ACT.Abs, bias=co("neg_iy", t, t + 1)).then_inc(s_hy, 1)
                    act.wait_ge(s_kv, 1)
                    nc.scalar.activation(kv[:, :, 0, :], pt[:, 2, :].rearrange("p (n j) -> p n j", n=NCH),
                                         ACT.Copy).then_inc(s_kvc, 1)
                    act.wait_ge(s_k, 2)
                    for h in range(2):
                        nc.scalar.activation(vall[:, h * 4:(h + 1) * 4, :].rearrange("p a b -> p (a b)"), pq[:, h, :],
                                             ACT.Copy).then_inc(s_kc, 1)

                @block.vector
                def _(dve):
                    dve.wait_ge(s_small, 16)
                    nc.vector.tensor_scalar(bn_s[:, :], sm("bn1_g"), 1.0 / math.sqrt(1.0 + EPS), None,
                                            ALU.mult).then_inc(s_bn, 1)
                    dve.wait_ge(s_bn, 1)
                    for cc in range(CC):
                        dve.wait_ge(s_x[cc], 16)
                        nc.vector.tensor_scalar(xn[:, cc, :, :], xs[:, cc, :, :], bn_s[:, cc:cc + 1],
                                                sm("bn1_b", cc, cc + 1), ALU.mult, ALU.add).then_inc(s_xn, 1)
                    dve.wait_ge(s_qc, 2 * NCH)
                    qv = q[:, :, :].rearrange("p n (y x) -> p n y x", y=HH)
                    done = 0
                    first = True
                    taps = [(2, 2)] + [(ky, kx) for ky in range(6) for kx in range(6) if (ky, kx) != (2, 2)]
                    for ky, kx in taps:
                        y0, x0 = (1 if ky == 0 else 0), (1 if kx == 0 else 0)
                        y1, x1 = (HD - 1 if ky == 5 else HD), (WD - 1 if kx == 5 else WD)
                        ys, xs_ = 4 * y0 - 1 + ky, 4 * x0 - 1 + kx
                        src = qv[:, :, ys:ys + 4 * (y1 - y0 - 1) + 1:4, xs_:xs_ + 4 * (x1 - x0 - 1) + 1:4]
                        dst = dw[:, :, y0:y1, x0:x1]
                        w = sm("dw_w", ky * 6 + kx, ky * 6 + kx + 1)
                        if done:
                            dve.wait_ge(s_dwc, done)
                        if first:
                            nc.vector.tensor_scalar(dst, src, w, None, ALU.mult).then_inc(s_dwc, 1)
                            first = False
                        else:
                            tmp = dwt[:, :, y0:y1, x0:x1]
                            nc.vector.tensor_scalar(tmp, src, w, None, ALU.mult).then_inc(s_dwc, 1)
                            done += 1
                            dve.wait_ge(s_dwc, done)
                            nc.vector.tensor_tensor(dst, dst, tmp, ALU.add).then_inc(s_dwc, 1)
                        done += 1
                    dve.wait_ge(s_dwc, done)
                    nc.vector.engine_nop().then_inc(s_dw, 1) if False else nc.vector.tensor_scalar(
                        dwt[:, 0, 0, 0:1], dw[:, 0, 0, 0:1], 1.0, None, ALU.mult).then_inc(s_dw, 1)
                    own = 0

                    def grid_of(dst, grid, waited):
                        nonlocal own
                        dve.wait_ge(s_tanh, waited)
                        g = grid[:, None, :].to_broadcast([P, 2 * NCH, J])
                        d3 = dst.rearrange("p (n j) -> p n j", j=J)
                        nc.vector.tensor_scalar(dst, dst, 4.0, None, ALU.mult).then_inc(s_bn, 1)
                        own += 1
                        dve.wait_ge(s_bn, 1 + own)
                        nc.vector.tensor_tensor(d3, d3, g, ALU.add).then_inc(s_bn, 1)
                        own += 1
                        dve.wait_ge(s_bn, 1 + own)
                        nc.vector.tensor_scalar(dst, dst, 2.0 / (HD - 1), -1.0, ALU.mult, ALU.add).then_inc(s_bn, 1)
                        own += 1
                        dve.wait_ge(s_bn, 1 + own)

                    grid_of(th_f, co("grid_feat"), 2)
                    nc.vector.tensor_scalar(th_f, th_f, -1.0, co("query_pos"), ALU.mult, ALU.add).then_inc(s_f, 1)
                    for dst, name, k in ((th_x, "grid_x", 4), (th_y, "grid_y", 6)):
                        grid_of(dst, co(name), k)
                        nc.vector.tensor_scalar(dst, dst, 1.0, WW / 2.0, ALU.add, ALU.mult).then_inc(s_bn, 1)
                        own += 1
                        dve.wait_ge(s_bn, 1 + own)
                        nc.vector.tensor_scalar(dst, dst, -0.5, None, ALU.add).then_inc(s_f, 1)
                        if name == "grid_x":
                            dve.wait_ge(s_fa, 3)
                            nc.vector.tensor_tensor(feat[:, :, :, :].rearrange("p a n j -> p (a n j)"), s1, s2,
                                                    ALU.mult).then_inc(s_f, 1)
                    dve.wait_ge(s_hy, 1)
                    nc.vector.tensor_scalar(hx, hx, -1.0, 0.0, ALU.add, ALU.min).then_inc(s_hv, 1)
                    for t in range(8):
                        cur = (th_x, s1)[t % 2]
                        dve.wait_ge(s_hy, t + 2)
                        nc.vector.tensor_scalar(s2, cur, -1.0, 0.0, ALU.add, ALU.min).then_inc(s_hv, 1)
                        dve.wait_ge(s_hv, t + 2)
                        nc.vector.tensor_tensor(wt[:, t, :], s2, hx, ALU.mult).then_inc(s_wt, 1)
                        dve.wait_ge(s_wt, t + 1)
                    dve.wait_ge(s_kvc, 1)
                    nc.vector.tensor_copy(kv[:, :, 1, :], pt[:, 2, :].rearrange("p (n j) -> p n j", n=NCH)
                                          ).then_inc(s_kvc, 1)
                    dve.wait_ge(s_k, 1)
                    nc.vector.tensor_scalar(kall[:, :, :].rearrange("p n j -> p (n j)"), pt[:, 3, :], DH ** -0.5, None,
                                            ALU.mult).then_inc(s_kc, 1)

            with ExitStack() as bctx:
                onehot = sb(bctx, "onehot", [P, T], f32r)
                w2h = sb(bctx, "w2h", [P, P], f32r)
                w2l = sb(bctx, "w2l", [P, P], f32r)
                tsl = sb(bctx, "tsl", [P, 2, 2, P], f32r)
                v1 = sb(bctx, "v1", [P, 2, P])
                v2 = sb(bctx, "v2", [P, 2, P])
                vh = sb(bctx, "vh", [P, 2, P], f32r)
                h1h = sb(bctx, "h1h", [P, 4, T], f32r)
                h1l = sb(bctx, "h1l", [P, 4, T], f32r)
                h2 = sb(bctx, "h2", [P, 2, 2, 2, HALF])
                wz = sb(bctx, "wz", [P, 2, 32])
                qs = sb(bctx, "qs", [P, T])
                ks = sb(bctx, "ks", [P, J])
                vs = sb(bctx, "vs", [P, DH])
                sims = sb(bctx, "sims", [P, HALF])
                negm = sb(bctx, "negm", [P, 8])
                psum_ = sb(bctx, "prob_sum", [P, 8])
                prob = sb(bctx, "prob", [P, 8, J])
                probn = sb(bctx, "probn", [P, 8, J])
                pts = sb(bctx, "pts", [P, HALF])
                p1 = pb(bctx, "p1", [P, 2, T])
                p2 = pb(bctx, "p2", [P, 2, HALF])
                sim = pb(bctx, "sim", [P, HALF])
                misc = pb(bctx, "misc", [P, 8, J])
                miscf = misc[:, :, :].rearrange("p a j -> p (a j)")

                const_ready = sem(bctx, "const_ready")
                w2_ready = sem(bctx, "w2_ready")
                rows_own = sem(bctx, "rows_own")
                rows_ready = sem(bctx, "rows_ready")
                l1_done = sem(bctx, "l1_done")
                hi_done = sem(bctx, "hi_done")
                lo_done = sem(bctx, "lo_done")
                l2_done = sem(bctx, "l2_done")
                relu_a = sem(bctx, "relu_a")
                relu_b = sem(bctx, "relu_b")
                wz_ready = sem(bctx, "wz_ready")
                l3_done = sem(bctx, "l3_done")
                kq_ready = sem(bctx, "kq_ready")
                seed_done = sem(bctx, "seed_done")
                sim_done = sem(bctx, "sim_done")
                sim_copied = sem(bctx, "sim_copied")
                turned = sem(bctx, "turned")
                max_done = sem(bctx, "max_done")
                shifted = sem(bctx, "shifted")
                exp_done = sem(bctx, "exp_done")
                sum_done = sem(bctx, "sum_done")
                normed = sem(bctx, "normed")
                turned_back = sem(bctx, "turned_back")
                pt_copied = sem(bctx, "pt_copied")
                vs_ready = sem(bctx, "vs_ready")
                pv_done = sem(bctx, "pv_done")
                ao_done = sem(bctx, "ao_done")
                block = bctx.enter_context(nc.Block())

                LAST_M = STEPS - 1
                UN = 2 * STEPS

                def walk(eng, step):
                    def chunk(n, first, last):
                        for par in range(2):
                            prev = not (first and par == 0)
                            for m in range(4):
                                step(n, par, m, prev, True)
                            with eng.Fori(4, STEPS - 2, 2) as mm:
                                step(n, par, mm, prev, True, parity=0)
                                step(n, par, mm + 1, prev, True, parity=1)
                            step(n, par, LAST_M - 1, prev, True)
                            step(n, par, LAST_M, prev, not (last and par == 1))

                    chunk(0, True, False)
                    with eng.Fori(1, NCH - 1) as n:
                        chunk(n, False, False)
                    chunk(NCH - 1, False, True)

                @block.sync
                def _(sp):
                    sp.nop()

                @block.tensor
                def _(pe):
                    def rows(par_slot, jb):
                        for ih in range(2):
                            mm = nc.tensor.matmul(p1[:, jb, ih * HALF:(ih + 1) * HALF], tsl[:, par_slot, jb, :],
                                                  onehot[:, ih * HALF:(ih + 1) * HALF], start=True, stop=True)
                        mm.then_inc(l1_done, 1)

                    def third(slot, pair_last):
                        for ih in range(2):
                            for jb in range(2):
                                at = ih * J + jb * 32
                                mm = nc.tensor.matmul(sim[at:at + 32, :], wz[:, slot, :], h2[:, slot, jb, ih, :],
                                                      start=False, stop=pair_last, skip_group_check=True)
                        mm.then_inc(l3_done, 1)

                    def seed(n, par, r):
                        pe.wait_ge(kq_ready, 2 * n + 2)
                        pe.sem_inc(pe_held, 1)
                        rr = slice(par * DH, (par + 1) * DH)
                        for ih in range(2):
                            mm = nc.tensor.matmul(sim[ih * J:(ih + 1) * J, :], ks[rr, :],
                                                  qs[rr, ih * HALF:(ih + 1) * HALF], start=True, stop=False,
                                                  skip_group_check=True)
                        mm.then_inc(seed_done, 1)

                    def turn(r):
                        if not (isinstance(r, int) and r < 2):
                            pe.wait_ge(ao_done, 2 * r - 2)
                        for i in range(4):
                            mm = nc.tensor.transpose(miscf[:, i * P:(i + 1) * P], sims[:, i * P:(i + 1) * P], ident)
                        mm.then_inc(turned, 1)

                    def turn_back(r):
                        pe.wait_ge(normed, r)
                        pn = probn[:, :, :].rearrange("p a j -> p (a j)")
                        for i in range(4):
                            mm = nc.tensor.transpose(miscf[:, i * P:(i + 1) * P], pn[:, i * P:(i + 1) * P], ident)
                        mm.then_inc(turned_back, 1)

                    def values(r, pp, ih):
                        if ih == 0:
                            pe.wait_ge(pt_copied, r)
                            pe.wait_ge(vs_ready, r)
                        else:
                            pe.wait_ge(ao_done, 2 * r - 1)
                        pe.sem_inc(pe_held, 1)
                        nc.tensor.matmul(miscf[pp * DH:(pp + 1) * DH, :], vs[ih * J:(ih + 1) * J, :],
                                         pts[ih * J:(ih + 1) * J, :], start=True, stop=True).then_inc(pv_done, 1)

                    def step(n, par, m, prev, nxt, parity=None):
                        sp_ = m % 2 if parity is None else parity
                        r = 2 * n + par
                        s = r * STEPS + m
                        k0 = 2 * s
                        for jb in range(2):
                            k = k0 + jb
                            pe.wait_ge(lo_done, k + 1)
                            if nxt:
                                if jb == 0:
                                    pe.wait_ge(rows_ready, s + 2)
                                rows(1 - sp_, jb)
                            u = 2 * sp_ + jb
                            for ih in range(2):
                                if not (isinstance(k, int) and k == 0):
                                    pe.wait_ge(relu_a if ih == 0 else relu_b, k)
                                cols = slice(ih * HALF, (ih + 1) * HALF)
                                nc.tensor.matmul(p2[:, ih, :], w2h[:, :], h1h[:, u, cols], start=True, stop=False)
                                nc.tensor.matmul(p2[:, ih, :], w2h[:, :], h1l[:, u, cols], start=False, stop=False)
                                nc.tensor.matmul(p2[:, ih, :], w2l[:, :], h1h[:, u, cols], start=False,
                                                 stop=True).then_inc(l2_done, 1)
                        static = isinstance(m, int)
                        if static and m == 1:
                            if prev:
                                pe.wait_ge(sim_copied, r)
                            seed(n, par, r)
                        if not (static and m == 0 and not prev):
                            pe.wait_ge(relu_a, 2 * s)
                            pe.wait_ge(relu_b, 2 * s)
                            pe.wait_ge(wz_ready, s)
                            third(1 - sp_, static and m == 0)
                        if static and prev:
                            if m == 1:
                                turn(r)
                            if m == 3:
                                turn_back(r)
                            if m == LAST_M - 1:
                                values(r, 1 - par, 0)
                            if m == LAST_M:
                                values(r, 1 - par, 1)

                    pe.wait_ge(const_ready, 16)
                    pe.wait_ge(w2_ready, 3)
                    pe.wait_ge(rows_ready, 1)
                    for jb in range(2):
                        rows(0, jb)
                    walk(pe, step)
                    s, r = 2 * NCH * STEPS, 2 * NCH
                    pe.wait_ge(relu_a, 2 * s)
                    pe.wait_ge(relu_b, 2 * s)
                    pe.wait_ge(wz_ready, s)
                    third(1, True)
                    pe.wait_ge(sim_copied, r)
                    turn(r)
                    turn_back(r)
                    values(r, 1, 0)
                    values(r, 1, 1)

                @block.scalar
                def _(act):
                    def hi(u, jb):
                        nc.scalar.activation(h1h[:, u, :], p1[:, jb, :], ACT.Relu).then_inc(hi_done, 1)

                    def copy_sim(r, s):
                        act.wait_ge(l3_done, s)
                        if not (isinstance(r, int) and r < 2):
                            act.wait_ge(turned, r - 1)
                        nc.scalar.activation(sims[:, :], sim[:, :], ACT.Identity, bias=sm("cpb_b3")
                                             ).then_inc(sim_copied, 1)

                    def exp(r):
                        act.wait_ge(shifted, r)
                        nc.scalar.activation(prob[:, :, :], prob[:, :, :], ACT.Exp).then_inc(exp_done, 1)

                    def copy_pt(r):
                        act.wait_ge(turned_back, r)
                        if not (isinstance(r, int) and r < 2):
                            act.wait_ge(pv_done, 2 * r - 2)
                        nc.scalar.activation(pts[:, :], miscf, ACT.Copy).then_inc(pt_copied, 1)

                    def copy_out(r, n, pp, ih):
                        act.wait_ge(pv_done, 2 * r - 1 + ih)
                        rr = slice(pp * DH, (pp + 1) * DH)
                        o = (ao[rr, n, ih * HALF:(ih + 1) * HALF] if isinstance(n, int) else
                             ao[rr, bass.ds(n, 1), ih * HALF:(ih + 1) * HALF].rearrange("p a t -> p (a t)"))
                        nc.scalar.activation(o, miscf[rr, :], ACT.Copy).then_inc(ao_done, 1)

                    def step(n, par, m, prev, nxt, parity=None):
                        sp_ = m % 2 if parity is None else parity
                        r = 2 * n + par
                        s = r * STEPS + m
                        static = isinstance(m, int)
                        if static and prev and m == LAST_M - 1:
                            copy_pt(r)
                        pn = n if par == 1 else n - 1
                        if static and prev and m == LAST_M:
                            copy_out(r, pn, 1 - par, 0)
                        for jb in range(2):
                            k = 2 * s + jb
                            if nxt:
                                act.wait_ge(l1_done, k + 3)
                                if not (isinstance(k, int) and k < 2):
                                    act.wait_ge(l2_done, 2 * k - 2)
                                hi((2 * sp_ + jb + 2) % 4, jb)
                            act.wait_ge(l2_done, 2 * k + 1)
                            if jb == 0 and not (isinstance(s, int) and s < 2):
                                act.wait_ge(l3_done, s - 1)
                            nc.scalar.activation(h2[:, sp_, jb, 0, :], p2[:, 0, :], ACT.Relu,
                                                 bias=sm("cpb_b2")).then_inc(relu_a, 1)
                        if static and prev:
                            if m == 0:
                                copy_sim(r, s)
                            if m == 2:
                                exp(r)
                            if m == LAST_M:
                                copy_out(r, pn, 1 - par, 1)

                    nc.scalar.activation(w2h[:, :], sm("cpb_w2"), ACT.Identity).then_inc(w2_ready, 1)
                    for jb in range(2):
                        act.wait_ge(l1_done, jb + 1)
                        hi(jb, jb)
                    walk(act, step)
                    r = 2 * NCH
                    copy_sim(r, r * STEPS)
                    exp(r)
                    copy_pt(r)
                    copy_out(r, NCH - 1, 1, 0)
                    copy_out(r, NCH - 1, 1, 1)

                @block.vector
                def _(dve):
                    def lo(u, jb):
                        nc.vector.scalar_tensor_tensor(out=h1l[:, u, :], in0=p1[:, jb, :], scalar=0.0,
                                                       in1=h1h[:, u, :].bitcast(fp32), op0=ALU.max,
                                                       op1=ALU.subtract).then_inc(lo_done, 1)

                    def window(m, slot):
                        at = _COLS["w3_window"][0] + 31
                        src = (small[:, at - m:at - m + 32] if isinstance(m, int) else
                               small[:, bass.ds(at - m, 32)])
                        nc.vector.tensor_copy(wz[:, slot, :], src).then_inc(wz_ready, 1)

                    def shift(r):
                        dve.wait_ge(turned, r)
                        if not (isinstance(r, int) and r < 2):
                            dve.wait_ge(normed, r - 1)
                        nc.vector.tensor_reduce(negm[:, :], misc[:, :, :], X, ALU.max, negate=True
                                                ).then_inc(max_done, 1)
                        dve.wait_ge(max_done, r)
                        nc.vector.tensor_tensor(prob[:, :, :], misc[:, :, :],
                                                negm[:, :, None].to_broadcast([P, 8, J]), ALU.add
                                                ).then_inc(shifted, 1)

                    def norm(r):
                        dve.wait_ge(exp_done, r)
                        nc.vector.tensor_reduce(psum_[:, :], prob[:, :, :], X, ALU.add).then_inc(sum_done, 1)
                        dve.wait_ge(sum_done, 2 * r - 1)
                        nc.vector.reciprocal(psum_[:, :], psum_[:, :]).then_inc(sum_done, 1)
                        dve.wait_ge(sum_done, 2 * r)
                        if not (isinstance(r, int) and r < 2):
                            dve.wait_ge(turned_back, r - 1)
                        nc.vector.tensor_tensor(probn[:, :, :], prob[:, :, :],
                                                psum_[:, :, None].to_broadcast([P, 8, J]), ALU.mult
                                                ).then_inc(normed, 1)

                    def step(n, par, m, prev, nxt, parity=None):
                        sp_ = m % 2 if parity is None else parity
                        r = 2 * n + par
                        s = r * STEPS + m
                        static = isinstance(m, int)
                        if static and prev:
                            if m == 2:
                                shift(r)
                            if m == 3:
                                norm(r)
                        for jb in range(2):
                            k = 2 * s + jb
                            if nxt:
                                dve.wait_ge(hi_done, k + 3)
                                lo((2 * sp_ + jb + 2) % 4, jb)
                            dve.wait_ge(l2_done, 2 * k + 2)
                            if jb == 0 and not (isinstance(s, int) and s < 2):
                                dve.wait_ge(l3_done, s - 1)
                            nc.vector.tensor_scalar(h2[:, sp_, jb, 1, :], p2[:, 1, :], sm("cpb_b2"), 0.0, ALU.add,
                                                    ALU.max).then_inc(relu_b, 1)
                        window(m, sp_)

                    dve.wait_ge(w2_ready, 1)
                    nc.vector.tensor_tensor(w2l[:, :], sm("cpb_w2"), w2h[:, :].bitcast(fp32), ALU.subtract
                                            ).then_inc(w2_ready, 2)
                    for jb in range(2):
                        dve.wait_ge(hi_done, jb + 1)
                        lo(jb, jb)
                    walk(dve, step)
                    shift(2 * NCH)
                    norm(2 * NCH)

                @block.gpsimd
                def _(pool):
                    pool.dma_start(onehot[:, :], onehot_d).then_inc(const_ready, 16)
                    nc.gpsimd.memset(vh[0:64, :, :].bitcast(fp32), 0.0).then_inc(rows_own, 1)
                    w1r = sm("w1_rows")[:, None, :].to_broadcast([P, 2, P])
                    b1r = sm("b1_rows")[:, None, :].to_broadcast([P, 2, P])
                    featf = feat[:, :, :, :].rearrange("p a n j -> p (a n j)")

                    def make_rows(n, par, m, slot):
                        s = (2 * n + par) * STEPS + m
                        own = 3 * s + 1
                        at = par * (NCH * J) + n * J + m
                        f = (featf[:, at:at + 33:32] if isinstance(at, int) else featf[:, bass.ds(at, 2, 32)])
                        if isinstance(s, int) and s == 0:
                            pool.wait_ge(rows_own, 1)
                        else:
                            pool.wait_ge(rows_ready, s)
                            pool.sem_inc(pool_held, 1)
                        nc.gpsimd.tensor_tensor(v1[:, :, :], w1r, f[:, :, None].to_broadcast([P, 2, P]), ALU.mult
                                                ).then_inc(rows_own, 1)
                        pool.wait_ge(rows_own, own + 1)
                        nc.gpsimd.tensor_tensor(v2[:, :, :], v1[:, :, :], b1r, ALU.add).then_inc(rows_own, 1)
                        pool.wait_ge(rows_own, own + 2)
                        nc.gpsimd.tensor_tensor(vh[64:P, :, :], v1[64:P, :, :],
                                                sm("b1_rows")[64:P, None, :].to_broadcast([64, 2, P]), ALU.add
                                                ).then_inc(rows_own, 1)
                        pool.wait_ge(rows_own, own + 3)
                        if not (isinstance(s, int) and s < 2):
                            pool.wait_ge(l1_done, 2 * s - 2)
                        nc.gpsimd.tensor_tensor(tsl[:, slot, :, :], v2[:, :, :], vh[:, :, :].bitcast(fp32),
                                                ALU.subtract).then_inc(rows_ready, 1)

                    def copy_queries(n, r, prev):
                        if prev:
                            pool.wait_ge(seed_done, r)
                            pool.sem_inc(pool_held, 1)
                        dyn = not isinstance(n, int)
                        qsrc = q[:, bass.ds(n, 1), :].rearrange("p a t -> p (a t)") if dyn else q[:, n, :]
                        ksrc = kall[:, bass.ds(n, 1), :].rearrange("p a t -> p (a t)") if dyn else kall[:, n, :]
                        nc.gpsimd.tensor_copy(qs[:, :], qsrc).then_inc(kq_ready, 1)
                        nc.gpsimd.tensor_copy(ks[:, :], ksrc).then_inc(kq_ready, 1)

                    def copy_values(r, pn, pp):
                        if not (isinstance(r, int) and r < 2):
                            pool.wait_ge(pv_done, 2 * r - 2)
                            pool.sem_inc(pool_held, 1)
                        vsrc = (vall[:, pn, pp * DH:(pp + 1) * DH] if isinstance(pn, int) else
                                vall[:, bass.ds(pn, 1), pp * DH:(pp + 1) * DH].rearrange("p a t -> p (a t)"))
                        nc.gpsimd.tensor_copy(vs[:, :], vsrc).then_inc(vs_ready, 1)

                    def step(n, par, m, prev, nxt, parity=None):
                        sp_ = m % 2 if parity is None else parity
                        r = 2 * n + par
                        make_rows(n, par, m, sp_)
                        if isinstance(m, int) and m == 0 and par == 0:
                            copy_queries(n, r, prev)
                        if isinstance(m, int) and m == 3 and prev:
                            copy_values(r, n if par == 1 else n - 1, 1 - par)

                    walk(pool, step)
                    copy_values(2 * NCH, NCH - 1, 1)

        with ExitStack() as c:
            ow = sb(c, "ow", [P, CC, C])
            w1 = sb(c, "w1", [P, CC, HID])
            w2 = sb(c, "w2", [P, HC, C])
            xb2 = sb(c, "xb2", [P, CC, HALF])
            hid = sb(c, "hid", [P, HC, HALF])
            bn2_s = sb(c, "bn2_s", [P, CC])
            pd = pb(c, "pd", [P, 4, HALF])
            pa = pb(c, "pa", [P, 4, HALF])
            ow_in = sem(c, "ow_in")
            w1_in = sem(c, "w1_in")
            w2_in = sem(c, "w2_in")
            bn2_ready = sem(c, "bn2_ready")
            sum_ready = sem(c, "sum_ready")
            sum_used = sem(c, "sum_used")
            resid = sem(c, "resid")
            xb_ready = sem(c, "xb_ready")
            h_ready = sem(c, "h_ready")
            h_done = sem(c, "h_done")
            block = c.enter_context(nc.Block())

            @block.sync
            def _(sp):
                sp.dma_start(ow[:, :, :], ow_d).then_inc(ow_in, 16)
                sp.dma_start(w1[:, :, :], w1_d).then_inc(w1_in, 16)
                sp.dma_start(w2[:, :, :], w2_d).then_inc(w2_in, 16)

            @block.tensor
            def _(pe):
                def chunk(lhs, rhs, n_in, oc, k, t, wait):
                    d = 8 * k + t
                    if wait:
                        pe.wait_ge(sum_used, d - 3)
                    for ci in range(n_in):
                        mm = nc.tensor.matmul(pd[:, t % 4, :], lhs[:, ci, oc * P:(oc + 1) * P], rhs(ci),
                                              start=(ci == 0), stop=(ci == n_in - 1))
                    mm.then_inc(sum_ready, 1)

                def token_block(b, th):
                    k = 2 * b + th
                    later = b > 0
                    cols = slice(th * HALF, (th + 1) * HALF)
                    for oc in range(CC):
                        chunk(ow, lambda ci: aof(b, ci, cols), CC, oc, k, oc, later or k > 0)
                    pe.wait_ge(xb_ready, CC * (k + 1))
                    for i in range(HC):
                        if later or k > 0 or i >= 4:
                            pe.wait_ge(h_done, HC * k + i - 3)
                        for ci in range(CC):
                            mm = nc.tensor.matmul(pa[:, i % 4, :], w1[:, ci, i * P:(i + 1) * P], xb2[:, ci, :],
                                                  start=(ci == 0), stop=(ci == CC - 1))
                        mm.then_inc(h_ready, 1)
                    pe.wait_ge(h_done, HC * (k + 1))
                    for oc in range(CC):
                        chunk(w2, lambda ci: hid[:, ci, :], HC, oc, k, CC + oc, True)

                def aof(b, ci, cols):
                    return ao[:, b * CC + ci, cols]

                pe.wait_ge(ow_in, 16)
                pe.wait_ge(w1_in, 16)
                pe.wait_ge(w2_in, 16)
                for b in range(B):
                    for th in range(2):
                        token_block(b, th)

            @block.scalar
            def _(act):
                with act.Fori(0, 2 * B) as k:
                    for i in range(HC):
                        act.wait_ge(h_ready, HC * k + i + 1)
                        nc.scalar.activation(hid[:, i, :], pa[:, i % 4, :], ACT.Gelu, bias=sm("mlp_b1", i, i + 1)
                                             ).then_inc(h_done, 1)

            @block.vector
            def _(dve):
                nc.vector.tensor_scalar(bn2_s[:, :], sm("bn2_g"), 1.0 / math.sqrt(1.0 + EPS), None, ALU.mult
                                        ).then_inc(bn2_ready, 1)
                dve.wait_ge(bn2_ready, 1)
                with dve.Fori(0, 2 * B) as k:
                    xk = [xs[:, cc, :, :].rearrange("p b t -> p (b t)")[:, bass.ds(k * HALF, HALF)] for cc in range(CC)]
                    for oc in range(CC):
                        dve.wait_ge(sum_ready, 8 * k + oc + 1)
                        nc.vector.scalar_tensor_tensor(out=xk[oc], in0=pd[:, oc, :], scalar=sm("out_b", oc, oc + 1),
                                                       in1=xk[oc], op0=ALU.add, op1=ALU.add).then_inc(resid, 1)
                        dve.wait_ge(resid, 5 * k + oc + 1)
                        dve.sem_inc(dve_held, 1)
                        nc.vector.tensor_scalar(xb2[:, oc, :], xk[oc], bn2_s[:, oc:oc + 1], sm("bn2_b", oc, oc + 1),
                                                ALU.mult, ALU.add).then_inc(xb_ready, 1)
                        dve.sem_inc(sum_used, 1)
                    for oc in range(CC):
                        dve.wait_ge(sum_ready, 8 * k + CC + oc + 1)
                        nc.vector.scalar_tensor_tensor(out=xk[oc], in0=pd[:, oc, :], scalar=sm("mlp_b2", oc, oc + 1),
                                                       in1=xk[oc], op0=ALU.add, op1=ALU.add).then_inc(sum_used, 1)
                    dve.wait_ge(sum_used, 8 * k + 8)
                    dve.sem_inc(resid, 1)

        with ExitStack() as d:
            qkw = sb(d, "qkw", [P, CC, 2 * C])
            vpw = sb(d, "vpw", [P, CC, C])
            pw = sb(d, "pw", [P, CC, C])
            qk = sb(d, "qk", [P, 2 * CC, T])
            va = sb(d, "va", [P, 8, C])
            pr = sb(d, "pr", [P, 2, 2, T])
            ptr = sb(d, "ptr", [P, 2, 8, HALF])
            stats = sb(d, "stats", [P, CC, B, 2, 6])
            mv = sb(d, "mv", [P, 2, CC * B])
            dev = sb(d, "dev", [P, CC * B])
            gsc = sb(d, "gsc", [P, CC, B])
            gbi = sb(d, "gbi", [P, CC, B])
            mvt = sb(d, "mvt", [P, CC * B, 2])
            rmax = sb(d, "rmax", [P, 2, 2])
            rsum = sb(d, "rsum", [P, 2, 2])
            rinv = sb(d, "rinv", [P, 2, 2])
            att = ao[:, 0:CC, :]
            xg = ao[:, CC:2 * CC, :]
            ps = pb(d, "ps", [P, 2, T])
            pp_ = pb(d, "pp_", [P, 2, HALF])
            po = pb(d, "po", [P, 2, HALF])
            w_in = sem(d, "w_in")
            st_own = sem(d, "st_own")
            st_v = sem(d, "st_v")
            gm = sem(d, "gm")
            gd = sem(d, "gd")
            sq = sem(d, "sq")
            gready = sem(d, "gready")
            xg_ready = sem(d, "xg_ready")
            pj = sem(d, "pj")
            pj_used = sem(d, "pj_used")
            qk_done = sem(d, "qk_done")
            mx = sem(d, "mx")
            ex = sem(d, "ex")
            ri = sem(d, "ri")
            nm = sem(d, "nm")
            tr = sem(d, "tr")
            tra = sem(d, "tra")
            trb = sem(d, "trb")
            pv = sem(d, "pv")
            pvc = sem(d, "pvc")
            fin = sem(d, "fin")
            stored = sem(d, "stored")
            block = d.enter_context(nc.Block())
            TT = T // P
            NB = 24 + 8
            SC = 1.0 / math.sqrt(math.sqrt(DH))

            @block.sync
            def _(sp):
                sp.dma_start(qkw[:, :, :], qkw_d).then_inc(w_in, 16)
                sp.dma_start(vpw[:, :, :], vpw_d).then_inc(w_in, 16)
                sp.dma_start(pw[:, :, :], pw_d).then_inc(w_in, 16)
                for b in range(B):
                    for i in range(8):
                        sp.wait_ge(fin, 8 * b + i + 1)
                        oc, th = i // 2, i % 2
                        sp.dma_start(out_d[:, oc, b, th * HALF:(th + 1) * HALF],
                                     xs[:, oc, b, th * HALF:(th + 1) * HALF]).then_inc(stored, 16)
                sp.wait_ge(stored, 16 * 8 * B)

            @block.tensor
            def _(pe):
                pe.wait_ge(gm, 1)
                nc.tensor.matmul(po[:, 0, 0:CC * B], co("group_mean"), mv[:, 0, :], start=True, stop=True
                                 ).then_inc(gd, 1)
                pe.wait_ge(gm, 2)
                nc.tensor.matmul(po[:, 1, 0:CC * B], co("group_mean"), dev[:, :], start=True, stop=True
                                 ).then_inc(gd, 1)
                pe.wait_ge(w_in, 48)

                def transposes(b, g, hh):
                    par = g % 2
                    u = 2 * (g + b * 32) + hh
                    pe.wait_ge(nm, u + 1)
                    if u > 0:
                        pe.wait_ge(tra, u)
                        pe.wait_ge(trb, u)
                    for st in range(8):
                        mm = nc.tensor.transpose(pp_[:, st // 4, (st % 4) * P:(st % 4 + 1) * P],
                                                 pr[:, par, hh, st * P:(st + 1) * P], ident)
                        if st % 4 == 3:
                            mm.then_inc(tr, 1)

                def weighted(b, g):
                    hp, th = g // 8, (g // 4) % 2
                    i = b * 8 + g // 4
                    pe.wait_ge(tra, 2 * (b * 32 + g) + 2)
                    pe.wait_ge(trb, 2 * (b * 32 + g) + 2)
                    if i >= 2:
                        pe.wait_ge(pvc, i - 1)
                    for st in range(8):
                        for hh in range(2):
                            at = (2 * hp + hh) * DH
                            mm = nc.tensor.matmul(po[hh * DH:(hh + 1) * DH, th, :], va[:, st, at:at + DH],
                                                  ptr[:, hh, st, :], start=(st == 0), stop=(st == 7),
                                                  skip_group_check=True)
                    mm.then_inc(pv, 1)

                def image(b):
                    later = b > 0
                    pe.wait_ge(xg_ready, CC * (b + 1))
                    banks = [ps[:, i // 2, (i % 2) * HALF:(i % 2 + 1) * HALF] for i in range(4)]
                    for i in range(24):
                        if later or i >= 4:
                            pe.wait_ge(pj_used, NB * b + i - 3)
                        for ci in range(CC):
                            if i < 16:
                                lhs, rhs = qkw[:, ci, i // 2 * P:(i // 2 + 1) * P], xg[:, ci, i % 2 * HALF:(i % 2 + 1) * HALF]
                            else:
                                lhs, rhs = xg[:, ci, (i - 16) * P:(i - 15) * P], vpw[:, ci, :]
                            mm = nc.tensor.matmul(banks[i % 4], lhs, rhs, start=(ci == 0), stop=(ci == CC - 1))
                        mm.then_inc(pj, 1)
                    pe.wait_ge(pj_used, NB * b + 24)
                    for g in range(32):
                        hp, tt = g // 8, g % 8
                        for hh in range(2):
                            if g > 0:
                                pe.wait_ge(ex, 2 * (b * 32 + g) - 1 + hh)
                        for sh in range(2):
                            for hh in range(2):
                                r = slice(hh * DH, (hh + 1) * DH)
                                mm = nc.tensor.matmul(ps[:, hh, sh * HALF:(sh + 1) * HALF],
                                                      qk[r, hp, tt * P:(tt + 1) * P],
                                                      qk[r, CC + hp, sh * HALF:(sh + 1) * HALF],
                                                      start=True, stop=True)
                                if sh == 1:
                                    mm.then_inc(qk_done, 1)
                        if g > 0:
                            for hh in range(2):
                                transposes(b, g - 1, hh)
                            if g % 4 == 0:
                                weighted(b, g - 1)
                    for hh in range(2):
                        transposes(b, 31, hh)
                    weighted(b, 31)
                    pe.wait_ge(pvc, 8 * (b + 1))
                    for i in range(8):
                        oc, th = i // 2, i % 2
                        if i >= 4:
                            pe.wait_ge(pj_used, NB * b + 24 + i - 3)
                        for ci in range(CC):
                            mm = nc.tensor.matmul(banks[i % 4], pw[:, ci, oc * P:(oc + 1) * P],
                                                  att[:, ci, th * HALF:(th + 1) * HALF],
                                                  start=(ci == 0), stop=(ci == CC - 1))
                        mm.then_inc(pj, 1)

                for b in range(B):
                    image(b)

            @block.scalar
            def _(act):
                banks = [ps[:, i // 2, (i % 2) * HALF:(i % 2 + 1) * HALF] for i in range(4)]
                act.wait_ge(sq, 1)
                nc.scalar.activation(gsc[:, :, :], gsc[:, :, :], ACT.Sqrt).then_inc(sq, 1)
                nc.scalar.activation(rsum[:, 0, :], co("query_pos").to_broadcast([P, 2]), ACT.Exp).then_inc(st_own, 1)

                def image(b):
                    act.wait_ge(gready, 1)
                    for cc in range(CC):
                        if b > 0:
                            act.wait_ge(pj_used, NB * b)
                        src, s_, b_ = xs[:, cc, b, :], gsc[:, cc, b:b + 1], gbi[:, cc, b:b + 1]
                        nc.scalar.activation(xg[:, cc, :], src, ACT.Identity, bias=b_, scale=s_).then_inc(xg_ready, 1)
                    for g in range(32):
                        for hh in range(2):
                            u = 2 * (b * 32 + g) + hh
                            act.wait_ge(mx, u + 1)
                            if u >= 4:
                                act.wait_ge(tr, 2 * u - 6)
                            nc.scalar.activation(pr[:, g % 2, hh, :], ps[:, hh, :], ACT.Exp, bias=rmax[:, g % 2, hh:hh + 1],
                                                 accum_out=rsum[:, g % 2, hh:hh + 1]).then_inc(ex, 1)
                        if g > 0:
                            half_copy(b, g - 1)
                            if g % 4 == 0:
                                out_copy(b, g - 1)
                    half_copy(b, 31)
                    out_copy(b, 31)

                def half_copy(b, g):
                    for hh in range(2):
                        u = 2 * (b * 32 + g) + hh
                        act.wait_ge(tr, 2 * u + 1)
                        if g % 4 == 0 and not (b == 0 and g == 0):
                            act.wait_ge(pv, b * 8 + g // 4)
                        nc.scalar.activation(ptr[:, hh, 0:4, (g % 4) * P:(g % 4 + 1) * P],
                                             pp_[:, 0, :].rearrange("p (a b) -> p a b", a=4), ACT.Copy).then_inc(tra, 1)

                def out_copy(b, g):
                    i = b * 8 + g // 4
                    hp, th = g // 8, (g // 4) % 2
                    act.wait_ge(pv, i + 1)
                    nc.scalar.activation(att[:, hp, th * HALF:(th + 1) * HALF], po[:, th, :], ACT.Copy).then_inc(pvc, 1)

                for b in range(B):
                    image(b)

            @block.vector
            def _(dve):
                own = 0

                def chain(ins):
                    nonlocal own
                    own += 1
                    ins.then_inc(st_v, 1)
                    dve.wait_ge(st_v, own)

                for i in range(CC * B):
                    cc, b = i // B, i % B
                    for h in range(2):
                        nc.vector.bn_stats(stats[:, cc, b, h, :], xs[:, cc, b, h * HALF:(h + 1) * HALF])
                chain(nc.vector.memset(mv[:, 0, 0:1], 0.0))
                for i in range(CC * B):
                    last = nc.vector.bn_aggr(mvt[:, i, :], stats[:, i // B, i % B, :, :])
                chain(last)
                nc.vector.tensor_copy(mv[:, 0, :], mvt[:, :, 0]).then_inc(gm, 1)
                dve.wait_ge(gd, 1)
                mean = dev
                chain(nc.vector.tensor_tensor(mv[:, 1, :], po[:, 0, 0:8], mvt[:, :, 0], ALU.subtract))
                chain(nc.vector.tensor_tensor(mv[:, 1, :], mv[:, 1, :], mv[:, 1, :], ALU.mult))
                nc.vector.tensor_tensor(dev[:, :], mv[:, 1, :], mvt[:, :, 1], ALU.add).then_inc(gm, 1)
                dve.wait_ge(gd, 2)
                gs = gsc[:, :, :].rearrange("p a b -> p (a b)")
                nc.vector.tensor_scalar(gs, po[:, 1, 0:8], EPS, None, ALU.add).then_inc(sq, 1)
                dve.wait_ge(sq, 2)
                chain(nc.vector.reciprocal(gs, gs))
                chain(nc.vector.tensor_tensor(gsc[:, :, :], gsc[:, :, :], sm("gn_w")[:, :, None].to_broadcast([P, CC, B]),
                                              ALU.mult))
                gb = gbi[:, :, :].rearrange("p a b -> p (a b)")
                chain(nc.vector.tensor_tensor(gb, gs, po[:, 0, 0:8], ALU.mult))
                nc.vector.tensor_tensor(gbi[:, :, :], sm("gn_b")[:, :, None].to_broadcast([P, CC, B]), gbi[:, :, :],
                                        ALU.subtract).then_inc(gready, 1)
                banks = [ps[:, i // 2, (i % 2) * HALF:(i % 2 + 1) * HALF] for i in range(4)]

                def image(b):
                    for i in range(24):
                        dve.wait_ge(pj, NB * b + i + 1)
                        if i < 16:
                            bias = sm("q_b" if i < 8 else "k_b", i // 2 % CC, i // 2 % CC + 1)
                            nc.vector.tensor_scalar(qk[:, i // 2, i % 2 * HALF:(i % 2 + 1) * HALF], banks[i % 4], bias, SC,
                                                    ALU.add, ALU.mult).then_inc(pj_used, 1)
                        else:
                            nc.vector.tensor_tensor(va[:, i - 16, :], banks[i % 4], sm("v_b"), ALU.add
                                                    ).then_inc(pj_used, 1)
                    for g in range(32):
                        for hh in range(2):
                            u = 2 * (b * 32 + g) + hh
                            dve.wait_ge(qk_done, u + 1)
                            nc.vector.tensor_reduce(rmax[:, g % 2, hh:hh + 1], ps[:, hh, :], X, ALU.max, negate=True
                                                    ).then_inc(mx, 1)
                        for hh in range(2):
                            u = 2 * (b * 32 + g) + hh
                            dve.wait_ge(ex, u + 1)
                            nc.vector.reciprocal(rinv[:, g % 2, hh:hh + 1], rsum[:, g % 2, hh:hh + 1]).then_inc(ri, 1)
                        if g > 0:
                            half_copy(b, g - 1)
                    half_copy(b, 31)
                    for i in range(8):
                        oc, th = i // 2, i % 2
                        cols = slice(th * HALF, (th + 1) * HALF)
                        dve.wait_ge(pj, NB * b + 24 + i + 1)
                        dst = xs[:, oc, b, cols]
                        dve.wait_ge(xg_ready, CC * (b + 1))
                        nc.vector.scalar_tensor_tensor(out=dst, in0=banks[i % 4], scalar=sm("proj_b", oc, oc + 1),
                                                       in1=xg[:, oc, cols], op0=ALU.add, op1=ALU.add
                                                       ).then_inc(pj_used, 1)
                        dve.wait_ge(pj_used, NB * b + 24 + i + 1)
                        dve.sem_inc(fin, 1)

                def half_copy(b, g):
                    for hh in range(2):
                        u = 2 * (b * 32 + g) + hh
                        dve.wait_ge(tr, 2 * u + 2)
                        if g % 4 == 0 and not (b == 0 and g == 0):
                            dve.wait_ge(pv, b * 8 + g // 4)
                        nc.vector.tensor_copy(ptr[:, hh, 4:8, (g % 4) * P:(g % 4 + 1) * P],
                                              pp_[:, 1, :].rearrange("p (a b) -> p a b", a=4)).then_inc(trb, 1)

                for b in range(B):
                    image(b)

            @block.gpsimd
            def _(pool):
                with pool.Fori(0, B) as b:
                    for g in range(32):
                        for hh in range(2):
                            u = 2 * (b * 32 + g) + hh
                            pool.wait_ge(ri, u + 1)
                            pool.sem_inc(pool_held, 1)
                            nc.gpsimd.tensor_scalar(pr[:, g % 2, hh, :], pr[:, g % 2, hh, :], rinv[:, g % 2, hh:hh + 1],
                                                    1.0, ALU.mult, ALU.mult).then_inc(nm, 1)


def kernel(**inputs):
    import concourse.bacc as bacc
    from concourse import mybir as _mybir
    from concourse.bass_utils import run_bass_kernel_spmd

    def arr(name):
        return np.asarray(inputs[name])

    L0, L1 = "L0_conv_", "L1_conv_"
    cols = lambda v, k: v.reshape(k, P).T
    small = np.zeros((P, SMALL), np.float32)

    def put(name, v):
        at, w = _COLS[name]
        small[:, at:at + w] = v

    for name, key, k in (("bn1_g", L0 + "bn1_g", CC), ("bn1_b", L0 + "bn1_b", CC), ("bn2_g", L0 + "bn2_g", CC),
                         ("bn2_b", L0 + "bn2_b", CC), ("out_b", L0 + "out_b", CC), ("mlp_b2", L0 + "mlp_b2", CC),
                         ("gn_w", L1 + "gn_w", CC), ("gn_b", L1 + "gn_b", CC), ("proj_b", L1 + "proj_b", CC),
                         ("mlp_b1", L0 + "mlp_b1", HC)):
        put(name, cols(arr(key), k))
    qkv_b = arr(L1 + "qkv_b").reshape(G, 3, DH)
    put("q_b", cols(qkv_b[:, 0].reshape(C), CC))
    put("k_b", cols(qkv_b[:, 1].reshape(C), CC))
    put("v_b", np.broadcast_to(qkv_b[:, 2].reshape(1, C), (P, C)))
    both = lambda v: np.concatenate([v, v], axis=0)
    put("dw_w", both(arr(L0 + "off_dw_w").reshape(DH, 36)))
    put("dw_b", both(arr(L0 + "off_dw_b").reshape(DH, 1)))
    put("cpb_b2", arr(L0 + "cpb_b2").reshape(P, 1))
    put("cpb_b3", np.broadcast_to(arr(L0 + "cpb_b3").reshape(1, 1), (P, 1)))
    w3 = np.zeros((P, 63), np.float32)
    w3[:, 31] = arr(L0 + "cpb_w3")[:, 0]
    put("w3_window", w3)
    put("cpb_w2", arr(L0 + "cpb_w2"))
    w1c = arr(L0 + "cpb_w1")
    axis = (np.arange(P) // 32) % 2
    put("w1_rows", w1c[axis])
    b1_rows = np.zeros((P, P), np.float32)
    b1_rows[axis == 1] = arr(L0 + "cpb_b1")
    put("b1_rows", b1_rows)
    pwo = arr(L0 + "off_pw_w")
    put("pw_feat", both(pwo[axis].T))
    put("pw_x", both(pwo[np.zeros(P, int)].T))
    put("pw_y", both(pwo[np.ones(P, int)].T))

    const = np.zeros((P, NCONST), np.float32)

    def putc(name, v):
        at, w = _CONST[name]
        const[:, at:at + w] = v

    p = np.arange(P)
    j = np.arange(J)
    putc("ident", np.eye(P, dtype=np.float32))
    putc("grid_x", np.broadcast_to(j % WD, (P, J)))
    putc("grid_y", np.broadcast_to(j // WD, (P, J)))
    putc("grid_feat", np.where(axis[:, None] == 0, j % WD, j // WD))
    putc("query_pos", (np.float32(2.0) * (p % 32).astype(np.float32) / np.float32(WW - 1) - np.float32(1.0))[:, None])
    putc("neg_ix", -(p % 32)[:, None])
    putc("neg_iy", -(4 * np.arange(8)[None, :] + (p // 32)[:, None]))
    putc("group_mean", (p[:, None] // GCH == p[None, :] // GCH) / GCH)
    i = np.arange(T)
    onehot = np.zeros((P, T), np.float32)
    for part in range(2):
        onehot[part * 64 + i % WW, i] = 1
        onehot[part * 64 + 32 + i // WW, i] = 1

    def diagonal(w):
        o = np.zeros((P, CC, P), np.float32)
        for g in range(G):
            a = (g % 2) * DH
            o[a:a + DH, g // 2, a:a + DH] = w[g].T
        return o

    rows = lambda w, k: w.reshape(k, P, -1).transpose(1, 0, 2)
    qkv_w = arr(L1 + "qkv_w").reshape(G, 3, DH, C)
    qk_w = np.concatenate([qkv_w[:, 0].reshape(C, C).T, qkv_w[:, 1].reshape(C, C).T], axis=1)
    data = [
        ("x", arr("x").reshape(B, CC, P, T).transpose(2, 1, 0, 3)),
        ("small", small), ("const", const), ("onehot", onehot),
        ("qw", diagonal(arr(L0 + "qw"))), ("kw", diagonal(arr(L0 + "kw"))), ("vw", diagonal(arr(L0 + "vw"))),
        ("ow", rows(arr(L0 + "out_w").T, CC)), ("w1", rows(arr(L0 + "mlp_w1").T, CC)),
        ("w2", rows(arr(L0 + "mlp_w2").T, HC)), ("qkw", rows(qk_w, CC)),
        ("vpw", rows(qkv_w[:, 2].reshape(C, C).T, CC)), ("pw", rows(arr(L1 + "proj_w").T, CC)),
    ]
    nc = bacc.Bacc("TRN2", target_bir_lowering=False, num_devices=1)
    arrays, args = {}, []
    for name, a in data:
        a = np.ascontiguousarray(a)
        arrays[f"in_{name}"] = a
        args.append(nc.dram_tensor(f"in_{name}", a.shape, _mybir.dt.from_np(a.dtype), kind="ExternalInput").ap())
    out = nc.dram_tensor("out", (P, CC, B, T), _mybir.dt.float32, kind="ExternalOutput").ap()
    deformable_then_attention(nc, *args, out)
    r = run_bass_kernel_spmd(nc, [arrays], core_ids=[0])
    got = r.results[0]["out"]
    return np.ascontiguousarray(got.transpose(2, 1, 0, 3)).reshape(B, C, HH, WW)
```

```python
import math
from contextlib import ExitStack

import numpy as np

import concourse.bass as bass
from concourse import mybir

B, C, HH, WW = 2, 512, 32, 32
T = HH * WW
P = 128
CC = C // P
G, DH = 8, 64
NCH = B * CC
HD = WD = 8
J = HD * WD
HALF = T // 2
HID = 4 * C
HC = HID // P
EPS = 1e-5
STEPS = J // 2
NG = 32
GCH = C // NG

_COLS = {}


def _col(name, width):
    at = sum(w for _, w in _COLS.values())
    _COLS[name] = (at, width)


for _n, _w in (("bn1_g", CC), ("bn1_b", CC), ("bn2_g", CC), ("bn2_b", CC), ("out_b", CC), ("mlp_b2", CC),
               ("gn_w", CC), ("gn_b", CC), ("proj_b", CC), ("mlp_b1", HC), ("q_b", CC), ("k_b", CC),
               ("dw_w", 36), ("dw_b", 1), ("cpb_b2", 1), ("cpb_b3", 1),
               ("w3_window", 63), ("cpb_w2", P), ("w1_rows", P), ("b1_rows", P),
               ("pw_feat", P), ("pw_x", P), ("pw_y", P), ("v_b", C)):
    _col(_n, _w)
SMALL = sum(w for _, w in _COLS.values())

_CONST = {}
for _n, _w in (("ident", P), ("grid_feat", J), ("grid_x", J), ("grid_y", J), ("query_pos", 1), ("neg_ix", 1),
               ("neg_iy", 8), ("group_mean", P)):
    _CONST[_n] = (sum(w for _, w in _CONST.values()), _w)
NCONST = sum(w for _, w in _CONST.values())


def deformable_then_attention(nc, x_d, small_d, const_d, onehot_d, qw_d, kw_d, vw_d, ow_d, w1_d, w2_d, qkw_d, vpw_d,
                              pw_d, out_d):
    fp32 = mybir.dt.float32
    f32r = mybir.dt.float32r
    ACT = mybir.ActivationFunctionType
    ALU = mybir.AluOpType
    AX = mybir.AxisListType
    X = AX.X
    outer = ExitStack()
    with outer:
        def sb(ctx, name, shape, dt=fp32):
            return ctx.enter_context(nc.sbuf_tensor(name, shape, dt))

        def pb(ctx, name, shape):
            return ctx.enter_context(nc.psum_tensor(name, shape, fp32))

        def sem(ctx, name):
            return ctx.enter_context(nc.semaphore(name))

        xs = sb(outer, "xs", [P, CC, B, T])
        ao = sb(outer, "ao", [P, NCH, T])
        small = sb(outer, "small", [P, SMALL])
        const = sb(outer, "const", [P, NCONST])

        def sm(name, a=0, b=None):
            at, w = _COLS[name]
            return small[:, at + a:at + (w if b is None else b)]

        def co(name, a=0, b=None):
            at, w = _CONST[name]
            return const[:, at + a:at + (w if b is None else b)]

        ident = co("ident")
        stats = sb(outer, "stats", [P, B, 2, CC, 6])
        pool_held, dve_held, act_held, pe_held = (sem(outer, x) for x in ("pool_held", "dve_held", "act_held", "pe_held"))

        with ExitStack() as l0:
            q = sb(l0, "q", [P, NCH, T])
            kall = sb(l0, "kall", [P, NCH, J])
            vall = sb(l0, "vall", [P, NCH, P])
            feat = sb(l0, "feat", [P, 2, NCH, J])

            with ExitStack() as a:
                xn = sb(a, "xn", [P, CC, B, T])
                xnt = sb(a, "xnt", [P, B, 8, C])
                qw = sb(a, "qw", [P, CC, P])
                kw = sb(a, "kw", [P, CC, P])
                vw = sb(a, "vw", [P, CC, P])
                bn_s = sb(a, "bn_s", [P, CC])
                dw = sb(a, "dw", [P, NCH, HD, WD])
                dwt = sb(a, "dwt", [P, NCH, HD, WD])
                kv = sb(a, "kv", [P, NCH, 2, J])
                pq = pb(a, "pq", [P, 4, HALF])
                pt = pb(a, "pt", [P, 4, C])
                wt = ao[:, :, :]
                flat = xn[:, :, :, :].rearrange("p a b c -> p (a b c)")
                th_f, th_x, th_y, s1, s2, hx = (flat[:, i * 1024:(i + 1) * 1024] for i in range(6))

                s_x = [sem(a, f"s_x{cc}") for cc in range(CC)]
                s_qw = sem(a, "s_qw")
                s_small = sem(a, "s_small")
                s_w = sem(a, "s_w")
                s_bn = sem(a, "s_bn")
                s_xn = sem(a, "s_xn")
                s_q = sem(a, "s_q")
                s_qc = sem(a, "s_qc")
                s_t = sem(a, "s_t")
                s_tc = sem(a, "s_tc")
                s_dw = sem(a, "s_dw")
                s_dwc = sem(a, "s_dwc")
                s_gelu = sem(a, "s_gelu")
                s_off = sem(a, "s_off")
                s_tanh = sem(a, "s_tanh")
                s_f = sem(a, "s_f")
                s_fa = sem(a, "s_fa")
                s_hy = sem(a, "s_hy")
                s_hv = sem(a, "s_hv")
                s_wt = sem(a, "s_wt")
                s_kv = sem(a, "s_kv")
                s_kvc = sem(a, "s_kvc")
                s_k = sem(a, "s_k")
                s_kc = sem(a, "s_kc")
                block = a.enter_context(nc.Block())

                @block.sync
                def _(sp):
                    sp.dma_start(small[:, :], small_d).then_inc(s_small, 16)
                    for cc in range(CC):
                        sp.dma_start(xs[:, cc, :, :], x_d[:, cc, :, :]).then_inc(s_x[cc], 16)
                        if cc == 0:
                            sp.dma_start(qw[:, :, :], qw_d).then_inc(s_qw, 16)
                            sp.dma_start(const[:, :], const_d).then_inc(s_w, 16)
                    sp.dma_start(kw[:, :, :], kw_d).then_inc(s_w, 16)
                    sp.dma_start(vw[:, :, :], vw_d).then_inc(s_w, 16)

                @block.tensor
                def _(pe):
                    pe.wait_ge(s_qw, 16)
                    pe.wait_ge(s_w, 48)
                    for i in range(NCH * 2):
                        n, h = i // 2, i % 2
                        b, cc = n % B, n // B
                        pe.wait_ge(s_xn, cc + 1)
                        if i >= 4:
                            pe.wait_ge(s_qc, i - 3)
                        nc.tensor.matmul(pq[:, i % 4, :], qw[:, cc, :], xn[:, cc, b, h * HALF:(h + 1) * HALF],
                                         start=True, stop=True).then_inc(s_q, 1)
                    for i in range(B * 8):
                        b, t = i // 8, i % 8
                        if i >= 4:
                            pe.wait_ge(s_tc, i - 3)
                        for cc in range(CC):
                            mm = nc.tensor.transpose(pt[:, i % 4, cc * P:(cc + 1) * P],
                                                     xn[:, cc, b, t * P:(t + 1) * P], ident)
                        mm.then_inc(s_t, 1)
                    pe.wait_ge(s_gelu, 1)
                    pe.wait_ge(s_qc, 2 * NCH)
                    dwf = dw[:, :, :, :].rearrange("p a b c -> p (a b c)")
                    pe.wait_ge(s_tc, B * 8)
                    for v, name in enumerate(("pw_feat", "pw_x", "pw_y")):
                        for par in range(2):
                            r = slice(par * DH, (par + 1) * DH)
                            o = pq[:, 2 * v + par, :] if v < 2 else pt[:, par, :]
                            at = _COLS[name][0]
                            nc.tensor.matmul(o, small[r, at:at + P], dwf[r, :], start=True, stop=True).then_inc(s_off, 1)
                    wtf = wt.rearrange("p t (a n j) -> p t a n j", a=2, n=NCH)
                    pe.wait_ge(s_wt, 8)
                    for n in range(NCH):
                        b, cc = n // CC, n % CC
                        for par in range(2):
                            r = slice(par * DH, (par + 1) * DH)
                            for t in range(8):
                                mm = nc.tensor.matmul(pt[r, 2, n * J:(n + 1) * J],
                                                      xnt[:, b, t, cc * P + par * DH:cc * P + (par + 1) * DH],
                                                      wtf[:, t, par, n, :], start=(t == 0), stop=(t == 7))
                    mm.then_inc(s_kv, 1)
                    pe.wait_ge(s_kvc, 2)
                    for n in range(NCH):
                        mm = nc.tensor.matmul(pt[:, 3, n * J:(n + 1) * J], kw[:, n % CC, :], kv[:, n, 0, :],
                                              start=True, stop=True)
                    mm.then_inc(s_k, 1)
                    pe.wait_ge(s_tanh, 6)
                    for n in range(NCH):
                        mm = nc.tensor.matmul(pq[:, n // 4, (n % 4) * P:(n % 4 + 1) * P],
                                              kv[:, n, :, :].rearrange("p a j -> p (a j)"), vw[:, n % CC, :],
                                              start=True, stop=True)
                    mm.then_inc(s_k, 1)

                @block.scalar
                def _(act):
                    for i in range(NCH * 2):
                        n, h = i // 2, i % 2
                        b, cc = n % B, n // B
                        act.wait_ge(s_q, i + 1)
                        nc.scalar.activation(q[:, b * CC + cc, h * HALF:(h + 1) * HALF], pq[:, i % 4, :],
                                             ACT.Copy).then_inc(s_qc, 1)
                    for i in range(B * 8):
                        act.wait_ge(s_t, i + 1)
                        nc.scalar.activation(xnt[:, i // 8, i % 8, :], pt[:, i % 4, :], ACT.Copy).then_inc(s_tc, 1)
                    dwf = dw[:, :, :, :].rearrange("p a b c -> p (a b c)")
                    act.wait_ge(s_dw, 1)
                    nc.scalar.activation(dwf, dwf, ACT.Gelu, bias=sm("dw_b")).then_inc(s_gelu, 1)
                    for v, dst in enumerate((th_f, th_x, th_y)):
                        for par in range(2):
                            act.wait_ge(s_off, 2 * v + par + 1)
                            o = pq[:, 2 * v + par, :] if v < 2 else pt[:, par, :]
                            nc.scalar.activation(dst[:, par * 512:(par + 1) * 512], o, ACT.Tanh).then_inc(s_tanh, 1)
                    act.wait_ge(s_f, 1)
                    nc.scalar.activation(s1, th_f, ACT.Abs).then_inc(s_fa, 1)
                    act.wait_ge(s_fa, 1)
                    nc.scalar.activation(s1, s1, ACT.Ln, bias=1.0).then_inc(s_fa, 1)
                    nc.scalar.activation(s2, th_f, ACT.Sign).then_inc(s_fa, 1)
                    act.wait_ge(s_f, 3)
                    act.wait_ge(s_fa, 3)
                    nc.scalar.activation(hx, th_x, ACT.Abs, bias=co("neg_ix")).then_inc(s_hy, 1)
                    for t in range(8):
                        if t == 0:
                            act.wait_ge(s_f, 4)
                            act.wait_ge(s_hy, 1)
                        if t >= 2:
                            act.wait_ge(s_hv, t)
                        nc.scalar.activation((th_x, s1)[t % 2], th_y, ACT.Abs, bias=co("neg_iy", t, t + 1)).then_inc(s_hy, 1)
                    act.wait_ge(s_kv, 1)
                    nc.scalar.activation(kv[:, :, 0, :], pt[:, 2, :].rearrange("p (n j) -> p n j", n=NCH),
                                         ACT.Copy).then_inc(s_kvc, 1)
                    act.wait_ge(s_k, 2)
                    for h in range(2):
                        nc.scalar.activation(vall[:, h * 4:(h + 1) * 4, :].rearrange("p a b -> p (a b)"), pq[:, h, :],
                                             ACT.Copy).then_inc(s_kc, 1)

                @block.vector
                def _(dve):
                    dve.wait_ge(s_small, 16)
                    nc.vector.tensor_scalar(bn_s[:, :], sm("bn1_g"), 1.0 / math.sqrt(1.0 + EPS), None,
                                            ALU.mult).then_inc(s_bn, 1)
                    dve.wait_ge(s_bn, 1)
                    for cc in range(CC):
                        dve.wait_ge(s_x[cc], 16)
                        nc.vector.tensor_scalar(xn[:, cc, :, :], xs[:, cc, :, :], bn_s[:, cc:cc + 1],
                                                sm("bn1_b", cc, cc + 1), ALU.mult, ALU.add).then_inc(s_xn, 1)
                    dve.wait_ge(s_qc, 2 * NCH)
                    qv = q[:, :, :].rearrange("p n (y x) -> p n y x", y=HH)
                    done = 0
                    first = True
                    taps = [(2, 2)] + [(ky, kx) for ky in range(6) for kx in range(6) if (ky, kx) != (2, 2)]
                    for ky, kx in taps:
                        y0, x0 = (1 if ky == 0 else 0), (1 if kx == 0 else 0)
                        y1, x1 = (HD - 1 if ky == 5 else HD), (WD - 1 if kx == 5 else WD)
                        ys, xs_ = 4 * y0 - 1 + ky, 4 * x0 - 1 + kx
                        src = qv[:, :, ys:ys + 4 * (y1 - y0 - 1) + 1:4, xs_:xs_ + 4 * (x1 - x0 - 1) + 1:4]
                        dst = dw[:, :, y0:y1, x0:x1]
                        w = sm("dw_w", ky * 6 + kx, ky * 6 + kx + 1)
                        if done:
                            dve.wait_ge(s_dwc, done)
                        if first:
                            nc.vector.tensor_scalar(dst, src, w, None, ALU.mult).then_inc(s_dwc, 1)
                            first = False
                        else:
                            tmp = dwt[:, :, y0:y1, x0:x1]
                            nc.vector.tensor_scalar(tmp, src, w, None, ALU.mult).then_inc(s_dwc, 1)
                            done += 1
                            dve.wait_ge(s_dwc, done)
                            nc.vector.tensor_tensor(dst, dst, tmp, ALU.add).then_inc(s_dwc, 1)
                        done += 1
                    dve.wait_ge(s_dwc, done)
                    nc.vector.engine_nop().then_inc(s_dw, 1) if False else nc.vector.tensor_scalar(
                        dwt[:, 0, 0, 0:1], dw[:, 0, 0, 0:1], 1.0, None, ALU.mult).then_inc(s_dw, 1)
                    own = 0

                    def grid_of(dst, grid, waited):
                        nonlocal own
                        dve.wait_ge(s_tanh, waited)
                        g = grid[:, None, :].to_broadcast([P, 2 * NCH, J])
                        d3 = dst.rearrange("p (n j) -> p n j", j=J)
                        nc.vector.tensor_scalar(dst, dst, 4.0, None, ALU.mult).then_inc(s_bn, 1)
                        own += 1
                        dve.wait_ge(s_bn, 1 + own)
                        nc.vector.tensor_tensor(d3, d3, g, ALU.add).then_inc(s_bn, 1)
                        own += 1
                        dve.wait_ge(s_bn, 1 + own)
                        nc.vector.tensor_scalar(dst, dst, 2.0 / (HD - 1), -1.0, ALU.mult, ALU.add).then_inc(s_bn, 1)
                        own += 1
                        dve.wait_ge(s_bn, 1 + own)

                    grid_of(th_f, co("grid_feat"), 2)
                    nc.vector.tensor_scalar(th_f, th_f, -1.0, co("query_pos"), ALU.mult, ALU.add).then_inc(s_f, 1)
                    for dst, name, k in ((th_x, "grid_x", 4), (th_y, "grid_y", 6)):
                        grid_of(dst, co(name), k)
                        nc.vector.tensor_scalar(dst, dst, 1.0, WW / 2.0, ALU.add, ALU.mult).then_inc(s_bn, 1)
                        own += 1
                        dve.wait_ge(s_bn, 1 + own)
                        nc.vector.tensor_scalar(dst, dst, -0.5, None, ALU.add).then_inc(s_f, 1)
                        if name == "grid_x":
                            dve.wait_ge(s_fa, 3)
                            nc.vector.tensor_tensor(feat[:, :, :, :].rearrange("p a n j -> p (a n j)"), s1, s2,
                                                    ALU.mult).then_inc(s_f, 1)
                    dve.wait_ge(s_hy, 1)
                    nc.vector.tensor_scalar(hx, hx, -1.0, 0.0, ALU.add, ALU.min).then_inc(s_hv, 1)
                    for t in range(8):
                        cur = (th_x, s1)[t % 2]
                        dve.wait_ge(s_hy, t + 2)
                        nc.vector.tensor_scalar(s2, cur, -1.0, 0.0, ALU.add, ALU.min).then_inc(s_hv, 1)
                        dve.wait_ge(s_hv, t + 2)
                        nc.vector.tensor_tensor(wt[:, t, :], s2, hx, ALU.mult).then_inc(s_wt, 1)
                        dve.wait_ge(s_wt, t + 1)
                    dve.wait_ge(s_kvc, 1)
                    nc.vector.tensor_copy(kv[:, :, 1, :], pt[:, 2, :].rearrange("p (n j) -> p n j", n=NCH)
                                          ).then_inc(s_kvc, 1)
                    dve.wait_ge(s_k, 1)
                    nc.vector.tensor_scalar(kall[:, :, :].rearrange("p n j -> p (n j)"), pt[:, 3, :], DH ** -0.5, None,
                                            ALU.mult).then_inc(s_kc, 1)

            with ExitStack() as bctx:
                onehot = sb(bctx, "onehot", [P, T], f32r)
                w2h = sb(bctx, "w2h", [P, P], f32r)
                w2l = sb(bctx, "w2l", [P, P], f32r)
                tsl = sb(bctx, "tsl", [P, 2, 2, P], f32r)
                v1 = sb(bctx, "v1", [P, 2, P])
                v2 = sb(bctx, "v2", [P, 2, P])
                vh = sb(bctx, "vh", [P, 2, P], f32r)
                h1h = sb(bctx, "h1h", [P, 4, T], f32r)
                h1l = sb(bctx, "h1l", [P, 4, T], f32r)
                h2 = sb(bctx, "h2", [P, 2, 2, 2, HALF])
                wz = sb(bctx, "wz", [P, 2, 32])
                qs = sb(bctx, "qs", [P, T])
                ks = sb(bctx, "ks", [P, J])
                vs = sb(bctx, "vs", [P, DH])
                sims = sb(bctx, "sims", [P, HALF])
                negm = sb(bctx, "negm", [P, 8])
                psum_ = sb(bctx, "prob_sum", [P, 8])
                prob = sb(bctx, "prob", [P, 8, J])
                probn = sb(bctx, "probn", [P, 8, J])
                pts = sb(bctx, "pts", [P, HALF])
                p1 = pb(bctx, "p1", [P, 2, T])
                p2 = pb(bctx, "p2", [P, 2, HALF])
                sim = pb(bctx, "sim", [P, HALF])
                misc = pb(bctx, "misc", [P, 8, J])
                miscf = misc[:, :, :].rearrange("p a j -> p (a j)")

                const_ready = sem(bctx, "const_ready")
                w2_ready = sem(bctx, "w2_ready")
                rows_own = sem(bctx, "rows_own")
                rows_ready = sem(bctx, "rows_ready")
                l1_done = sem(bctx, "l1_done")
                hi_done = sem(bctx, "hi_done")
                lo_done = sem(bctx, "lo_done")
                l2_done = sem(bctx, "l2_done")
                relu_a = sem(bctx, "relu_a")
                relu_b = sem(bctx, "relu_b")
                wz_ready = sem(bctx, "wz_ready")
                l3_done = sem(bctx, "l3_done")
                kq_ready = sem(bctx, "kq_ready")
                seed_done = sem(bctx, "seed_done")
                sim_done = sem(bctx, "sim_done")
                sim_copied = sem(bctx, "sim_copied")
                turned = sem(bctx, "turned")
                max_done = sem(bctx, "max_done")
                shifted = sem(bctx, "shifted")
                exp_done = sem(bctx, "exp_done")
                sum_done = sem(bctx, "sum_done")
                normed = sem(bctx, "normed")
                turned_back = sem(bctx, "turned_back")
                pt_copied = sem(bctx, "pt_copied")
                vs_ready = sem(bctx, "vs_ready")
                pv_done = sem(bctx, "pv_done")
                ao_done = sem(bctx, "ao_done")
                block = bctx.enter_context(nc.Block())

                LAST_M = STEPS - 1
                UN = 2 * STEPS

                def walk(eng, step):
                    def chunk(n, first, last):
                        for par in range(2):
                            prev = not (first and par == 0)
                            for m in range(4):
                                step(n, par, m, prev, True)
                            with eng.Fori(4, STEPS - 2, 2) as mm:
                                step(n, par, mm, prev, True, parity=0)
                                step(n, par, mm + 1, prev, True, parity=1)
                            step(n, par, LAST_M - 1, prev, True)
                            step(n, par, LAST_M, prev, not (last and par == 1))

                    chunk(0, True, False)
                    with eng.Fori(1, NCH - 1) as n:
                        chunk(n, False, False)
                    chunk(NCH - 1, False, True)

                @block.sync
                def _(sp):
                    sp.nop()

                @block.tensor
                def _(pe):
                    def rows(par_slot, jb):
                        for ih in range(2):
                            mm = nc.tensor.matmul(p1[:, jb, ih * HALF:(ih + 1) * HALF], tsl[:, par_slot, jb, :],
                                                  onehot[:, ih * HALF:(ih + 1) * HALF], start=True, stop=True)
                        mm.then_inc(l1_done, 1)

                    def third(slot, pair_last):
                        for ih in range(2):
                            for jb in range(2):
                                at = ih * J + jb * 32
                                mm = nc.tensor.matmul(sim[at:at + 32, :], wz[:, slot, :], h2[:, slot, jb, ih, :],
                                                      start=False, stop=pair_last, skip_group_check=True)
                        mm.then_inc(l3_done, 1)

                    def seed(n, par, r):
                        pe.wait_ge(kq_ready, 2 * n + 2)
                        pe.sem_inc(pe_held, 1)
                        rr = slice(par * DH, (par + 1) * DH)
                        for ih in range(2):
                            mm = nc.tensor.matmul(sim[ih * J:(ih + 1) * J, :], ks[rr, :],
                                                  qs[rr, ih * HALF:(ih + 1) * HALF], start=True, stop=False,
                                                  skip_group_check=True)
                        mm.then_inc(seed_done, 1)

                    def turn(r):
                        if not (isinstance(r, int) and r < 2):
                            pe.wait_ge(ao_done, 2 * r - 2)
                        for i in range(4):
                            mm = nc.tensor.transpose(miscf[:, i * P:(i + 1) * P], sims[:, i * P:(i + 1) * P], ident)
                        mm.then_inc(turned, 1)

                    def turn_back(r):
                        pe.wait_ge(normed, r)
                        pn = probn[:, :, :].rearrange("p a j -> p (a j)")
                        for i in range(4):
                            mm = nc.tensor.transpose(miscf[:, i * P:(i + 1) * P], pn[:, i * P:(i + 1) * P], ident)
                        mm.then_inc(turned_back, 1)

                    def values(r, pp, ih):
                        if ih == 0:
                            pe.wait_ge(pt_copied, r)
                            pe.wait_ge(vs_ready, r)
                        else:
                            pe.wait_ge(ao_done, 2 * r - 1)
                        pe.sem_inc(pe_held, 1)
                        nc.tensor.matmul(miscf[pp * DH:(pp + 1) * DH, :], vs[ih * J:(ih + 1) * J, :],
                                         pts[ih * J:(ih + 1) * J, :], start=True, stop=True).then_inc(pv_done, 1)

                    def step(n, par, m, prev, nxt, parity=None):
                        sp_ = m % 2 if parity is None else parity
                        r = 2 * n + par
                        s = r * STEPS + m
                        k0 = 2 * s
                        for jb in range(2):
                            k = k0 + jb
                            pe.wait_ge(lo_done, k + 1)
                            if nxt:
                                if jb == 0:
                                    pe.wait_ge(rows_ready, s + 2)
                                rows(1 - sp_, jb)
                            u = 2 * sp_ + jb
                            for ih in range(2):
                                if not (isinstance(k, int) and k == 0):
                                    pe.wait_ge(relu_a if ih == 0 else relu_b, k)
                                cols = slice(ih * HALF, (ih + 1) * HALF)
                                nc.tensor.matmul(p2[:, ih, :], w2h[:, :], h1h[:, u, cols], start=True, stop=False)
                                nc.tensor.matmul(p2[:, ih, :], w2h[:, :], h1l[:, u, cols], start=False, stop=False)
                                nc.tensor.matmul(p2[:, ih, :], w2l[:, :], h1h[:, u, cols], start=False,
                                                 stop=True).then_inc(l2_done, 1)
                        static = isinstance(m, int)
                        if static and m == 1:
                            if prev:
                                pe.wait_ge(sim_copied, r)
                            seed(n, par, r)
                        if not (static and m == 0 and not prev):
                            third(1 - sp_, static and m == 0)
                        if static and prev:
                            if m == 1:
                                turn(r)
                            if m == 3:
                                turn_back(r)
                            if m == LAST_M - 1:
                                values(r, 1 - par, 0)
                            if m == LAST_M:
                                values(r, 1 - par, 1)

                    pe.wait_ge(const_ready, 16)
                    pe.wait_ge(w2_ready, 3)
                    pe.wait_ge(rows_ready, 1)
                    for jb in range(2):
                        rows(0, jb)
                    walk(pe, step)
                    s, r = 2 * NCH * STEPS, 2 * NCH
                    pe.wait_ge(relu_a, 2 * s)
                    pe.wait_ge(relu_b, 2 * s)
                    pe.wait_ge(wz_ready, s)
                    third(1, True)
                    pe.wait_ge(sim_copied, r)
                    turn(r)
                    turn_back(r)
                    values(r, 1, 0)
                    values(r, 1, 1)

                @block.scalar
                def _(act):
                    def hi(u, jb):
                        nc.scalar.activation(h1h[:, u, :], p1[:, jb, :], ACT.Relu).then_inc(hi_done, 1)

                    def copy_sim(r, s):
                        act.wait_ge(l3_done, s)
                        if not (isinstance(r, int) and r < 2):
                            act.wait_ge(turned, r - 1)
                        nc.scalar.activation(sims[:, :], sim[:, :], ACT.Identity, bias=sm("cpb_b3")
                                             ).then_inc(sim_copied, 1)

                    def exp(r):
                        act.wait_ge(shifted, r)
                        nc.scalar.activation(prob[:, :, :], prob[:, :, :], ACT.Exp).then_inc(exp_done, 1)

                    def copy_pt(r):
                        act.wait_ge(turned_back, r)
                        if not (isinstance(r, int) and r < 2):
                            act.wait_ge(pv_done, 2 * r - 2)
                        nc.scalar.activation(pts[:, :], miscf, ACT.Copy).then_inc(pt_copied, 1)

                    def copy_out(r, n, pp, ih):
                        act.wait_ge(pv_done, 2 * r - 1 + ih)
                        rr = slice(pp * DH, (pp + 1) * DH)
                        o = (ao[rr, n, ih * HALF:(ih + 1) * HALF] if isinstance(n, int) else
                             ao[rr, bass.ds(n, 1), ih * HALF:(ih + 1) * HALF].rearrange("p a t -> p (a t)"))
                        nc.scalar.activation(o, miscf[rr, :], ACT.Copy).then_inc(ao_done, 1)

                    def step(n, par, m, prev, nxt, parity=None):
                        sp_ = m % 2 if parity is None else parity
                        r = 2 * n + par
                        s = r * STEPS + m
                        static = isinstance(m, int)
                        if static and prev and m == LAST_M - 1:
                            copy_pt(r)
                        pn = n if par == 1 else n - 1
                        if static and prev and m == LAST_M:
                            copy_out(r, pn, 1 - par, 0)
                        for jb in range(2):
                            k = 2 * s + jb
                            act.wait_ge(l2_done, 2 * k + 1)
                            if jb == 0 and not (isinstance(s, int) and s < 2):
                                act.wait_ge(l3_done, s - 1)
                            nc.scalar.activation(h2[:, sp_, jb, 0, :], p2[:, 0, :], ACT.Relu,
                                                 bias=sm("cpb_b2")).then_inc(relu_a, 1)
                            if nxt:
                                act.wait_ge(l1_done, k + 3)
                                if not (isinstance(k, int) and k < 2):
                                    act.wait_ge(l2_done, 2 * k - 2)
                                hi((2 * sp_ + jb + 2) % 4, jb)
                        if static and prev:
                            if m == 0:
                                copy_sim(r, s)
                            if m == 2:
                                exp(r)
                            if m == LAST_M:
                                copy_out(r, pn, 1 - par, 1)

                    nc.scalar.activation(w2h[:, :], sm("cpb_w2"), ACT.Identity).then_inc(w2_ready, 1)
                    for jb in range(2):
                        act.wait_ge(l1_done, jb + 1)
                        hi(jb, jb)
                    walk(act, step)
                    r = 2 * NCH
                    copy_sim(r, r * STEPS)
                    exp(r)
                    copy_pt(r)
                    copy_out(r, NCH - 1, 1, 0)
                    copy_out(r, NCH - 1, 1, 1)

                @block.vector
                def _(dve):
                    def lo(u, jb):
                        nc.vector.scalar_tensor_tensor(out=h1l[:, u, :], in0=p1[:, jb, :], scalar=0.0,
                                                       in1=h1h[:, u, :].bitcast(fp32), op0=ALU.max,
                                                       op1=ALU.subtract).then_inc(lo_done, 1)

                    def window(m, slot):
                        at = _COLS["w3_window"][0] + 31
                        src = (small[:, at - m:at - m + 32] if isinstance(m, int) else
                               small[:, bass.ds(at - m, 32)])
                        nc.vector.tensor_copy(wz[:, slot, :], src).then_inc(wz_ready, 1)

                    def shift(r):
                        dve.wait_ge(turned, r)
                        if not (isinstance(r, int) and r < 2):
                            dve.wait_ge(normed, r - 1)
                        nc.vector.tensor_reduce(negm[:, :], misc[:, :, :], X, ALU.max, negate=True
                                                ).then_inc(max_done, 1)
                        dve.wait_ge(max_done, r)
                        nc.vector.tensor_tensor(prob[:, :, :], misc[:, :, :],
                                                negm[:, :, None].to_broadcast([P, 8, J]), ALU.add
                                                ).then_inc(shifted, 1)

                    def norm(r):
                        dve.wait_ge(exp_done, r)
                        nc.vector.tensor_reduce(psum_[:, :], prob[:, :, :], X, ALU.add).then_inc(sum_done, 1)
                        dve.wait_ge(sum_done, 2 * r - 1)
                        nc.vector.reciprocal(psum_[:, :], psum_[:, :]).then_inc(sum_done, 1)
                        dve.wait_ge(sum_done, 2 * r)
                        if not (isinstance(r, int) and r < 2):
                            dve.wait_ge(turned_back, r - 1)
                        nc.vector.tensor_tensor(probn[:, :, :], prob[:, :, :],
                                                psum_[:, :, None].to_broadcast([P, 8, J]), ALU.mult
                                                ).then_inc(normed, 1)

                    def step(n, par, m, prev, nxt, parity=None):
                        sp_ = m % 2 if parity is None else parity
                        r = 2 * n + par
                        s = r * STEPS + m
                        static = isinstance(m, int)
                        if static and prev:
                            if m == 2:
                                shift(r)
                            if m == 3:
                                norm(r)
                        for jb in range(2):
                            k = 2 * s + jb
                            dve.wait_ge(l2_done, 2 * k + 2)
                            if jb == 0 and not (isinstance(s, int) and s < 2):
                                dve.wait_ge(l3_done, s - 1)
                            nc.vector.tensor_scalar(h2[:, sp_, jb, 1, :], p2[:, 1, :], sm("cpb_b2"), 0.0, ALU.add,
                                                    ALU.max).then_inc(relu_b, 1)
                            if jb == 1:
                                window(m, sp_)
                            if nxt:
                                dve.wait_ge(hi_done, k + 3)
                                lo((2 * sp_ + jb + 2) % 4, jb)

                    dve.wait_ge(w2_ready, 1)
                    nc.vector.tensor_tensor(w2l[:, :], sm("cpb_w2"), w2h[:, :].bitcast(fp32), ALU.subtract
                                            ).then_inc(w2_ready, 2)
                    for jb in range(2):
                        dve.wait_ge(hi_done, jb + 1)
                        lo(jb, jb)
                    walk(dve, step)
                    shift(2 * NCH)
                    norm(2 * NCH)

                @block.gpsimd
                def _(pool):
                    pool.dma_start(onehot[:, :], onehot_d).then_inc(const_ready, 16)
                    nc.gpsimd.memset(vh[0:64, :, :].bitcast(fp32), 0.0).then_inc(rows_own, 1)
                    w1r = sm("w1_rows")[:, None, :].to_broadcast([P, 2, P])
                    b1r = sm("b1_rows")[:, None, :].to_broadcast([P, 2, P])
                    featf = feat[:, :, :, :].rearrange("p a n j -> p (a n j)")

                    def make_rows(n, par, m, slot):
                        s = (2 * n + par) * STEPS + m
                        own = 3 * s + 1
                        at = par * (NCH * J) + n * J + m
                        f = (featf[:, at:at + 33:32] if isinstance(at, int) else featf[:, bass.ds(at, 2, 32)])
                        if isinstance(s, int) and s == 0:
                            pool.wait_ge(rows_own, 1)
                        else:
                            pool.wait_ge(rows_ready, s)
                            pool.sem_inc(pool_held, 1)
                        nc.gpsimd.tensor_tensor(v1[:, :, :], w1r, f[:, :, None].to_broadcast([P, 2, P]), ALU.mult
                                                ).then_inc(rows_own, 1)
                        pool.wait_ge(rows_own, own + 1)
                        nc.gpsimd.tensor_tensor(v2[:, :, :], v1[:, :, :], b1r, ALU.add).then_inc(rows_own, 1)
                        pool.wait_ge(rows_own, own + 2)
                        nc.gpsimd.tensor_tensor(vh[64:P, :, :], v1[64:P, :, :],
                                                sm("b1_rows")[64:P, None, :].to_broadcast([64, 2, P]), ALU.add
                                                ).then_inc(rows_own, 1)
                        pool.wait_ge(rows_own, own + 3)
                        if not (isinstance(s, int) and s < 2):
                            pool.wait_ge(l1_done, 2 * s - 2)
                        nc.gpsimd.tensor_tensor(tsl[:, slot, :, :], v2[:, :, :], vh[:, :, :].bitcast(fp32),
                                                ALU.subtract).then_inc(rows_ready, 1)

                    def copy_queries(n, r, prev):
                        if prev:
                            pool.wait_ge(seed_done, r)
                            pool.sem_inc(pool_held, 1)
                        dyn = not isinstance(n, int)
                        qsrc = q[:, bass.ds(n, 1), :].rearrange("p a t -> p (a t)") if dyn else q[:, n, :]
                        ksrc = kall[:, bass.ds(n, 1), :].rearrange("p a t -> p (a t)") if dyn else kall[:, n, :]
                        nc.gpsimd.tensor_copy(qs[:, :], qsrc).then_inc(kq_ready, 1)
                        nc.gpsimd.tensor_copy(ks[:, :], ksrc).then_inc(kq_ready, 1)

                    def copy_values(r, pn, pp):
                        if not (isinstance(r, int) and r < 2):
                            pool.wait_ge(pv_done, 2 * r - 2)
                            pool.sem_inc(pool_held, 1)
                        vsrc = (vall[:, pn, pp * DH:(pp + 1) * DH] if isinstance(pn, int) else
                                vall[:, bass.ds(pn, 1), pp * DH:(pp + 1) * DH].rearrange("p a t -> p (a t)"))
                        nc.gpsimd.tensor_copy(vs[:, :], vsrc).then_inc(vs_ready, 1)

                    def step(n, par, m, prev, nxt, parity=None):
                        sp_ = m % 2 if parity is None else parity
                        r = 2 * n + par
                        make_rows(n, par, m, sp_)
                        if isinstance(m, int) and m == 0 and par == 0:
                            copy_queries(n, r, prev)
                        if isinstance(m, int) and m == 3 and prev:
                            copy_values(r, n if par == 1 else n - 1, 1 - par)

                    walk(pool, step)
                    copy_values(2 * NCH, NCH - 1, 1)

        qkw = sb(outer, "qkw", [P, CC, 2 * C])
        w_in = sem(outer, "w_in")

        with ExitStack() as c:
            ow = sb(c, "ow", [P, CC, C])
            w1 = sb(c, "w1", [P, CC, HID])
            w2 = sb(c, "w2", [P, HC, C])
            xb2 = sb(c, "xb2", [P, CC, HALF])
            hid = sb(c, "hid", [P, HC, HALF])
            bn2_s = sb(c, "bn2_s", [P, CC])
            pd = pb(c, "pd", [P, 4, HALF])
            pa = pb(c, "pa", [P, 4, HALF])
            ow_in = sem(c, "ow_in")
            w1_in = sem(c, "w1_in")
            w2_in = sem(c, "w2_in")
            bn2_ready = sem(c, "bn2_ready")
            sum_ready = sem(c, "sum_ready")
            sum_used = sem(c, "sum_used")
            resid = sem(c, "resid")
            xb_ready = sem(c, "xb_ready")
            h_ready = sem(c, "h_ready")
            h_done = sem(c, "h_done")
            block = c.enter_context(nc.Block())

            @block.sync
            def _(sp):
                sp.dma_start(ow[:, :, :], ow_d).then_inc(ow_in, 16)
                sp.dma_start(w1[:, :, :], w1_d).then_inc(w1_in, 16)
                sp.dma_start(w2[:, :, :], w2_d).then_inc(w2_in, 16)
                sp.dma_start(qkw[:, :, :], qkw_d).then_inc(w_in, 16)

            @block.tensor
            def _(pe):
                def chunk(lhs, rhs, n_in, oc, k, t, wait):
                    d = 8 * k + t
                    if wait:
                        pe.wait_ge(sum_used, d - 3)
                    for ci in range(n_in):
                        mm = nc.tensor.matmul(pd[:, t % 4, :], lhs[:, ci, oc * P:(oc + 1) * P], rhs(ci),
                                              start=(ci == 0), stop=(ci == n_in - 1))
                    mm.then_inc(sum_ready, 1)

                def token_block(b, th):
                    k = 2 * b + th
                    later = b > 0
                    cols = slice(th * HALF, (th + 1) * HALF)
                    for oc in range(CC):
                        chunk(ow, lambda ci: aof(b, ci, cols), CC, oc, k, oc, later or k > 0)
                    pe.wait_ge(xb_ready, CC * (k + 1))
                    for i in range(HC):
                        if later or k > 0 or i >= 4:
                            pe.wait_ge(h_done, HC * k + i - 3)
                        for ci in range(CC):
                            mm = nc.tensor.matmul(pa[:, i % 4, :], w1[:, ci, i * P:(i + 1) * P], xb2[:, ci, :],
                                                  start=(ci == 0), stop=(ci == CC - 1))
                        mm.then_inc(h_ready, 1)
                    pe.wait_ge(h_done, HC * (k + 1))
                    for oc in range(CC):
                        chunk(w2, lambda ci: hid[:, ci, :], HC, oc, k, CC + oc, True)

                def aof(b, ci, cols):
                    return ao[:, b * CC + ci, cols]

                pe.wait_ge(ow_in, 16)
                pe.wait_ge(w1_in, 16)
                pe.wait_ge(w2_in, 16)
                for b in range(B):
                    for th in range(2):
                        token_block(b, th)

            @block.scalar
            def _(act):
                with act.Fori(0, 2 * B) as k:
                    for i in range(HC):
                        act.wait_ge(h_ready, HC * k + i + 1)
                        nc.scalar.activation(hid[:, i, :], pa[:, i % 4, :], ACT.Gelu, bias=sm("mlp_b1", i, i + 1)
                                             ).then_inc(h_done, 1)

            @block.vector
            def _(dve):
                nc.vector.tensor_scalar(bn2_s[:, :], sm("bn2_g"), 1.0 / math.sqrt(1.0 + EPS), None, ALU.mult
                                        ).then_inc(bn2_ready, 1)
                dve.wait_ge(bn2_ready, 1)
                with dve.Fori(0, 2 * B) as k:
                    xk = [xs[:, cc, :, :].rearrange("p b t -> p (b t)")[:, bass.ds(k * HALF, HALF)] for cc in range(CC)]
                    for oc in range(CC):
                        dve.wait_ge(sum_ready, 8 * k + oc + 1)
                        nc.vector.scalar_tensor_tensor(out=xk[oc], in0=pd[:, oc, :], scalar=sm("out_b", oc, oc + 1),
                                                       in1=xk[oc], op0=ALU.add, op1=ALU.add).then_inc(resid, 1)
                        dve.wait_ge(resid, 5 * k + oc + 1)
                        dve.sem_inc(dve_held, 1)
                        nc.vector.tensor_scalar(xb2[:, oc, :], xk[oc], bn2_s[:, oc:oc + 1], sm("bn2_b", oc, oc + 1),
                                                ALU.mult, ALU.add).then_inc(xb_ready, 1)
                        dve.sem_inc(sum_used, 1)
                    for oc in range(CC):
                        dve.wait_ge(sum_ready, 8 * k + CC + oc + 1)
                        nc.vector.scalar_tensor_tensor(out=xk[oc], in0=pd[:, oc, :], scalar=sm("mlp_b2", oc, oc + 1),
                                                       in1=xk[oc], op0=ALU.add, op1=ALU.add).then_inc(sum_used, 1)
                    dve.wait_ge(sum_used, 8 * k + 8)
                    sf = stats[:, :, :, :, :].rearrange("p b h c s -> p (b h c s)")
                    for oc in range(CC):
                        ins = nc.vector.bn_stats(sf[:, bass.ds(k * (CC * 6) + oc * 6, 6)], xk[oc])
                    ins.then_inc(resid, 1)

        with ExitStack() as d:
            vpw = sb(d, "vpw", [P, CC, C])
            pw = sb(d, "pw", [P, CC, C])
            qhl = sb(d, "qhl", [P, 2, 2, T], f32r)
            khh = sb(d, "khh", [P, 2, 2, T], f32r)
            kll = sb(d, "kll", [P, 2, 2, T], f32r)
            qlo = sb(d, "qlo", [P, T], f32r)
            va = sb(d, "va", [P, 8, C])
            pr = sb(d, "pr", [P, 4, T])
            ptr = sb(d, "ptr", [P, 2, 2, 8, P])
            mv = sb(d, "mv", [P, 2, CC * B])
            dev = sb(d, "dev", [P, CC * B])
            gsc = sb(d, "gsc", [P, CC, B])
            gbi = sb(d, "gbi", [P, CC, B])
            mvt = sb(d, "mvt", [P, CC * B, 2])
            rmax = sb(d, "rmax", [P, 4])
            rmx8 = sb(d, "rmx8", [P, 4])
            rsum = sb(d, "rsum", [P, 4])
            rinv = sb(d, "rinv", [P, 4])
            att = ao[:, 0:CC, :]
            xg = ao[:, CC:2 * CC, :]
            ps = pb(d, "ps", [P, 2, T])
            pp_ = pb(d, "pp_", [P, 2, HALF])
            po = pb(d, "po", [P, HALF])
            pq2 = pb(d, "pq2", [P, HALF])
            banks = [ps[:, i // 2, (i % 2) * HALF:(i % 2 + 1) * HALF] for i in range(4)]

            def made_in(c, t):
                return pq2[:, :] if c % CC or t in (0, 3) else pp_[:, t - 1, :]

            vpw_in = sem(d, "vpw_in")
            pw_in = sem(d, "pw_in")
            st_own = sem(d, "st_own")
            st_v = sem(d, "st_v")
            gm = sem(d, "gm")
            gd = sem(d, "gd")
            sq = sem(d, "sq")
            gready = sem(d, "gready")
            xg_ready = sem(d, "xg_ready")
            pj = sem(d, "pj")
            pj_used = sem(d, "pj_used")
            made = sem(d, "made")
            rounded = sem(d, "rounded")
            rest = sem(d, "rest")
            dup = sem(d, "dup")
            qk_done = sem(d, "qk_done")
            mx = sem(d, "mx")
            mx8 = sem(d, "mx8")
            ex = sem(d, "ex")
            ri = sem(d, "ri")
            nm = sem(d, "nm")
            tr = sem(d, "tr")
            tra = sem(d, "tra")
            trb = sem(d, "trb")
            pv = sem(d, "pv")
            pvc = sem(d, "pvc")
            fin = sem(d, "fin")
            stored = sem(d, "stored")
            block = d.enter_context(nc.Block())
            HP = CC
            TT = T // P
            UN2 = HP * TT * 2
            MAKE_AT = {2: 0, 4: 1, 6: 2, 8: 3}
            VT = 8

            @block.sync
            def _(sp):
                sp.dma_start(vpw[:, :, :], vpw_d).then_inc(vpw_in, 16)
                sp.dma_start(pw[:, :, :], pw_d).then_inc(pw_in, 16)
                for b in range(B):
                    for hp in range(HP):
                        c = b * HP + hp
                        sp.wait_ge(rounded, 4 * (c + 1))
                        sp.wait_ge(rest, 4 * (c + 1))
                        for hh in range(2):
                            mine, other = slice(hh * DH, (hh + 1) * DH), slice((1 - hh) * DH, (2 - hh) * DH)
                            sp.dma_start(qhl[other, c % 2, hh, :].bitcast(fp32), qlo[mine, :].bitcast(fp32)).then_inc(dup, 16)
                            sp.dma_start(khh[other, c % 2, hh, :].bitcast(fp32), khh[mine, c % 2, hh, :].bitcast(fp32)).then_inc(dup, 16)
                            sp.dma_start(kll[other, c % 2, hh, :].bitcast(fp32), kll[mine, c % 2, hh, :].bitcast(fp32)).then_inc(dup, 16)
                    for i in range(8):
                        sp.wait_ge(fin, 8 * b + i + 1)
                        oc, th = i // 2, i % 2
                        sp.dma_start(out_d[:, oc, b, th * HALF:(th + 1) * HALF],
                                     xs[:, oc, b, th * HALF:(th + 1) * HALF]).then_inc(stored, 16)
                sp.wait_ge(stored, 16 * 8 * B)

            @block.tensor
            def _(pe):
                pe.wait_ge(gm, 1)
                nc.tensor.matmul(po[:, 0:CC * B], co("group_mean"), mv[:, 0, :], start=True, stop=True
                                 ).then_inc(gd, 1)
                pe.wait_ge(gm, 2)
                nc.tensor.matmul(pq2[:, 0:CC * B], co("group_mean"), dev[:, :], start=True, stop=True
                                 ).then_inc(gd, 1)
                pe.wait_ge(w_in, 16)

                def project(b, i, lhs, rhs):
                    n = 2 * VT * b + i
                    if n >= 4:
                        pe.wait_ge(pj_used, n - 3)
                    for ci in range(CC):
                        mm = nc.tensor.matmul(banks[i % 4], lhs(ci), rhs(ci), start=(ci == 0), stop=(ci == CC - 1))
                    mm.then_inc(pj, 1)

                def make(c, t):
                    n = 4 * c + t
                    if c % HP == 0:
                        pe.wait_ge(*((gready, 1) if n == 0 else (rest, 4 * c if t < 3 else n - 2)))
                    else:
                        pe.wait_ge(rest, n)
                    at = (t // 2) * C + (c % HP) * P
                    for ci in range(CC):
                        mm = nc.tensor.matmul(made_in(c, t), qkw[:, ci, at:at + P], xg[:, ci, (t % 2) * HALF:(t % 2 + 1) * HALF],
                                              start=(ci == 0), stop=(ci == CC - 1))
                    mm.then_inc(made, 1)

                def scores(b, v):
                    u, c, tt, hh = b * UN2 + v, b * HP + v // 16, v // 2 % TT, v % 2
                    if v % 16 == 0:
                        pe.wait_ge(dup, 96 * (c + 1))
                    if v >= 2:
                        pe.wait_ge(ex, u - 1)
                    else:
                        pe.wait_ge(pj_used, 2 * VT * b + VT)
                    for sh in range(2):
                        cols = slice(sh * HALF, (sh + 1) * HALF)
                        nc.tensor.matmul(ps[:, hh, cols], qhl[:, c % 2, hh, tt * P:(tt + 1) * P], khh[:, c % 2, hh, cols],
                                         start=True, stop=False)
                        mm = nc.tensor.matmul(ps[:, hh, cols], qhl[:, c % 2, hh, tt * P:(tt + 1) * P],
                                              kll[:, c % 2, hh, cols], start=False, stop=True)
                    mm.then_inc(qk_done, 1)

                def turn(b, v):
                    u = b * UN2 + v
                    pe.wait_ge(nm, u + 1)
                    if u > 0:
                        pe.wait_ge(tra, u)
                        pe.wait_ge(trb, u)
                    for st in range(8):
                        mm = nc.tensor.transpose(pp_[:, st // 4, (st % 4) * P:(st % 4 + 1) * P],
                                                 pr[:, u % 4, st * P:(st + 1) * P], ident)
                        if st % 4 == 3:
                            mm.then_inc(tr, 1)

                def weighted(b, g):
                    hp, n = g // TT, b * (UN2 // 2) + g
                    pe.wait_ge(tra, 2 * n + 2)
                    pe.wait_ge(trb, 2 * n + 2)
                    if n % 4 == 0 and n > 0:
                        pe.wait_ge(pvc, n // 4)
                    for st in range(8):
                        for hh in range(2):
                            at = (2 * hp + hh) * DH
                            mm = nc.tensor.matmul(po[hh * DH:(hh + 1) * DH, (n % 4) * P:(n % 4 + 1) * P],
                                                  va[:, st, at:at + DH], ptr[:, n % 2, hh, st, :],
                                                  start=(st == 0), stop=(st == 7), skip_group_check=True)
                    mm.then_inc(pv, 1)

                for b in range(B):
                    pe.wait_ge(xg_ready, CC * (b + 1))
                    for t in range(4):
                        make(b * HP, t)
                    if b == 0:
                        pe.wait_ge(vpw_in, 16)
                    for i in range(VT):
                        project(b, i, lambda ci: xg[:, ci, i * P:(i + 1) * P], lambda ci: vpw[:, ci, :])
                    for v in range(UN2):
                        scores(b, v)
                        if v >= 2:
                            turn(b, v - 2)
                        if v >= 4 and v % 2 == 0:
                            weighted(b, v // 2 - 2)
                        if v % 16 in MAKE_AT and v // 16 < HP - 1:
                            make(b * HP + v // 16 + 1, MAKE_AT[v % 16])
                    turn(b, UN2 - 2)
                    weighted(b, UN2 // 2 - 2)
                    turn(b, UN2 - 1)
                    weighted(b, UN2 // 2 - 1)
                    pe.wait_ge(pvc, (UN2 // 8) * (b + 1))
                    if b == 0:
                        pe.wait_ge(pw_in, 16)
                    for i in range(8):
                        oc, th = i // 2, i % 2
                        project(b, VT + i, lambda ci: pw[:, ci, oc * P:(oc + 1) * P],
                                lambda ci: att[:, ci, th * HALF:(th + 1) * HALF])

            @block.scalar
            def _(act):
                act.wait_ge(sq, 1)
                nc.scalar.activation(gsc[:, :, :], gsc[:, :, :], ACT.Sqrt).then_inc(sq, 1)

                def round_(c, t):
                    n = 4 * c + t
                    act.wait_ge(made, n + 1)
                    dst, bias = (qhl, "q_b") if t < 2 else (khh, "k_b")
                    for hh in range(2):
                        mine = slice(hh * DH, (hh + 1) * DH)
                        at = _COLS[bias][0] + c % HP
                        ins = nc.scalar.activation(dst[mine, c % 2, hh, (t % 2) * HALF:(t % 2 + 1) * HALF],
                                                   made_in(c, t)[mine, :],
                                                   ACT.Identity, bias=small[mine, at:at + 1])
                    ins.then_inc(rounded, 1)

                def half_copy(b, v):
                    u = b * UN2 + v
                    act.wait_ge(tr, 2 * u + 1)
                    if u >= 4:
                        act.wait_ge(pv, (u - 4) // 2 + 1)
                    nc.scalar.activation(ptr[:, u // 2 % 2, u % 2, 0:4, :], pp_[:, 0, :].rearrange("p (a b) -> p a b", a=4),
                                         ACT.Copy).then_inc(tra, 1)

                def out_copy(b, g):
                    n = b * (UN2 // 2) + g
                    act.wait_ge(pv, n + 1)
                    nc.scalar.activation(att[:, g // TT, (g // 4 % 2) * HALF:(g // 4 % 2 + 1) * HALF], po[:, :],
                                         ACT.Copy).then_inc(pvc, 1)

                for b in range(B):
                    act.wait_ge(gready, 1)
                    for cc in range(CC):
                        if b > 0:
                            act.wait_ge(pj_used, 2 * VT * b)
                        nc.scalar.activation(xg[:, cc, :], xs[:, cc, b, :], ACT.Identity, bias=gbi[:, cc, b:b + 1],
                                             scale=gsc[:, cc, b:b + 1]).then_inc(xg_ready, 1)
                    for t in range(4):
                        round_(b * HP, t)
                    for v in range(UN2):
                        u = b * UN2 + v
                        if v >= 2:
                            half_copy(b, v - 2)
                        act.wait_ge(mx8, u + 1)
                        if u >= 4:
                            act.wait_ge(tr, 2 * u - 6)
                        nc.scalar.activation(pr[:, u % 4, :], ps[:, u % 2, :], ACT.Exp, bias=rmx8[:, u % 4:u % 4 + 1],
                                             scale=DH ** -0.5, accum_out=rsum[:, u % 4:u % 4 + 1]).then_inc(ex, 1)
                        if v % 16 - 1 in MAKE_AT and v // 16 < HP - 1:
                            round_(b * HP + v // 16 + 1, MAKE_AT[v % 16 - 1])
                        if v >= 4 and v % 2 == 0 and (v // 2 - 2) % 4 == 3:
                            out_copy(b, v // 2 - 2)
                    half_copy(b, UN2 - 2)
                    half_copy(b, UN2 - 1)
                    out_copy(b, UN2 // 2 - 1)

            @block.vector
            def _(dve):
                own = 0

                def chain(ins):
                    nonlocal own
                    own += 1
                    ins.then_inc(st_v, 1)
                    dve.wait_ge(st_v, own)

                for i in range(CC * B):
                    last = nc.vector.bn_aggr(mvt[:, i, :], stats[:, i % B, :, i // B, :])
                chain(last)
                nc.vector.tensor_copy(mv[:, 0, :], mvt[:, :, 0]).then_inc(gm, 1)
                dve.wait_ge(gd, 1)
                chain(nc.vector.tensor_tensor(mv[:, 1, :], po[:, 0:8], mvt[:, :, 0], ALU.subtract))
                chain(nc.vector.tensor_tensor(mv[:, 1, :], mv[:, 1, :], mv[:, 1, :], ALU.mult))
                nc.vector.tensor_tensor(dev[:, :], mv[:, 1, :], mvt[:, :, 1], ALU.add).then_inc(gm, 1)
                dve.wait_ge(gd, 2)
                gs = gsc[:, :, :].rearrange("p a b -> p (a b)")
                nc.vector.tensor_scalar(gs, pq2[:, 0:8], EPS, None, ALU.add).then_inc(sq, 1)
                dve.wait_ge(sq, 2)
                chain(nc.vector.reciprocal(gs, gs))
                chain(nc.vector.tensor_tensor(gsc[:, :, :], gsc[:, :, :], sm("gn_w")[:, :, None].to_broadcast([P, CC, B]),
                                              ALU.mult))
                gb = gbi[:, :, :].rearrange("p a b -> p (a b)")
                chain(nc.vector.tensor_tensor(gb, gs, po[:, 0:8], ALU.mult))
                nc.vector.tensor_tensor(gbi[:, :, :], sm("gn_b")[:, :, None].to_broadcast([P, CC, B]), gbi[:, :, :],
                                        ALU.subtract).then_inc(gready, 1)

                def keep_rest(c, t):
                    n = 4 * c + t
                    dve.wait_ge(rounded, n + 1)
                    if t == 0 and c > 0:
                        dve.wait_ge(dup, 96 * c)
                    cols = slice((t % 2) * HALF, (t % 2 + 1) * HALF)
                    for hh in range(2):
                        mine = slice(hh * DH, (hh + 1) * DH)
                        at = _COLS["q_b" if t < 2 else "k_b"][0] + c % HP
                        hi = (qhl if t < 2 else khh)[mine, c % 2, hh, cols]
                        lo = qlo[mine, cols] if t < 2 else kll[mine, c % 2, hh, cols]
                        ins = nc.vector.scalar_tensor_tensor(out=lo, in0=made_in(c, t)[mine, :], scalar=small[mine, at:at + 1],
                                                             in1=hi.bitcast(fp32), op0=ALU.add, op1=ALU.subtract)
                    ins.then_inc(rest, 1)

                def half_copy(b, v):
                    u = b * UN2 + v
                    dve.wait_ge(tr, 2 * u + 2)
                    if u >= 4:
                        dve.wait_ge(pv, (u - 4) // 2 + 1)
                    nc.vector.tensor_copy(ptr[:, u // 2 % 2, u % 2, 4:8, :], pp_[:, 1, :].rearrange("p (a b) -> p a b", a=4)
                                          ).then_inc(trb, 1)

                for b in range(B):
                    for t in range(4):
                        keep_rest(b * HP, t)
                    for i in range(VT):
                        dve.wait_ge(pj, 2 * VT * b + i + 1)
                        nc.vector.tensor_tensor(va[:, i, :], banks[i % 4], sm("v_b"), ALU.add).then_inc(pj_used, 1)
                    for v in range(UN2):
                        u = b * UN2 + v
                        w = slice(u % 4, u % 4 + 1)
                        dve.wait_ge(qk_done, u + 1)
                        nc.vector.tensor_reduce(rmax[:, w], ps[:, u % 2, :], X, ALU.max, negate=True).then_inc(mx, 1)
                        dve.wait_ge(mx, u + 1)
                        if u >= 4:
                            dve.wait_ge(ex, u - 3)
                        nc.vector.tensor_scalar(rmx8[:, w], rmax[:, w], DH ** -0.5, None, ALU.mult).then_inc(mx8, 1)
                        if v >= 2:
                            half_copy(b, v - 2)
                        dve.wait_ge(ex, u + 1)
                        if u >= 4:
                            dve.wait_ge(nm, u - 3)
                        nc.vector.reciprocal(rinv[:, w], rsum[:, w]).then_inc(ri, 1)
                        if v % 16 - 1 in MAKE_AT and v // 16 < HP - 1:
                            keep_rest(b * HP + v // 16 + 1, MAKE_AT[v % 16 - 1])
                    half_copy(b, UN2 - 2)
                    half_copy(b, UN2 - 1)
                    for i in range(8):
                        oc, th = i // 2, i % 2
                        cols = slice(th * HALF, (th + 1) * HALF)
                        dve.wait_ge(pj, 2 * VT * b + VT + i + 1)
                        dve.wait_ge(xg_ready, CC * (b + 1))
                        nc.vector.scalar_tensor_tensor(out=xs[:, oc, b, cols], in0=banks[i % 4],
                                                       scalar=sm("proj_b", oc, oc + 1), in1=xg[:, oc, cols],
                                                       op0=ALU.add, op1=ALU.add).then_inc(pj_used, 1)
                        dve.wait_ge(pj_used, 2 * VT * b + VT + i + 1)
                        dve.sem_inc(fin, 1)

            @block.gpsimd
            def _(pool):
                for u in range(B * UN2):
                    pool.wait_ge(ri, u + 1)
                    nc.gpsimd.tensor_scalar(pr[:, u % 4, :], pr[:, u % 4, :], rinv[:, u % 4:u % 4 + 1],
                                            1.0, ALU.mult, ALU.mult).then_inc(nm, 1)


def kernel(**inputs):
    import concourse.bacc as bacc
    from concourse import mybir as _mybir
    from concourse.bass_utils import run_bass_kernel_spmd

    def arr(name):
        return np.asarray(inputs[name])

    L0, L1 = "L0_conv_", "L1_conv_"
    cols = lambda v, k: v.reshape(k, P).T
    small = np.zeros((P, SMALL), np.float32)

    def put(name, v):
        at, w = _COLS[name]
        small[:, at:at + w] = v

    for name, key, k in (("bn1_g", L0 + "bn1_g", CC), ("bn1_b", L0 + "bn1_b", CC), ("bn2_g", L0 + "bn2_g", CC),
                         ("bn2_b", L0 + "bn2_b", CC), ("out_b", L0 + "out_b", CC), ("mlp_b2", L0 + "mlp_b2", CC),
                         ("gn_w", L1 + "gn_w", CC), ("gn_b", L1 + "gn_b", CC), ("proj_b", L1 + "proj_b", CC),
                         ("mlp_b1", L0 + "mlp_b1", HC)):
        put(name, cols(arr(key), k))
    qkv_b = arr(L1 + "qkv_b").reshape(G, 3, DH)
    put("q_b", cols(qkv_b[:, 0].reshape(C), CC))
    put("k_b", cols(qkv_b[:, 1].reshape(C), CC))
    put("v_b", np.broadcast_to(qkv_b[:, 2].reshape(1, C), (P, C)))
    both = lambda v: np.concatenate([v, v], axis=0)
    put("dw_w", both(arr(L0 + "off_dw_w").reshape(DH, 36)))
    put("dw_b", both(arr(L0 + "off_dw_b").reshape(DH, 1)))
    put("cpb_b2", arr(L0 + "cpb_b2").reshape(P, 1))
    put("cpb_b3", np.broadcast_to(arr(L0 + "cpb_b3").reshape(1, 1), (P, 1)))
    w3 = np.zeros((P, 63), np.float32)
    w3[:, 31] = arr(L0 + "cpb_w3")[:, 0]
    put("w3_window", w3)
    put("cpb_w2", arr(L0 + "cpb_w2"))
    w1c = arr(L0 + "cpb_w1")
    axis = (np.arange(P) // 32) % 2
    put("w1_rows", w1c[axis])
    b1_rows = np.zeros((P, P), np.float32)
    b1_rows[axis == 1] = arr(L0 + "cpb_b1")
    put("b1_rows", b1_rows)
    pwo = arr(L0 + "off_pw_w")
    put("pw_feat", both(pwo[axis].T))
    put("pw_x", both(pwo[np.zeros(P, int)].T))
    put("pw_y", both(pwo[np.ones(P, int)].T))

    const = np.zeros((P, NCONST), np.float32)

    def putc(name, v):
        at, w = _CONST[name]
        const[:, at:at + w] = v

    p = np.arange(P)
    j = np.arange(J)
    putc("ident", np.eye(P, dtype=np.float32))
    putc("grid_x", np.broadcast_to(j % WD, (P, J)))
    putc("grid_y", np.broadcast_to(j // WD, (P, J)))
    putc("grid_feat", np.where(axis[:, None] == 0, j % WD, j // WD))
    putc("query_pos", (np.float32(2.0) * (p % 32).astype(np.float32) / np.float32(WW - 1) - np.float32(1.0))[:, None])
    putc("neg_ix", -(p % 32)[:, None])
    putc("neg_iy", -(4 * np.arange(8)[None, :] + (p // 32)[:, None]))
    putc("group_mean", (p[:, None] // GCH == p[None, :] // GCH) / GCH)
    i = np.arange(T)
    onehot = np.zeros((P, T), np.float32)
    for part in range(2):
        onehot[part * 64 + i % WW, i] = 1
        onehot[part * 64 + 32 + i // WW, i] = 1

    def diagonal(w):
        o = np.zeros((P, CC, P), np.float32)
        for g in range(G):
            a = (g % 2) * DH
            o[a:a + DH, g // 2, a:a + DH] = w[g].T
        return o

    rows = lambda w, k: w.reshape(k, P, -1).transpose(1, 0, 2)
    qkv_w = arr(L1 + "qkv_w").reshape(G, 3, DH, C)
    qk_w = np.concatenate([qkv_w[:, 0].reshape(C, C).T, qkv_w[:, 1].reshape(C, C).T], axis=1)
    data = [
        ("x", arr("x").reshape(B, CC, P, T).transpose(2, 1, 0, 3)),
        ("small", small), ("const", const), ("onehot", onehot),
        ("qw", diagonal(arr(L0 + "qw"))), ("kw", diagonal(arr(L0 + "kw"))), ("vw", diagonal(arr(L0 + "vw"))),
        ("ow", rows(arr(L0 + "out_w").T, CC)), ("w1", rows(arr(L0 + "mlp_w1").T, CC)),
        ("w2", rows(arr(L0 + "mlp_w2").T, HC)), ("qkw", rows(qk_w, CC)),
        ("vpw", rows(qkv_w[:, 2].reshape(C, C).T, CC)), ("pw", rows(arr(L1 + "proj_w").T, CC)),
    ]
    nc = bacc.Bacc("TRN2", target_bir_lowering=False, num_devices=1)
    arrays, args = {}, []
    for name, a in data:
        a = np.ascontiguousarray(a)
        arrays[f"in_{name}"] = a
        args.append(nc.dram_tensor(f"in_{name}", a.shape, _mybir.dt.from_np(a.dtype), kind="ExternalInput").ap())
    out = nc.dram_tensor("out", (P, CC, B, T), _mybir.dt.float32, kind="ExternalOutput").ap()
    deformable_then_attention(nc, *args, out)
    r = run_bass_kernel_spmd(nc, [arrays], core_ids=[0])
    got = r.results[0]["out"]
    return np.ascontiguousarray(got.transpose(2, 1, 0, 3)).reshape(B, C, HH, WW)
```

```python
import math
from contextlib import ExitStack

import numpy as np

import concourse.bass as bass
from concourse import mybir

B, C, HH, WW = 2, 512, 32, 32
T = HH * WW
P = 128
CC = C // P
G, DH = 8, 64
NCH = B * CC
HD = WD = 8
J = HD * WD
HALF = T // 2
HID = 4 * C
HC = HID // P
EPS = 1e-5
STEPS = J // 2
NG = 32
GCH = C // NG

_COLS = {}


def _col(name, width):
    at = sum(w for _, w in _COLS.values())
    _COLS[name] = (at, width)


for _n, _w in (("bn1_g", CC), ("bn1_b", CC), ("bn2_g", CC), ("bn2_b", CC), ("out_b", CC), ("mlp_b2", CC),
               ("gn_w", CC), ("gn_b", CC), ("proj_b", CC), ("mlp_b1", HC), ("q_b", CC), ("k_b", CC),
               ("dw_w", 36), ("dw_b", 1), ("cpb_b2", 1), ("cpb_b3", 1),
               ("w3_window", 63), ("cpb_w2", P), ("w1_rows", P), ("b1_rows", P),
               ("pw_feat", P), ("pw_x", P), ("pw_y", P), ("v_b", C)):
    _col(_n, _w)
SMALL = sum(w for _, w in _COLS.values())

_CONST = {}
for _n, _w in (("ident", P), ("grid_feat", J), ("grid_x", J), ("grid_y", J), ("query_pos", 1), ("neg_ix", 1),
               ("neg_iy", 8), ("group_mean", P)):
    _CONST[_n] = (sum(w for _, w in _CONST.values()), _w)
NCONST = sum(w for _, w in _CONST.values())


def deformable_then_attention(nc, x_d, small_d, const_d, onehot_d, qw_d, kw_d, vw_d, ow_d, w1_d, w2_d, qkw_d, vpw_d,
                              pw_d, out_d):
    fp32 = mybir.dt.float32
    f32r = mybir.dt.float32r
    ACT = mybir.ActivationFunctionType
    ALU = mybir.AluOpType
    AX = mybir.AxisListType
    X = AX.X
    outer = ExitStack()
    with outer:
        def sb(ctx, name, shape, dt=fp32):
            return ctx.enter_context(nc.sbuf_tensor(name, shape, dt))

        def pb(ctx, name, shape):
            return ctx.enter_context(nc.psum_tensor(name, shape, fp32))

        def sem(ctx, name):
            return ctx.enter_context(nc.semaphore(name))

        xs = sb(outer, "xs", [P, CC, B, T])
        ao = sb(outer, "ao", [P, NCH, T])
        small = sb(outer, "small", [P, SMALL])
        const = sb(outer, "const", [P, NCONST])

        def sm(name, a=0, b=None):
            at, w = _COLS[name]
            return small[:, at + a:at + (w if b is None else b)]

        def co(name, a=0, b=None):
            at, w = _CONST[name]
            return const[:, at + a:at + (w if b is None else b)]

        ident = co("ident")
        ow = sb(outer, "ow", [P, CC, C])
        ow_in = sem(outer, "ow_in")
        stats = sb(outer, "stats", [P, B, 2, CC, 6])
        pool_held, dve_held, act_held, pe_held = (sem(outer, x) for x in ("pool_held", "dve_held", "act_held", "pe_held"))

        with ExitStack() as l0:
            q = sb(l0, "q", [P, NCH, T])
            kall = sb(l0, "kall", [P, NCH, J])
            vall = sb(l0, "vall", [P, NCH, P])
            feat = sb(l0, "feat", [P, 2, NCH, J])

            with ExitStack() as a:
                xn = sb(a, "xn", [P, CC, B, T])
                xnt = sb(a, "xnt", [P, B, 8, C])
                qw = sb(a, "qw", [P, CC, P])
                kw = sb(a, "kw", [P, CC, P])
                vw = sb(a, "vw", [P, CC, P])
                bn_s = sb(a, "bn_s", [P, CC])
                dw = sb(a, "dw", [P, NCH, HD, WD])
                kv = sb(a, "kv", [P, NCH, 2, J])
                pq = pb(a, "pq", [P, 4, HALF])
                pt = pb(a, "pt", [P, 4, C])
                wt = ao[:, :, :]
                pe_taps = [(2, 2)] + [(ky, kx) for ky in (0, 5) for kx in range(6)]
                dve_taps = [(ky, kx) for ky in (2, 1, 3, 4) for kx in (1, 2, 3, 4, 0, 5) if (ky, kx) != (2, 2)]
                diag = ao[:, :, :].rearrange("p n t -> p (n t)")[:, 0:len(pe_taps) * P].rearrange("p (k c) -> p k c", c=P)

                def reach(k, n_out):
                    first, last = (1 if k == 0 else 0), (n_out - 1 if k == 5 else n_out)
                    return first, last, 4 * first - 1 + k

                flat = xn[:, :, :, :].rearrange("p a b c -> p (a b c)")
                th_f, th_x, th_y, hx, log_f, m0, m1, m2 = (flat[:, i * 1024:(i + 1) * 1024] for i in range(8))
                ring_y = [x[:, i * HALF:(i + 1) * HALF] for x in (th_x, m0) for i in range(2)]
                ring_v = [m1[:, i * HALF:(i + 1) * HALF] for i in range(2)]
                ring_p = [m2[:, i * HALF:(i + 1) * HALF] for i in range(2)]

                def image(v, b):
                    w = v.shape[-1] // 2
                    v = v.rearrange("p (a m) -> p a m", a=2)
                    return v if w == HALF // 2 else v[:, :, b * (w // 2):(b + 1) * (w // 2)]

                x_in = [sem(a, f"x_in{cc}") for cc in range(CC)]
                q_weights_in = sem(a, "q_weights_in")
                small_in = sem(a, "small_in")
                const_in = sem(a, "const_in")
                kv_weights_in = sem(a, "kv_weights_in")
                weights_odd = sem(a, "weights_odd")
                points_copied_again = sem(a, "points_copied_again")
                steps_done = sem(a, "steps_done")
                xn_ready = sem(a, "xn_ready")
                q_done = sem(a, "q_done")
                q_copied = sem(a, "q_copied")
                tile_turned = sem(a, "tile_turned")
                tile_copied = sem(a, "tile_copied")
                taps_added = sem(a, "taps_added")
                diag_ready = sem(a, "diag_ready")
                pe_taps_done = sem(a, "pe_taps_done")
                gelu_done = sem(a, "gelu_done")
                offset_done = sem(a, "offset_done")
                tanh_done = sem(a, "tanh_done")
                grid_done = sem(a, "grid_done")
                feat_steps = sem(a, "feat_steps")
                distance_done = sem(a, "distance_done")
                hat_done = sem(a, "hat_done")
                weights_even = sem(a, "weights_even")
                points_sampled = sem(a, "points_sampled")
                points_copied = sem(a, "points_copied")
                kv_done = sem(a, "kv_done")
                kv_kept = sem(a, "kv_kept")
                block = a.enter_context(nc.Block())

                @block.sync
                def _(sp):
                    sp.dma_start(small[:, :], small_d).then_inc(small_in, 16)
                    for cc in range(CC):
                        sp.dma_start(xs[:, cc, :, :], x_d[:, cc, :, :]).then_inc(x_in[cc], 16)
                        if cc == 0:
                            sp.dma_start(qw[:, :, :], qw_d).then_inc(q_weights_in, 16)
                            sp.dma_start(const[:, :], const_d).then_inc(const_in, 16)
                    sp.dma_start(kw[:, :, :], kw_d).then_inc(kv_weights_in, 16)
                    sp.dma_start(vw[:, :, :], vw_d).then_inc(kv_weights_in, 16)
                    sp.dma_start(ow[:, :, :], ow_d).then_inc(ow_in, 16)

                @block.tensor
                def _(pe):
                    pe.wait_ge(q_weights_in, 16)
                    for i in range(NCH * 2):
                        n, h = i // 2, i % 2
                        b, cc = n % B, n // B
                        pe.wait_ge(xn_ready, cc + 1)
                        if i >= 4:
                            pe.wait_ge(q_copied, i - 3)
                        nc.tensor.matmul(pq[:, i % 4, :], qw[:, cc, :], xn[:, cc, b, h * HALF:(h + 1) * HALF],
                                         start=True, stop=True).then_inc(q_done, 1)
                    pe.wait_ge(diag_ready, len(pe_taps))
                    pe.wait_ge(q_copied, 2 * NCH)
                    qv = q[:, :, :].rearrange("p n (y x) -> p n y x", y=HH)
                    cv = pq[:, 0, :].rearrange("p (n y x) -> p n y x", y=HD, x=WD)
                    for i, (ky, kx) in enumerate(pe_taps):
                        (y0, y1, ys), (x0, x1, x_) = reach(ky, HD), reach(kx, WD)
                        mm = nc.tensor.matmul(cv[:, :, y0:y1, x0:x1], diag[:, i, :],
                                              qv[:, :, ys:ys + 4 * (y1 - y0 - 1) + 1:4, x_:x_ + 4 * (x1 - x0 - 1) + 1:4],
                                              start=(i == 0), stop=(i == len(pe_taps) - 1), skip_group_check=True)
                    mm.then_inc(pe_taps_done, 1)
                    pe.wait_ge(const_in, 16)
                    for i in range(B * 8):
                        b, t = i // 8, i % 8
                        if i >= 4:
                            pe.wait_ge(tile_copied, i - 3)
                        for cc in range(CC):
                            mm = nc.tensor.transpose(pt[:, i % 4, cc * P:(cc + 1) * P],
                                                     xn[:, cc, b, t * P:(t + 1) * P], ident)
                        mm.then_inc(tile_turned, 1)
                    pe.wait_ge(gelu_done, 1)
                    pe.wait_ge(q_copied, 2 * NCH)
                    dwf = dw[:, :, :, :].rearrange("p a b c -> p (a b c)")
                    pe.wait_ge(tile_copied, B * 8)
                    for v, name in enumerate(("pw_feat", "pw_x", "pw_y")):
                        for par in range(2):
                            r = slice(par * DH, (par + 1) * DH)
                            o = pq[:, 2 * v + par, :] if v < 2 else pt[:, par, :]
                            at = _COLS[name][0]
                            nc.tensor.matmul(o, small[r, at:at + P], dwf[r, :], start=True, stop=True).then_inc(offset_done, 1)
                    wtf = wt.rearrange("p t (a n j) -> p t a n j", a=2, n=NCH)
                    for b in range(B):
                        pe.wait_ge(weights_even, 4 * (b + 1))
                        pe.wait_ge(weights_odd, 4 * (b + 1))
                        for cc in range(CC):
                            for t in range(8):
                                for par in range(2):
                                    mm = nc.tensor.matmul(pt[par * DH:(par + 1) * DH, 2 + b, cc * J:(cc + 1) * J],
                                                          xnt[:, b, t, cc * P + par * DH:cc * P + (par + 1) * DH],
                                                          wtf[:, t, par, b * CC + cc, :], start=(t == 0), stop=(t == 7),
                                                          skip_group_check=True)
                        mm.then_inc(points_sampled, 1)
                    pe.wait_ge(kv_weights_in, 32)
                    pe.wait_ge(tanh_done, 6)
                    for b in range(B):
                        pe.wait_ge(points_copied, b + 1)
                        for cc in range(CC):
                            mm = nc.tensor.matmul(pq[:, 2 + b, cc * J:(cc + 1) * J], kw[:, cc, :], kv[:, b * CC + cc, 0, :],
                                                  start=True, stop=True)
                        mm.then_inc(kv_done, 1)
                        pe.wait_ge(points_copied_again, b + 1)
                        for cc in range(CC):
                            mm = nc.tensor.matmul(pq[:, b, cc * P:(cc + 1) * P],
                                                  kv[:, b * CC + cc, :, :].rearrange("p a j -> p (a j)"), vw[:, cc, :],
                                                  start=True, stop=True)
                        mm.then_inc(kv_done, 1)

                @block.scalar
                def _(act):
                    for i in range(NCH * 2):
                        n, h = i // 2, i % 2
                        b, cc = n % B, n // B
                        act.wait_ge(q_done, i + 1)
                        nc.scalar.activation(q[:, b * CC + cc, h * HALF:(h + 1) * HALF], pq[:, i % 4, :],
                                             ACT.Copy).then_inc(q_copied, 1)
                    for i in range(B * 8):
                        act.wait_ge(tile_turned, i + 1)
                        nc.scalar.activation(xnt[:, i // 8, i % 8, :], pt[:, i % 4, :], ACT.Copy).then_inc(tile_copied, 1)
                    dwf = dw[:, :, :, :].rearrange("p a b c -> p (a b c)")
                    act.wait_ge(taps_added, len(dve_taps) + 1)
                    nc.scalar.activation(dwf, dwf, ACT.Gelu, bias=sm("dw_b")).then_inc(gelu_done, 1)
                    for v, dst in enumerate((th_f, th_x, th_y)):
                        for par in range(2):
                            act.wait_ge(offset_done, 2 * v + par + 1)
                            o = pq[:, 2 * v + par, :] if v < 2 else pt[:, par, :]
                            nc.scalar.activation(dst[:, par * 512:(par + 1) * 512], o, ACT.Tanh).then_inc(tanh_done, 1)
                    act.wait_ge(grid_done, 2)
                    nc.scalar.activation(hx, th_x, ACT.Abs, bias=co("neg_ix")).then_inc(distance_done, 1)
                    act.wait_ge(grid_done, 3)
                    act.wait_ge(distance_done, 1)
                    for k in range(8 * B):
                        b, t = k // 8, k % 8
                        if k >= 4:
                            act.wait_ge(hat_done, k - 2)
                        nc.scalar.activation(image(ring_y[k % 4], 0), image(th_y, b), ACT.Abs, bias=co("neg_iy", t, t + 1)
                                             ).then_inc(distance_done, 1)
                    for b in range(B):
                        act.wait_ge(points_sampled, b + 1)
                        nc.scalar.activation(kv[:, b * CC:(b + 1) * CC, 0, :],
                                             pt[:, 2 + b, 0:CC * J].rearrange("p (n j) -> p n j", n=CC),
                                             ACT.Copy).then_inc(points_copied, 1)
                        if b == 0:
                            nc.scalar.activation(log_f, th_f, ACT.Abs).then_inc(feat_steps, 1)
                            act.wait_ge(feat_steps, 1)
                            nc.scalar.activation(log_f, log_f, ACT.Ln, bias=1.0).then_inc(feat_steps, 1)
                            nc.scalar.activation(th_f, th_f, ACT.Sign).then_inc(feat_steps, 1)
                    for b in range(B):
                        act.wait_ge(kv_done, 2 * b + 2)
                        nc.scalar.activation(vall[:, b * CC:(b + 1) * CC, :].rearrange("p a b -> p (a b)"), pq[:, b, :],
                                             ACT.Copy).then_inc(kv_kept, 1)

                @block.vector
                def _(dve):
                    dve.wait_ge(small_in, 16)
                    nc.vector.tensor_scalar(bn_s[:, :], sm("bn1_g"), 1.0 / math.sqrt(1.0 + EPS), None,
                                            ALU.mult).then_inc(steps_done, 1)
                    dve.wait_ge(steps_done, 1)
                    for cc in range(CC):
                        dve.wait_ge(x_in[cc], 16)
                        nc.vector.tensor_scalar(xn[:, cc, :, :], xs[:, cc, :, :], bn_s[:, cc:cc + 1],
                                                sm("bn1_b", cc, cc + 1), ALU.mult, ALU.add).then_inc(xn_ready, 1)
                    dve.wait_ge(q_copied, 2 * NCH)
                    qr = q[:, :, :].rearrange("p n (y r x) -> p (n y) r x", r=HH // HD, x=WW)
                    dwr = dw[:, :, :, :].rearrange("p n y x -> p (n y) x")
                    for i, (ky, kx) in enumerate(dve_taps):
                        x0, x1, x_ = reach(kx, WD)
                        src = qr[:, :, ky - 1, x_:x_ + 4 * (x1 - x0 - 1) + 1:4]
                        w = sm("dw_w", ky * 6 + kx, ky * 6 + kx + 1)
                        if i == 0:
                            nc.vector.tensor_scalar(dwr[:, :, x0:x1], src, w, None, ALU.mult).then_inc(taps_added, 1)
                        else:
                            dve.wait_ge(taps_added, i)
                            nc.vector.scalar_tensor_tensor(out=dwr[:, :, x0:x1], in0=src, scalar=w, in1=dwr[:, :, x0:x1],
                                                           op0=ALU.mult, op1=ALU.add).then_inc(taps_added, 1)
                    dve.wait_ge(taps_added, len(dve_taps))
                    dve.wait_ge(pe_taps_done, 1)
                    dwf = dw[:, :, :, :].rearrange("p a b c -> p (a b c)")
                    nc.vector.tensor_tensor(dwf, pq[:, 0, :], dwf, ALU.add).then_inc(taps_added, 1)
                    own = 0

                    def grid_of(dst, grid, waited):
                        nonlocal own
                        dve.wait_ge(tanh_done, waited)
                        g = grid[:, None, :].to_broadcast([P, 2 * NCH, J])
                        d3 = dst.rearrange("p (n j) -> p n j", j=J)
                        nc.vector.tensor_scalar(dst, dst, 4.0, None, ALU.mult).then_inc(steps_done, 1)
                        own += 1
                        dve.wait_ge(steps_done, 1 + own)
                        nc.vector.tensor_tensor(d3, d3, g, ALU.add).then_inc(steps_done, 1)
                        own += 1
                        dve.wait_ge(steps_done, 1 + own)
                        nc.vector.tensor_scalar(dst, dst, 2.0 / (HD - 1), -1.0, ALU.mult, ALU.add).then_inc(steps_done, 1)
                        own += 1
                        dve.wait_ge(steps_done, 1 + own)

                    grid_of(th_f, co("grid_feat"), 2)
                    nc.vector.tensor_scalar(th_f, th_f, -1.0, co("query_pos"), ALU.mult, ALU.add).then_inc(grid_done, 1)
                    for dst, name, k in ((th_x, "grid_x", 4), (th_y, "grid_y", 6)):
                        grid_of(dst, co(name), k)
                        nc.vector.tensor_scalar(dst, dst, 1.0, WW / 2.0, ALU.add, ALU.mult).then_inc(steps_done, 1)
                        own += 1
                        dve.wait_ge(steps_done, 1 + own)
                        nc.vector.tensor_scalar(dst, dst, -0.5, None, ALU.add).then_inc(grid_done, 1)
                    dve.wait_ge(distance_done, 1)
                    nc.vector.tensor_scalar(hx, hx, -1.0, 0.0, ALU.add, ALU.min).then_inc(hat_done, 1)
                    for i in range(4 * B):
                        for k, ring in ((2 * i, ring_v), (2 * i + 1, ring_p)):
                            dve.wait_ge(distance_done, k + 2)
                            if i >= 2:
                                dve.wait_ge(weights_even if k % 2 == 0 else weights_odd, i - 1)
                            nc.vector.tensor_scalar(ring[i % 2], ring_y[k % 4], -1.0, 0.0, ALU.add, ALU.min
                                                    ).then_inc(hat_done, 1)
                        dve.wait_ge(hat_done, 2 * i + 2)
                        b, t = i // 4, 2 * (i % 4)
                        nc.vector.tensor_tensor(image(wt[:, t, :], b), image(ring_v[i % 2], 0), image(hx, b), ALU.mult
                                                ).then_inc(weights_even, 1)
                    for b in range(B):
                        dve.wait_ge(points_copied, b + 1)
                        nc.vector.tensor_copy(kv[:, b * CC:(b + 1) * CC, 1, :],
                                              pt[:, 2 + b, 0:CC * J].rearrange("p (n j) -> p n j", n=CC)
                                              ).then_inc(points_copied_again, 1)
                    dve.wait_ge(feat_steps, 3)
                    nc.vector.tensor_tensor(feat[:, :, :, :].rearrange("p a n j -> p (a n j)"), log_f, th_f,
                                            ALU.mult).then_inc(grid_done, 1)
                    for b in range(B):
                        dve.wait_ge(kv_done, 2 * b + 1)
                        nc.vector.tensor_scalar(kall[:, b * CC:(b + 1) * CC, :].rearrange("p n j -> p (n j)"),
                                                pq[:, 2 + b, 0:CC * J], DH ** -0.5, None, ALU.mult).then_inc(kv_kept, 1)

                @block.gpsimd
                def _(pool):
                    pool.wait_ge(small_in, 16)
                    pool.wait_ge(const_in, 16)
                    for i, (ky, kx) in enumerate(pe_taps):
                        nc.gpsimd.tensor_scalar(diag[:, i, :], ident, sm("dw_w", ky * 6 + kx, ky * 6 + kx + 1), 1.0,
                                                ALU.mult, ALU.mult).then_inc(diag_ready, 1)
                    for i in range(4 * B):
                        b, t = i // 4, 2 * (i % 4) + 1
                        pool.wait_ge(hat_done, 2 * i + 3)
                        nc.gpsimd.tensor_tensor(image(wt[:, t, :], b), image(ring_p[i % 2], 0), image(hx, b), ALU.mult
                                                ).then_inc(weights_odd, 1)

            with ExitStack() as bctx:
                onehot = sb(bctx, "onehot", [P, T], f32r)
                w2h = sb(bctx, "w2h", [P, P], f32r)
                w2l = sb(bctx, "w2l", [P, P], f32r)
                tsl = sb(bctx, "tsl", [P, 2, 2, P], f32r)
                v1 = sb(bctx, "v1", [P, 2, P])
                v2 = sb(bctx, "v2", [P, 2, P])
                vh = sb(bctx, "vh", [P, 2, P], f32r)
                h1h = sb(bctx, "h1h", [P, 4, T], f32r)
                h1l = sb(bctx, "h1l", [P, 4, T], f32r)
                h2 = sb(bctx, "h2", [P, 2, 2, 2, HALF])
                wz = sb(bctx, "wz", [P, 2, 32])
                qs = sb(bctx, "qs", [P, T])
                ks = sb(bctx, "ks", [P, J])
                vs = sb(bctx, "vs", [P, DH])
                sims = sb(bctx, "sims", [P, HALF])
                negm = sb(bctx, "negm", [P, 8])
                psum_ = sb(bctx, "prob_sum", [P, 8])
                prob = sb(bctx, "prob", [P, 8, J])
                probn = sb(bctx, "probn", [P, 8, J])
                pts = sb(bctx, "pts", [P, HALF])
                p1 = pb(bctx, "p1", [P, 2, T])
                p2 = pb(bctx, "p2", [P, 2, HALF])
                sim = pb(bctx, "sim", [P, HALF])
                misc = pb(bctx, "misc", [P, 8, J])
                miscf = misc[:, :, :].rearrange("p a j -> p (a j)")

                const_ready = sem(bctx, "const_ready")
                w2_ready = sem(bctx, "w2_ready")
                rows_own = sem(bctx, "rows_own")
                rows_ready = sem(bctx, "rows_ready")
                l1_done = sem(bctx, "l1_done")
                hi_done = sem(bctx, "hi_done")
                lo_done = sem(bctx, "lo_done")
                l2_done = sem(bctx, "l2_done")
                relu_a = sem(bctx, "relu_a")
                relu_b = sem(bctx, "relu_b")
                wz_ready = sem(bctx, "wz_ready")
                l3_done = sem(bctx, "l3_done")
                kq_ready = sem(bctx, "kq_ready")
                seed_done = sem(bctx, "seed_done")
                sim_copied = sem(bctx, "sim_copied")
                turned = sem(bctx, "turned")
                max_done = sem(bctx, "max_done")
                shifted = sem(bctx, "shifted")
                exp_done = sem(bctx, "exp_done")
                sum_done = sem(bctx, "sum_done")
                normed = sem(bctx, "normed")
                turned_back = sem(bctx, "turned_back")
                pt_copied = sem(bctx, "pt_copied")
                vs_ready = sem(bctx, "vs_ready")
                pv_done = sem(bctx, "pv_done")
                ao_done = sem(bctx, "ao_done")
                block = bctx.enter_context(nc.Block())

                LAST_M = STEPS - 1

                def walk(eng, step):
                    def chunk(n, first, last):
                        for par in range(2):
                            prev = not (first and par == 0)
                            for m in range(4):
                                step(n, par, m, prev, 2)
                            with eng.Fori(4, STEPS - 2, 2) as mm:
                                step(n, par, mm, prev, 2, parity=0)
                                step(n, par, mm + 1, prev, 2, parity=1)
                            end = last and par == 1
                            step(n, par, LAST_M - 1, prev, 1 if end else 2)
                            step(n, par, LAST_M, prev, 0 if end else 2)

                    chunk(0, True, False)
                    with eng.Fori(1, NCH - 1) as n:
                        chunk(n, False, False)
                    chunk(NCH - 1, False, True)

                @block.tensor
                def _(pe):
                    def rows(par_slot, jb):
                        for ih in range(2):
                            mm = nc.tensor.matmul(p1[:, jb, ih * HALF:(ih + 1) * HALF], tsl[:, par_slot, jb, :],
                                                  onehot[:, ih * HALF:(ih + 1) * HALF], start=True, stop=True)
                        mm.then_inc(l1_done, 1)

                    def third(slot, pair_last):
                        for ih in range(2):
                            for jb in range(2):
                                at = ih * J + jb * 32
                                mm = nc.tensor.matmul(sim[at:at + 32, :], wz[:, slot, :], h2[:, slot, jb, ih, :],
                                                      start=False, stop=pair_last, skip_group_check=True)
                        mm.then_inc(l3_done, 1)

                    def seed(n, par, r):
                        pe.wait_ge(kq_ready, 2 * n + 2)
                        pe.sem_inc(pe_held, 1)
                        rr = slice(par * DH, (par + 1) * DH)
                        for ih in range(2):
                            mm = nc.tensor.matmul(sim[ih * J:(ih + 1) * J, :], ks[rr, :],
                                                  qs[rr, ih * HALF:(ih + 1) * HALF], start=True, stop=False,
                                                  skip_group_check=True)
                        mm.then_inc(seed_done, 1)

                    def turn(r):
                        if not (isinstance(r, int) and r < 2):
                            pe.wait_ge(ao_done, 2 * r - 2)
                        for i in range(4):
                            mm = nc.tensor.transpose(miscf[:, i * P:(i + 1) * P], sims[:, i * P:(i + 1) * P], ident)
                        mm.then_inc(turned, 1)

                    def turn_back(r):
                        pe.wait_ge(normed, r)
                        pn = probn[:, :, :].rearrange("p a j -> p (a j)")
                        for i in range(4):
                            mm = nc.tensor.transpose(miscf[:, i * P:(i + 1) * P], pn[:, i * P:(i + 1) * P], ident)
                        mm.then_inc(turned_back, 1)

                    def values(r, pp, ih):
                        if ih == 0:
                            pe.wait_ge(pt_copied, r)
                            pe.wait_ge(vs_ready, r)
                        else:
                            pe.wait_ge(ao_done, 2 * r - 1)
                        pe.sem_inc(pe_held, 1)
                        nc.tensor.matmul(miscf[pp * DH:(pp + 1) * DH, :], vs[ih * J:(ih + 1) * J, :],
                                         pts[ih * J:(ih + 1) * J, :], start=True, stop=True).then_inc(pv_done, 1)

                    def step(n, par, m, prev, behind, parity=None):
                        sp_ = m % 2 if parity is None else parity
                        r = 2 * n + par
                        s = r * STEPS + m
                        k0 = 2 * s
                        for jb in range(2):
                            k = k0 + jb
                            pe.wait_ge(lo_done, k + 1)
                            if jb == 1:
                                if behind > 0:
                                    pe.wait_ge(rows_ready, s + 2)
                                    rows(1 - sp_, 1)
                                if behind > 1:
                                    pe.wait_ge(lo_done, k + 2)
                                    pe.wait_ge(rows_ready, s + 3)
                                    rows(sp_, 0)
                            u = 2 * sp_ + jb
                            for ih in range(2):
                                if not (isinstance(k, int) and k == 0):
                                    pe.wait_ge(relu_a if ih == 0 else relu_b, k)
                                cols = slice(ih * HALF, (ih + 1) * HALF)
                                nc.tensor.matmul(p2[:, ih, :], w2h[:, :], h1h[:, u, cols], start=True, stop=False)
                                nc.tensor.matmul(p2[:, ih, :], w2h[:, :], h1l[:, u, cols], start=False, stop=False)
                                nc.tensor.matmul(p2[:, ih, :], w2l[:, :], h1h[:, u, cols], start=False,
                                                 stop=True).then_inc(l2_done, 1)
                        static = isinstance(m, int)
                        if static and m == 1:
                            if prev:
                                pe.wait_ge(sim_copied, r)
                            seed(n, par, r)
                        if not (static and m == 0 and not prev):
                            third(1 - sp_, static and m == 0)
                        if static and prev:
                            if m == 1:
                                turn(r)
                            if m == 3:
                                turn_back(r)
                            if m == LAST_M - 1:
                                values(r, 1 - par, 0)
                            if m == LAST_M:
                                values(r, 1 - par, 1)

                    pe.wait_ge(const_ready, 16)
                    pe.wait_ge(w2_ready, 3)
                    pe.wait_ge(rows_ready, 1)
                    for jb in range(2):
                        rows(0, jb)
                    pe.wait_ge(rows_ready, 2)
                    pe.wait_ge(lo_done, 1)
                    rows(1, 0)
                    walk(pe, step)
                    s, r = 2 * NCH * STEPS, 2 * NCH
                    pe.wait_ge(relu_a, 2 * s)
                    pe.wait_ge(relu_b, 2 * s)
                    pe.wait_ge(wz_ready, s)
                    third(1, True)
                    pe.wait_ge(sim_copied, r)
                    turn(r)
                    turn_back(r)
                    values(r, 1, 0)
                    values(r, 1, 1)

                @block.scalar
                def _(act):
                    def hi(u, jb):
                        nc.scalar.activation(h1h[:, u, :], p1[:, jb, :], ACT.Relu).then_inc(hi_done, 1)

                    def copy_sim(r, s):
                        act.wait_ge(l3_done, s)
                        if not (isinstance(r, int) and r < 2):
                            act.wait_ge(turned, r - 1)
                        nc.scalar.activation(sims[:, :], sim[:, :], ACT.Identity, bias=sm("cpb_b3")
                                             ).then_inc(sim_copied, 1)

                    def exp(r):
                        act.wait_ge(shifted, r)
                        nc.scalar.activation(prob[:, :, :], prob[:, :, :], ACT.Exp).then_inc(exp_done, 1)

                    def copy_pt(r):
                        act.wait_ge(turned_back, r)
                        if not (isinstance(r, int) and r < 2):
                            act.wait_ge(pv_done, 2 * r - 2)
                        nc.scalar.activation(pts[:, :], miscf, ACT.Copy).then_inc(pt_copied, 1)

                    def copy_out(r, n, pp, ih):
                        act.wait_ge(pv_done, 2 * r - 1 + ih)
                        rr = slice(pp * DH, (pp + 1) * DH)
                        o = (ao[rr, n, ih * HALF:(ih + 1) * HALF] if isinstance(n, int) else
                             ao[rr, bass.ds(n, 1), ih * HALF:(ih + 1) * HALF].rearrange("p a t -> p (a t)"))
                        nc.scalar.activation(o, miscf[rr, :], ACT.Copy).then_inc(ao_done, 1)

                    def step(n, par, m, prev, behind, parity=None):
                        sp_ = m % 2 if parity is None else parity
                        r = 2 * n + par
                        s = r * STEPS + m
                        static = isinstance(m, int)
                        if static and prev and m == LAST_M - 1:
                            copy_pt(r)
                        pn = n if par == 1 else n - 1
                        if static and prev and m == LAST_M:
                            copy_out(r, pn, 1 - par, 0)
                        for jb in range(2):
                            k = 2 * s + jb
                            act.wait_ge(l2_done, 2 * k + 1)
                            if jb == 0 and not (isinstance(s, int) and s < 2):
                                act.wait_ge(l3_done, s - 1)
                            nc.scalar.activation(h2[:, sp_, jb, 0, :], p2[:, 0, :], ACT.Relu,
                                                 bias=sm("cpb_b2")).then_inc(relu_a, 1)
                            if behind > jb:
                                act.wait_ge(l1_done, k + 4)
                                hi((2 * sp_ + jb + 3) % 4, 1 - jb)
                        if static and prev:
                            if m == 0:
                                copy_sim(r, s)
                            if m == 2:
                                exp(r)
                            if m == LAST_M:
                                copy_out(r, pn, 1 - par, 1)

                    nc.scalar.activation(w2h[:, :], sm("cpb_w2"), ACT.Identity).then_inc(w2_ready, 1)
                    for k in range(3):
                        act.wait_ge(l1_done, k + 1)
                        hi(k, k % 2)
                    walk(act, step)
                    r = 2 * NCH
                    copy_sim(r, r * STEPS)
                    exp(r)
                    copy_pt(r)
                    copy_out(r, NCH - 1, 1, 0)
                    copy_out(r, NCH - 1, 1, 1)

                @block.vector
                def _(dve):
                    def lo(u, jb):
                        nc.vector.scalar_tensor_tensor(out=h1l[:, u, :], in0=p1[:, jb, :], scalar=0.0,
                                                       in1=h1h[:, u, :].bitcast(fp32), op0=ALU.max,
                                                       op1=ALU.subtract).then_inc(lo_done, 1)

                    def window(m, slot):
                        at = _COLS["w3_window"][0] + 31
                        src = (small[:, at - m:at - m + 32] if isinstance(m, int) else
                               small[:, bass.ds(at - m, 32)])
                        nc.vector.tensor_copy(wz[:, slot, :], src).then_inc(wz_ready, 1)

                    def shift(r):
                        dve.wait_ge(turned, r)
                        if not (isinstance(r, int) and r < 2):
                            dve.wait_ge(normed, r - 1)
                        nc.vector.tensor_reduce(negm[:, :], misc[:, :, :], X, ALU.max, negate=True
                                                ).then_inc(max_done, 1)
                        dve.wait_ge(max_done, r)
                        nc.vector.tensor_tensor(prob[:, :, :], misc[:, :, :],
                                                negm[:, :, None].to_broadcast([P, 8, J]), ALU.add
                                                ).then_inc(shifted, 1)

                    def norm(r):
                        dve.wait_ge(exp_done, r)
                        nc.vector.tensor_reduce(psum_[:, :], prob[:, :, :], X, ALU.add).then_inc(sum_done, 1)
                        dve.wait_ge(sum_done, 2 * r - 1)
                        nc.vector.reciprocal(psum_[:, :], psum_[:, :]).then_inc(sum_done, 1)
                        dve.wait_ge(sum_done, 2 * r)
                        if not (isinstance(r, int) and r < 2):
                            dve.wait_ge(turned_back, r - 1)
                        nc.vector.tensor_tensor(probn[:, :, :], prob[:, :, :],
                                                psum_[:, :, None].to_broadcast([P, 8, J]), ALU.mult
                                                ).then_inc(normed, 1)

                    def step(n, par, m, prev, behind, parity=None):
                        sp_ = m % 2 if parity is None else parity
                        r = 2 * n + par
                        s = r * STEPS + m
                        static = isinstance(m, int)
                        if static and prev:
                            if m == 2:
                                shift(r)
                            if m == 3:
                                norm(r)
                        for jb in range(2):
                            k = 2 * s + jb
                            dve.wait_ge(l2_done, 2 * k + 2)
                            if jb == 0 and not (isinstance(s, int) and s < 2):
                                dve.wait_ge(l3_done, s - 1)
                            nc.vector.tensor_scalar(h2[:, sp_, jb, 1, :], p2[:, 1, :], sm("cpb_b2"), 0.0, ALU.add,
                                                    ALU.max).then_inc(relu_b, 1)
                            if behind > jb:
                                dve.wait_ge(hi_done, k + 4)
                                lo((2 * sp_ + jb + 3) % 4, 1 - jb)
                            if jb == 1:
                                window(m, sp_)

                    dve.wait_ge(w2_ready, 1)
                    nc.vector.tensor_tensor(w2l[:, :], sm("cpb_w2"), w2h[:, :].bitcast(fp32), ALU.subtract
                                            ).then_inc(w2_ready, 2)
                    for k in range(3):
                        dve.wait_ge(hi_done, k + 1)
                        lo(k, k % 2)
                    walk(dve, step)
                    shift(2 * NCH)
                    norm(2 * NCH)

                @block.gpsimd
                def _(pool):
                    pool.dma_start(onehot[:, :], onehot_d).then_inc(const_ready, 16)
                    nc.gpsimd.memset(vh[0:64, :, :].bitcast(fp32), 0.0).then_inc(rows_own, 1)
                    w1r = sm("w1_rows")[:, None, :].to_broadcast([P, 2, P])
                    b1r = sm("b1_rows")[:, None, :].to_broadcast([P, 2, P])
                    featf = feat[:, :, :, :].rearrange("p a n j -> p (a n j)")

                    def make_rows(n, par, m, slot):
                        s = (2 * n + par) * STEPS + m
                        own = 3 * s + 1
                        at = par * (NCH * J) + n * J + m
                        f = (featf[:, at:at + 33:32] if isinstance(at, int) else featf[:, bass.ds(at, 2, 32)])
                        if isinstance(s, int) and s == 0:
                            pool.wait_ge(rows_own, 1)
                        else:
                            pool.wait_ge(rows_ready, s)
                            pool.sem_inc(pool_held, 1)
                        nc.gpsimd.tensor_tensor(v1[:, :, :], w1r, f[:, :, None].to_broadcast([P, 2, P]), ALU.mult
                                                ).then_inc(rows_own, 1)
                        pool.wait_ge(rows_own, own + 1)
                        nc.gpsimd.tensor_tensor(v2[:, :, :], v1[:, :, :], b1r, ALU.add).then_inc(rows_own, 1)
                        pool.wait_ge(rows_own, own + 2)
                        nc.gpsimd.tensor_tensor(vh[64:P, :, :], v1[64:P, :, :],
                                                sm("b1_rows")[64:P, None, :].to_broadcast([64, 2, P]), ALU.add
                                                ).then_inc(rows_own, 1)
                        pool.wait_ge(rows_own, own + 3)
                        if not (isinstance(s, int) and s < 2):
                            pool.wait_ge(l1_done, 2 * s - 2)
                        nc.gpsimd.tensor_tensor(tsl[:, slot, :, :], v2[:, :, :], vh[:, :, :].bitcast(fp32),
                                                ALU.subtract).then_inc(rows_ready, 1)

                    def copy_queries(n, r, prev):
                        if prev:
                            pool.wait_ge(seed_done, r)
                            pool.sem_inc(pool_held, 1)
                        dyn = not isinstance(n, int)
                        qsrc = q[:, bass.ds(n, 1), :].rearrange("p a t -> p (a t)") if dyn else q[:, n, :]
                        ksrc = kall[:, bass.ds(n, 1), :].rearrange("p a t -> p (a t)") if dyn else kall[:, n, :]
                        nc.gpsimd.tensor_copy(qs[:, :], qsrc).then_inc(kq_ready, 1)
                        nc.gpsimd.tensor_copy(ks[:, :], ksrc).then_inc(kq_ready, 1)

                    def copy_values(r, pn, pp):
                        if not (isinstance(r, int) and r < 2):
                            pool.wait_ge(pv_done, 2 * r - 2)
                            pool.sem_inc(pool_held, 1)
                        vsrc = (vall[:, pn, pp * DH:(pp + 1) * DH] if isinstance(pn, int) else
                                vall[:, bass.ds(pn, 1), pp * DH:(pp + 1) * DH].rearrange("p a t -> p (a t)"))
                        nc.gpsimd.tensor_copy(vs[:, :], vsrc).then_inc(vs_ready, 1)

                    def step(n, par, m, prev, behind, parity=None):
                        sp_ = m % 2 if parity is None else parity
                        r = 2 * n + par
                        make_rows(n, par, m, sp_)
                        if isinstance(m, int) and m == 1 and par == 0:
                            copy_queries(n, r, prev)
                        if isinstance(m, int) and m == 3 and prev:
                            copy_values(r, n if par == 1 else n - 1, 1 - par)

                    walk(pool, step)
                    copy_values(2 * NCH, NCH - 1, 1)

        qkw = ao[:, 0:CC, :]
        vpw = ao[:, CC:CC + 2, :].rearrange("p a (b c) -> p (a b) c", c=C)
        pw = ow
        aw_in = sem(outer, "aw_in")

        with ExitStack() as c:
            HPP = 2
            PARTS = HC // HPP
            NB = 2 * B
            PW = HPP * P
            raw1 = sb(c, "raw1", [P, CC, PW])
            raw2 = sb(c, "raw2", [P, HPP, C])
            up_h, up_l = (sb(c, x, [P, 2, CC, PW], f32r) for x in ("up_h", "up_l"))
            down_h, down_l = (sb(c, x, [P, 2, HPP, C], f32r) for x in ("down_h", "down_l"))
            xbh, xbl = (sb(c, x, [P, CC, NB, HALF], f32r) for x in ("xbh", "xbl"))
            gl = sb(c, "gl", [P, HPP, HALF])
            xt = gl
            hdh, hdl = (sb(c, x, [P, 2, HPP, HALF], f32r) for x in ("hdh", "hdl"))
            bn2_s = sb(c, "bn2_s", [P, CC])
            pd = pb(c, "pd", [P, CC, HALF])
            pa = pb(c, "pa", [P, 4, HALF])
            raw_in = sem(c, "raw_in")
            split_hi = sem(c, "split_hi")
            split_lo = sem(c, "split_lo")
            bn2_ready = sem(c, "bn2_ready")
            sum_ready = sem(c, "sum_ready")
            summed = sem(c, "summed")
            xbh_ready = sem(c, "xbh_ready")
            xt_ready = sem(c, "xt_ready")
            xb_ready = sem(c, "xb_ready")
            h_ready = sem(c, "h_ready")
            h_free = sem(c, "h_free")
            hdh_ready = sem(c, "hdh_ready")
            hdl_ready = sem(c, "hdl_ready")
            stats_done = sem(c, "stats_done")
            block = c.enter_context(nc.Block())
            D0 = CC * NB

            @block.sync
            def _(sp):
                for e in range(PARTS):
                    if e > 0:
                        sp.wait_ge(split_lo, 2 * e)
                    sp.dma_start(raw1[:, :, :], w1_d[:, :, e * PW:(e + 1) * PW]).then_inc(raw_in, 16)
                    sp.dma_start(raw2[:, :, :], w2_d[:, e * HPP:(e + 1) * HPP, :]).then_inc(raw_in, 16)
                    if e == 1:
                        sp.wait_ge(sum_ready, D0)
                        sp.dma_start(qkw, qkw_d).then_inc(aw_in, 16)
                        sp.dma_start(vpw, vpw_d).then_inc(aw_in, 16)
                        sp.dma_start(pw[:, :, :], pw_d).then_inc(aw_in, 16)

            @block.gpsimd
            def _(pool):
                def split(e, par):
                    if not isinstance(e, int) or e >= 2:
                        pool.wait_ge(sum_ready, CC * NB * (e - 1) + D0)
                    pool.wait_ge(raw_in, 32 * e + 32)
                    pool.sem_inc(pool_held, 1)
                    nc.gpsimd.tensor_copy(up_h[:, par, :, :], raw1[:, :, :]).then_inc(split_hi, 1)
                    nc.gpsimd.tensor_copy(down_h[:, par, :, :], raw2[:, :, :]).then_inc(split_hi, 1)
                    for i, (lo, raw, hi) in enumerate(((up_l, raw1, up_h), (down_l, raw2, down_h))):
                        pool.wait_ge(split_hi, 2 * e + i + 1)
                        pool.sem_inc(pool_held, 1)
                        nc.gpsimd.tensor_tensor(lo[:, par, :, :], raw[:, :, :], hi[:, par, :, :].bitcast(fp32),
                                                ALU.subtract).then_inc(split_lo, 1)

                split(0, 0)
                split(1, 1)
                with pool.Fori(1, PARTS // 2) as r:
                    split(2 * r, 0)
                    split(2 * r + 1, 1)

            @block.tensor
            def _(pe):
                def hidden(e, par, k, s):
                    if k == 0:
                        pe.wait_ge(split_lo, 2 * e + 2)
                    for i in range(HPP):
                        pe.wait_ge(h_free, HPP * s + i + 1)
                        pe.sem_inc(pe_held, 1)
                        for n, (w, x) in enumerate(((up_h, xbh), (up_h, xbl), (up_l, xbh))):
                            for ci in range(CC):
                                mm = nc.tensor.matmul(pa[:, (HPP * k + i) % 4, :], w[:, par, ci, i * P:(i + 1) * P],
                                                      x[:, ci, k, :], start=(n == 0 and ci == 0),
                                                      stop=(n == 2 and ci == CC - 1))
                        mm.then_inc(h_ready, 1)

                def back(e, par, k, s):
                    pe.wait_ge(hdl_ready, HPP * s + HPP)
                    for oc in range(CC):
                        pe.wait_ge(summed, D0 + CC * s + oc - 3)
                        pe.sem_inc(pe_held, 1)
                        for n, (w, x) in enumerate(((down_h, hdh), (down_l, hdh), (down_h, hdl))):
                            for i in range(HPP):
                                mm = nc.tensor.matmul(pd[:, oc, :], w[:, par, i, oc * P:(oc + 1) * P],
                                                      x[:, k % 2, i, :], start=(n == 0 and i == 0),
                                                      stop=(n == 2 and i == HPP - 1))
                        mm.then_inc(sum_ready, 1)

                pe.wait_ge(ow_in, 16)
                for k in range(NB):
                    for oc in range(CC):
                        d = CC * k + oc
                        if d >= 4:
                            pe.wait_ge(summed, d - 3)
                        for ci in range(CC):
                            mm = nc.tensor.matmul(pd[:, oc, :], ow[:, ci, oc * P:(oc + 1) * P],
                                                  ao[:, k // 2 * CC + ci, (k % 2) * HALF:(k % 2 + 1) * HALF],
                                                  start=(ci == 0), stop=(ci == CC - 1))
                        mm.then_inc(sum_ready, 1)
                pe.wait_ge(xb_ready, CC)
                hidden(0, 0, 0, 0)
                pe.wait_ge(xb_ready, CC * NB)

                def two_parts(r, last):
                    for j in range(2 * NB):
                        s = 2 * NB * r + j
                        if not (last and j == 2 * NB - 1):
                            j1 = j + 1
                            hidden(2 * r + j1 // NB, j1 // NB % 2, j1 % NB, s + 1)
                        back(2 * r + j // NB, j // NB, j % NB, s)

                with pe.Fori(0, PARTS // 2 - 1) as r:
                    two_parts(r, False)
                two_parts(PARTS // 2 - 1, True)

            @block.scalar
            def _(act):
                act.sem_inc(h_free, 4)
                act.wait_ge(bn2_ready, 1)
                for k in range(NB):
                    for oc in range(CC):
                        act.wait_ge(summed, CC * k + oc + 1)
                        nc.scalar.activation(xbh[:, oc, k, :], xs[:, oc, k // 2, (k % 2) * HALF:(k % 2 + 1) * HALF],
                                             ACT.Identity, bias=sm("bn2_b", oc, oc + 1), scale=bn2_s[:, oc:oc + 1]
                                             ).then_inc(xbh_ready, 1)

                def part(e):
                    for k in range(NB):
                        s = NB * e + k
                        at = _COLS["mlp_b1"][0]
                        for i in range(HPP):
                            if not (isinstance(e, int) and s == 0):
                                act.wait_ge(hdl_ready, HPP * s + i - 1)
                            act.wait_ge(h_ready, HPP * s + i + 1)
                            act.sem_inc(act_held, 1)
                            bias = (small[:, at + HPP * e + i:at + HPP * e + i + 1] if isinstance(e, int) else
                                    small[:, bass.ds(HPP * e + (at + i), 1)])
                            nc.scalar.activation(gl[:, i, :], pa[:, (HPP * k + i) % 4, :], ACT.Gelu, bias=bias
                                                 ).then_inc(h_free, 1)
                            act.wait_ge(sum_ready, D0 + CC * s - CC)
                            act.wait_ge(h_free, 4 + HPP * s + i + 1)
                            act.sem_inc(act_held, 1)
                            nc.scalar.activation(hdh[:, k % 2, i, :], gl[:, i, :], ACT.Copy).then_inc(hdh_ready, 1)

                act.wait_ge(xb_ready, CC * NB)
                part(0)
                with act.Fori(1, PARTS) as e:
                    part(e)

            @block.vector
            def _(dve):
                def xk(oc, k):
                    return xs[:, oc, k // 2, (k % 2) * HALF:(k % 2 + 1) * HALF]

                nc.vector.tensor_scalar(bn2_s[:, :], sm("bn2_g"), 1.0 / math.sqrt(1.0 + EPS), None, ALU.mult
                                        ).then_inc(bn2_ready, 1)
                dve.wait_ge(bn2_ready, 1)
                for k in range(NB):
                    for oc in range(CC):
                        d = CC * k + oc
                        dve.wait_ge(sum_ready, d + 1)
                        nc.vector.scalar_tensor_tensor(out=xk(oc, k), in0=pd[:, oc, :], scalar=sm("out_b", oc, oc + 1),
                                                       in1=xk(oc, k), op0=ALU.add, op1=ALU.add).then_inc(summed, 1)
                        dve.wait_ge(summed, d + 1)
                        if d >= 2:
                            dve.wait_ge(xb_ready, d - 1)
                        nc.vector.tensor_scalar(xt[:, oc % 2, :], xk(oc, k), bn2_s[:, oc:oc + 1], sm("bn2_b", oc, oc + 1),
                                                ALU.mult, ALU.add).then_inc(xt_ready, 1)
                        dve.wait_ge(xt_ready, d + 1)
                        dve.wait_ge(xbh_ready, d + 1)
                        nc.vector.tensor_tensor(xbl[:, oc, k, :], xt[:, oc % 2, :], xbh[:, oc, k, :].bitcast(fp32),
                                                ALU.subtract).then_inc(xb_ready, 1)

                def hidden_rest(s, k):
                    for i in range(HPP):
                        dve.wait_ge(sum_ready, D0 + CC * s - CC)
                        dve.wait_ge(hdh_ready, HPP * s + i + 1)
                        dve.sem_inc(dve_held, 1)
                        nc.vector.tensor_tensor(hdl[:, k % 2, i, :], gl[:, i, :], hdh[:, k % 2, i, :].bitcast(fp32),
                                                ALU.subtract).then_inc(hdl_ready, 1)

                def add(s, k, last=False):
                    for oc in range(CC):
                        dve.wait_ge(sum_ready, D0 + CC * s + oc + 1)
                        dve.wait_ge(summed, D0 + CC * s + oc - (CC * NB - 1))
                        dve.sem_inc(dve_held, 1)
                        if last:
                            nc.vector.scalar_tensor_tensor(out=xk(oc, k), in0=pd[:, oc, :],
                                                           scalar=sm("mlp_b2", oc, oc + 1), in1=xk(oc, k),
                                                           op0=ALU.add, op1=ALU.add).then_inc(summed, 1)
                        else:
                            nc.vector.tensor_tensor(xk(oc, k), pd[:, oc, :], xk(oc, k), ALU.add).then_inc(summed, 1)
                    if last:
                        dve.wait_ge(summed, D0 + CC * s + CC)
                        for oc in range(CC):
                            ins = nc.vector.bn_stats(stats[:, k // 2, k % 2, oc, :], xk(oc, k))
                        ins.then_inc(stats_done, 1)

                def part(e, last):
                    for k in range(NB):
                        s = NB * e + k
                        hidden_rest(s, k)
                        if not (isinstance(e, int) and s == 0):
                            add(s - 1, (k - 1) % NB, last and k > 0)

                part(0, False)
                with dve.Fori(1, PARTS - 1) as e:
                    part(e, False)
                part(PARTS - 1, True)
                add(NB * PARTS - 1, NB - 1, True)

        with ExitStack() as d:
            att = sb(d, "att", [P, CC, T])
            xg = sb(d, "xg", [P, CC, T])
            qhl = sb(d, "qhl", [P, 2, 2, T], f32r)
            khh = sb(d, "khh", [P, 2, 2, T], f32r)
            kll = sb(d, "kll", [P, 2, 2, T], f32r)
            qlo = sb(d, "qlo", [P, T], f32r)
            va = sb(d, "va", [P, 8, C])
            pr = sb(d, "pr", [P, 4, T])
            ptr = (ao[:, CC + 2:CC + 4, :].rearrange("p a (b c) -> p a b c", c=P), sb(d, "ptr", [P, 2, 8, P]))
            mv = sb(d, "mv", [P, 2, CC * B])
            dev = sb(d, "dev", [P, CC * B])
            gsc = sb(d, "gsc", [P, CC, B])
            gbi = sb(d, "gbi", [P, CC, B])
            mvt = sb(d, "mvt", [P, CC * B, 2])
            rmax = sb(d, "rmax", [P, 4])
            rmx8 = sb(d, "rmx8", [P, 4])
            rsum = sb(d, "rsum", [P, 4])
            rinv = sb(d, "rinv", [P, 4])
            ps = pb(d, "ps", [P, 2, T])
            pp_ = pb(d, "pp_", [P, 2, HALF])
            po = pb(d, "po", [P, HALF])
            pq2 = pb(d, "pq2", [P, HALF])
            banks = [ps[:, i // 2, (i % 2) * HALF:(i % 2 + 1) * HALF] for i in range(4)]

            def made_in(c, t):
                return pq2[:, :] if c % CC or t in (0, 3) else pp_[:, t - 1, :]

            own_steps = sem(d, "own_steps")
            gn_given = sem(d, "gn_given")
            gn_averaged = sem(d, "gn_averaged")
            gn_spread = sem(d, "gn_spread")
            gn_ready = sem(d, "gn_ready")
            xg_ready = sem(d, "xg_ready")
            xg_ready_too = sem(d, "xg_ready_too")
            projected = sem(d, "projected")
            projection_used = sem(d, "projection_used")
            made = sem(d, "made")
            rounded = sem(d, "rounded")
            rest_kept = sem(d, "rest_kept")
            halves_copied = sem(d, "halves_copied")
            qk_done = sem(d, "qk_done")
            max_found = sem(d, "max_found")
            max_scaled = sem(d, "max_scaled")
            exp_summed = sem(d, "exp_summed")
            inverse_ready = sem(d, "inverse_ready")
            probs_ready = sem(d, "probs_ready")
            half_turned = sem(d, "half_turned")
            first_half_copied = sem(d, "first_half_copied")
            second_half_copied = sem(d, "second_half_copied")
            weighted_done = sem(d, "weighted_done")
            weighted_copied = sem(d, "weighted_copied")
            out_ready = sem(d, "out_ready")
            stored = sem(d, "stored")
            block = d.enter_context(nc.Block())
            HP = CC
            TT = T // P
            UN2 = HP * TT * 2
            MAKE_AT = {2: 0, 4: 1, 6: 2, 8: 3}
            VT = 8

            @block.sync
            def _(sp):
                for b in range(B):
                    for hp in range(HP):
                        c = b * HP + hp
                        sp.wait_ge(rounded, 4 * (c + 1))
                        sp.wait_ge(rest_kept, 4 * (c + 1))
                        for hh in range(2):
                            mine, other = slice(hh * DH, (hh + 1) * DH), slice((1 - hh) * DH, (2 - hh) * DH)
                            sp.dma_start(qhl[other, c % 2, hh, :].bitcast(fp32), qlo[mine, :].bitcast(fp32)).then_inc(halves_copied, 16)
                            sp.dma_start(khh[other, c % 2, hh, :].bitcast(fp32), khh[mine, c % 2, hh, :].bitcast(fp32)).then_inc(halves_copied, 16)
                            sp.dma_start(kll[other, c % 2, hh, :].bitcast(fp32), kll[mine, c % 2, hh, :].bitcast(fp32)).then_inc(halves_copied, 16)
                    for i in range(8):
                        sp.wait_ge(out_ready, 8 * b + i + 1)
                        oc, th = i // 2, i % 2
                        sp.dma_start(out_d[:, oc, b, th * HALF:(th + 1) * HALF],
                                     xs[:, oc, b, th * HALF:(th + 1) * HALF]).then_inc(stored, 16)
                sp.wait_ge(stored, 16 * 8 * B)

            @block.tensor
            def _(pe):
                pe.wait_ge(gn_given, 1)
                nc.tensor.matmul(po[:, 0:CC * B], co("group_mean"), mv[:, 0, :], start=True, stop=True
                                 ).then_inc(gn_averaged, 1)
                pe.wait_ge(gn_given, 2)
                nc.tensor.matmul(pq2[:, 0:CC * B], co("group_mean"), dev[:, :], start=True, stop=True
                                 ).then_inc(gn_averaged, 1)
                pe.wait_ge(aw_in, 48)

                def project(b, i, lhs, rhs):
                    n = 2 * VT * b + i
                    if n >= 4:
                        pe.wait_ge(projection_used, n - 3)
                    for ci in range(CC):
                        mm = nc.tensor.matmul(banks[i % 4], lhs(ci), rhs(ci), start=(ci == 0), stop=(ci == CC - 1))
                    mm.then_inc(projected, 1)

                def make(c, t):
                    n = 4 * c + t
                    if c % HP == 0:
                        pe.wait_ge(*((gn_ready, 1) if n == 0 else (rest_kept, 4 * c if t < 3 else n - 2)))
                    else:
                        pe.wait_ge(rest_kept, n)
                    at = (t // 2) * C + (c % HP) * P
                    for ci in range(CC):
                        if c % HP == 0 and t == 0:
                            normed, chunk = (xg_ready, ci) if ci < CC // 2 else (xg_ready_too, ci - CC // 2)
                            pe.wait_ge(normed, CC // 2 * (c // HP) + chunk + 1)
                        mm = nc.tensor.matmul(made_in(c, t), qkw[:, ci, at:at + P], xg[:, ci, (t % 2) * HALF:(t % 2 + 1) * HALF],
                                              start=(ci == 0), stop=(ci == CC - 1))
                    mm.then_inc(made, 1)

                def scores(b, v):
                    u, c, tt, hh = b * UN2 + v, b * HP + v // 16, v // 2 % TT, v % 2
                    if v % 16 == 0:
                        pe.wait_ge(halves_copied, 96 * (c + 1))
                    if v >= 2:
                        pe.wait_ge(exp_summed, u - 1)
                    else:
                        pe.wait_ge(projection_used, 2 * VT * b + VT)
                    for sh in range(2):
                        cols = slice(sh * HALF, (sh + 1) * HALF)
                        nc.tensor.matmul(ps[:, hh, cols], qhl[:, c % 2, hh, tt * P:(tt + 1) * P], khh[:, c % 2, hh, cols],
                                         start=True, stop=False)
                        mm = nc.tensor.matmul(ps[:, hh, cols], qhl[:, c % 2, hh, tt * P:(tt + 1) * P],
                                              kll[:, c % 2, hh, cols], start=False, stop=True)
                    mm.then_inc(qk_done, 1)

                def turn(b, v):
                    u = b * UN2 + v
                    pe.wait_ge(probs_ready, u + 1)
                    if u > 0:
                        pe.wait_ge(first_half_copied, u)
                        pe.wait_ge(second_half_copied, u)
                    for st in range(8):
                        mm = nc.tensor.transpose(pp_[:, st // 4, (st % 4) * P:(st % 4 + 1) * P],
                                                 pr[:, u % 4, st * P:(st + 1) * P], ident)
                        if st % 4 == 3:
                            mm.then_inc(half_turned, 1)

                def weighted(b, g, part):
                    hp, n = g // TT, b * (UN2 // 2) + g
                    if part == 0:
                        pe.wait_ge(first_half_copied, 2 * n + 2)
                        pe.wait_ge(second_half_copied, 2 * n + 2)
                        if n % 4 == 0 and n > 0:
                            pe.wait_ge(weighted_copied, n // 4)
                    for st in range(4 * part, 4 * part + 4):
                        for hh in range(2):
                            at = (2 * hp + hh) * DH
                            mm = nc.tensor.matmul(po[hh * DH:(hh + 1) * DH, (n % 4) * P:(n % 4 + 1) * P],
                                                  va[:, st, at:at + DH], ptr[n % 2][:, hh, st, :],
                                                  start=(st == 0), stop=(st == 7), skip_group_check=True)
                    if part == 1:
                        mm.then_inc(weighted_done, 1)

                for b in range(B):
                    for t in range(4):
                        make(b * HP, t)
                    for i in range(VT):
                        project(b, i, lambda ci: xg[:, ci, i * P:(i + 1) * P], lambda ci: vpw[:, ci, :])
                    for v in range(UN2):
                        scores(b, v)
                        if v >= 5:
                            weighted(b, (v - 5) // 2, 1 - v % 2)
                        if v >= 2:
                            turn(b, v - 2)
                        if v % 16 in MAKE_AT and v // 16 < HP - 1:
                            make(b * HP + v // 16 + 1, MAKE_AT[v % 16])
                    weighted(b, UN2 // 2 - 3, 1)
                    turn(b, UN2 - 2)
                    weighted(b, UN2 // 2 - 2, 0)
                    turn(b, UN2 - 1)
                    weighted(b, UN2 // 2 - 2, 1)
                    weighted(b, UN2 // 2 - 1, 0)
                    weighted(b, UN2 // 2 - 1, 1)
                    pe.wait_ge(weighted_copied, (UN2 // 8) * (b + 1))
                    for i in range(8):
                        oc, th = i // 2, i % 2
                        project(b, VT + i, lambda ci: pw[:, ci, oc * P:(oc + 1) * P],
                                lambda ci: att[:, ci, th * HALF:(th + 1) * HALF])

            @block.scalar
            def _(act):
                act.wait_ge(gn_spread, 1)
                nc.scalar.activation(gsc[:, :, :], gsc[:, :, :], ACT.Sqrt).then_inc(gn_spread, 1)

                def round_(c, t):
                    n = 4 * c + t
                    act.wait_ge(made, n + 1)
                    dst, bias = (qhl, "q_b") if t < 2 else (khh, "k_b")
                    for hh in range(2):
                        mine = slice(hh * DH, (hh + 1) * DH)
                        at = _COLS[bias][0] + c % HP
                        ins = nc.scalar.activation(dst[mine, c % 2, hh, (t % 2) * HALF:(t % 2 + 1) * HALF],
                                                   made_in(c, t)[mine, :],
                                                   ACT.Identity, bias=small[mine, at:at + 1])
                    ins.then_inc(rounded, 1)

                def half_copy(b, v):
                    u = b * UN2 + v
                    act.wait_ge(half_turned, 2 * u + 1)
                    if u >= 4:
                        act.wait_ge(weighted_done, (u - 4) // 2 + 1)
                    nc.scalar.activation(ptr[u // 2 % 2][:, u % 2, 0:4, :], pp_[:, 0, :].rearrange("p (a b) -> p a b", a=4),
                                         ACT.Copy).then_inc(first_half_copied, 1)

                def out_copy(b, g):
                    n = b * (UN2 // 2) + g
                    act.wait_ge(weighted_done, n + 1)
                    nc.scalar.activation(att[:, g // TT, (g // 4 % 2) * HALF:(g // 4 % 2 + 1) * HALF], po[:, :],
                                         ACT.Copy).then_inc(weighted_copied, 1)

                for b in range(B):
                    act.wait_ge(gn_ready, 1)
                    for cc in range(CC // 2):
                        if b > 0:
                            act.wait_ge(projection_used, 2 * VT * b - 2 * (CC - 1 - cc))
                        nc.scalar.activation(xg[:, cc, :], xs[:, cc, b, :], ACT.Identity, bias=gbi[:, cc, b:b + 1],
                                             scale=gsc[:, cc, b:b + 1]).then_inc(xg_ready, 1)
                    for t in range(4):
                        round_(b * HP, t)
                    for v in range(UN2):
                        u = b * UN2 + v
                        if v % 16 - 1 in MAKE_AT and v // 16 < HP - 1:
                            round_(b * HP + v // 16 + 1, MAKE_AT[v % 16 - 1])
                        if v >= 12 and (v - 12) % 8 == 0:
                            out_copy(b, v // 2 - 3)
                        if v >= 2:
                            half_copy(b, v - 2)
                        act.wait_ge(max_scaled, u + 1)
                        if u >= 4:
                            act.wait_ge(half_turned, 2 * u - 6)
                        nc.scalar.activation(pr[:, u % 4, :], ps[:, u % 2, :], ACT.Exp, bias=rmx8[:, u % 4:u % 4 + 1],
                                             scale=DH ** -0.5, accum_out=rsum[:, u % 4:u % 4 + 1]).then_inc(exp_summed, 1)
                    half_copy(b, UN2 - 2)
                    half_copy(b, UN2 - 1)
                    out_copy(b, UN2 // 2 - 1)

            @block.vector
            def _(dve):
                own = 0

                def chain(ins):
                    nonlocal own
                    own += 1
                    ins.then_inc(own_steps, 1)
                    dve.wait_ge(own_steps, own)

                for i in range(CC * B):
                    last = nc.vector.bn_aggr(mvt[:, i, :], stats[:, i % B, :, i // B, :])
                chain(last)
                nc.vector.tensor_copy(mv[:, 0, :], mvt[:, :, 0]).then_inc(gn_given, 1)
                dve.wait_ge(gn_averaged, 1)
                chain(nc.vector.tensor_tensor(mv[:, 1, :], po[:, 0:8], mvt[:, :, 0], ALU.subtract))
                chain(nc.vector.tensor_tensor(mv[:, 1, :], mv[:, 1, :], mv[:, 1, :], ALU.mult))
                nc.vector.tensor_tensor(dev[:, :], mv[:, 1, :], mvt[:, :, 1], ALU.add).then_inc(gn_given, 1)
                dve.wait_ge(gn_averaged, 2)
                gs = gsc[:, :, :].rearrange("p a b -> p (a b)")
                nc.vector.tensor_scalar(gs, pq2[:, 0:8], EPS, None, ALU.add).then_inc(gn_spread, 1)
                dve.wait_ge(gn_spread, 2)
                chain(nc.vector.reciprocal(gs, gs))
                chain(nc.vector.tensor_tensor(gsc[:, :, :], gsc[:, :, :], sm("gn_w")[:, :, None].to_broadcast([P, CC, B]),
                                              ALU.mult))
                gb = gbi[:, :, :].rearrange("p a b -> p (a b)")
                chain(nc.vector.tensor_tensor(gb, gs, po[:, 0:8], ALU.mult))
                nc.vector.tensor_tensor(gbi[:, :, :], sm("gn_b")[:, :, None].to_broadcast([P, CC, B]), gbi[:, :, :],
                                        ALU.subtract).then_inc(gn_ready, 1)

                def keep_rest(c, t):
                    n = 4 * c + t
                    dve.wait_ge(rounded, n + 1)
                    if t == 0 and c > 0:
                        dve.wait_ge(halves_copied, 96 * c)
                    cols = slice((t % 2) * HALF, (t % 2 + 1) * HALF)
                    for hh in range(2):
                        mine = slice(hh * DH, (hh + 1) * DH)
                        at = _COLS["q_b" if t < 2 else "k_b"][0] + c % HP
                        hi = (qhl if t < 2 else khh)[mine, c % 2, hh, cols]
                        lo = qlo[mine, cols] if t < 2 else kll[mine, c % 2, hh, cols]
                        ins = nc.vector.scalar_tensor_tensor(out=lo, in0=made_in(c, t)[mine, :], scalar=small[mine, at:at + 1],
                                                             in1=hi.bitcast(fp32), op0=ALU.add, op1=ALU.subtract)
                    ins.then_inc(rest_kept, 1)

                def half_copy(b, v):
                    u = b * UN2 + v
                    dve.wait_ge(half_turned, 2 * u + 2)
                    if u >= 4:
                        dve.wait_ge(weighted_done, (u - 4) // 2 + 1)
                    nc.vector.tensor_copy(ptr[u // 2 % 2][:, u % 2, 4:8, :], pp_[:, 1, :].rearrange("p (a b) -> p a b", a=4)
                                          ).then_inc(second_half_copied, 1)

                def inverse(b, v):
                    u = b * UN2 + v
                    w = slice(u % 4, u % 4 + 1)
                    dve.wait_ge(exp_summed, u + 1)
                    if u >= 4:
                        dve.wait_ge(probs_ready, u - 3)
                    nc.vector.reciprocal(rinv[:, w], rsum[:, w]).then_inc(inverse_ready, 1)

                for b in range(B):
                    dve.wait_ge(gn_ready, 1)
                    for cc in range(CC // 2, CC):
                        if b > 0:
                            dve.wait_ge(projection_used, 2 * VT * b - 2 * (CC - 1 - cc))
                        nc.vector.tensor_scalar(xg[:, cc, :], xs[:, cc, b, :], gsc[:, cc, b:b + 1], gbi[:, cc, b:b + 1],
                                                ALU.mult, ALU.add).then_inc(xg_ready_too, 1)
                    for t in range(4):
                        keep_rest(b * HP, t)
                    for i in range(VT):
                        dve.wait_ge(projected, 2 * VT * b + i + 1)
                        nc.vector.tensor_tensor(va[:, i, :], banks[i % 4], sm("v_b"), ALU.add).then_inc(projection_used, 1)
                    for v in range(UN2):
                        u = b * UN2 + v
                        w = slice(u % 4, u % 4 + 1)
                        dve.wait_ge(qk_done, u + 1)
                        nc.vector.tensor_reduce(rmax[:, w], ps[:, u % 2, :], X, ALU.max, negate=True).then_inc(max_found, 1)
                        dve.wait_ge(max_found, u + 1)
                        if u >= 4:
                            dve.wait_ge(exp_summed, u - 3)
                        nc.vector.tensor_scalar(rmx8[:, w], rmax[:, w], DH ** -0.5, None, ALU.mult).then_inc(max_scaled, 1)
                        if v >= 1:
                            inverse(b, v - 1)
                        if v % 16 - 1 in MAKE_AT and v // 16 < HP - 1:
                            keep_rest(b * HP + v // 16 + 1, MAKE_AT[v % 16 - 1])
                        if v >= 2:
                            half_copy(b, v - 2)
                    inverse(b, UN2 - 1)
                    half_copy(b, UN2 - 2)
                    half_copy(b, UN2 - 1)
                    for i in range(8):
                        oc, th = i // 2, i % 2
                        cols = slice(th * HALF, (th + 1) * HALF)
                        dve.wait_ge(projected, 2 * VT * b + VT + i + 1)
                        dve.wait_ge(xg_ready, CC // 2 * (b + 1))
                        dve.wait_ge(xg_ready_too, CC // 2 * (b + 1))
                        nc.vector.scalar_tensor_tensor(out=xs[:, oc, b, cols], in0=banks[i % 4],
                                                       scalar=sm("proj_b", oc, oc + 1), in1=xg[:, oc, cols],
                                                       op0=ALU.add, op1=ALU.add).then_inc(projection_used, 1)
                        dve.wait_ge(projection_used, 2 * VT * b + VT + i + 1)
                        dve.sem_inc(out_ready, 1)

            @block.gpsimd
            def _(pool):
                for u in range(B * UN2):
                    pool.wait_ge(inverse_ready, u + 1)
                    nc.gpsimd.tensor_scalar(pr[:, u % 4, :], pr[:, u % 4, :], rinv[:, u % 4:u % 4 + 1],
                                            1.0, ALU.mult, ALU.mult).then_inc(probs_ready, 1)


def kernel(**inputs):
    import concourse.bacc as bacc
    from concourse import mybir as _mybir
    from concourse.bass_utils import run_bass_kernel_spmd

    def arr(name):
        return np.asarray(inputs[name])

    L0, L1 = "L0_conv_", "L1_conv_"
    cols = lambda v, k: v.reshape(k, P).T
    small = np.zeros((P, SMALL), np.float32)

    def put(name, v):
        at, w = _COLS[name]
        small[:, at:at + w] = v

    for name, key, k in (("bn1_g", L0 + "bn1_g", CC), ("bn1_b", L0 + "bn1_b", CC), ("bn2_g", L0 + "bn2_g", CC),
                         ("bn2_b", L0 + "bn2_b", CC), ("out_b", L0 + "out_b", CC), ("mlp_b2", L0 + "mlp_b2", CC),
                         ("gn_w", L1 + "gn_w", CC), ("gn_b", L1 + "gn_b", CC), ("proj_b", L1 + "proj_b", CC),
                         ("mlp_b1", L0 + "mlp_b1", HC)):
        put(name, cols(arr(key), k))
    qkv_b = arr(L1 + "qkv_b").reshape(G, 3, DH)
    put("q_b", cols(qkv_b[:, 0].reshape(C), CC))
    put("k_b", cols(qkv_b[:, 1].reshape(C), CC))
    put("v_b", np.broadcast_to(qkv_b[:, 2].reshape(1, C), (P, C)))
    both = lambda v: np.concatenate([v, v], axis=0)
    put("dw_w", both(arr(L0 + "off_dw_w").reshape(DH, 36)))
    put("dw_b", both(arr(L0 + "off_dw_b").reshape(DH, 1)))
    put("cpb_b2", arr(L0 + "cpb_b2").reshape(P, 1))
    put("cpb_b3", np.broadcast_to(arr(L0 + "cpb_b3").reshape(1, 1), (P, 1)))
    w3 = np.zeros((P, 63), np.float32)
    w3[:, 31] = arr(L0 + "cpb_w3")[:, 0]
    put("w3_window", w3)
    put("cpb_w2", arr(L0 + "cpb_w2"))
    w1c = arr(L0 + "cpb_w1")
    axis = (np.arange(P) // 32) % 2
    put("w1_rows", w1c[axis])
    b1_rows = np.zeros((P, P), np.float32)
    b1_rows[axis == 1] = arr(L0 + "cpb_b1")
    put("b1_rows", b1_rows)
    pwo = arr(L0 + "off_pw_w")
    put("pw_feat", both(pwo[axis].T))
    put("pw_x", both(pwo[np.zeros(P, int)].T))
    put("pw_y", both(pwo[np.ones(P, int)].T))

    const = np.zeros((P, NCONST), np.float32)

    def putc(name, v):
        at, w = _CONST[name]
        const[:, at:at + w] = v

    p = np.arange(P)
    j = np.arange(J)
    putc("ident", np.eye(P, dtype=np.float32))
    putc("grid_x", np.broadcast_to(j % WD, (P, J)))
    putc("grid_y", np.broadcast_to(j // WD, (P, J)))
    putc("grid_feat", np.where(axis[:, None] == 0, j % WD, j // WD))
    putc("query_pos", (np.float32(2.0) * (p % 32).astype(np.float32) / np.float32(WW - 1) - np.float32(1.0))[:, None])
    putc("neg_ix", -(p % 32)[:, None])
    putc("neg_iy", -(4 * np.arange(8)[None, :] + (p // 32)[:, None]))
    putc("group_mean", (p[:, None] // GCH == p[None, :] // GCH) / GCH)
    i = np.arange(T)
    onehot = np.zeros((P, T), np.float32)
    for part in range(2):
        onehot[part * 64 + i % WW, i] = 1
        onehot[part * 64 + 32 + i // WW, i] = 1

    def diagonal(w):
        o = np.zeros((P, CC, P), np.float32)
        for g in range(G):
            a = (g % 2) * DH
            o[a:a + DH, g // 2, a:a + DH] = w[g].T
        return o

    rows = lambda w, k: w.reshape(k, P, -1).transpose(1, 0, 2)
    qkv_w = arr(L1 + "qkv_w").reshape(G, 3, DH, C)
    qk_w = np.concatenate([qkv_w[:, 0].reshape(C, C).T, qkv_w[:, 1].reshape(C, C).T], axis=1)
    data = [
        ("x", arr("x").reshape(B, CC, P, T).transpose(2, 1, 0, 3)),
        ("small", small), ("const", const), ("onehot", onehot),
        ("qw", diagonal(arr(L0 + "qw"))), ("kw", diagonal(arr(L0 + "kw"))), ("vw", diagonal(arr(L0 + "vw"))),
        ("ow", rows(arr(L0 + "out_w").T, CC)), ("w1", rows(arr(L0 + "mlp_w1").T, CC)),
        ("w2", rows(arr(L0 + "mlp_w2").T, HC)), ("qkw", rows(qk_w, CC)),
        ("vpw", rows(qkv_w[:, 2].reshape(C, C).T, CC)), ("pw", rows(arr(L1 + "proj_w").T, CC)),
    ]
    nc = bacc.Bacc("TRN2", target_bir_lowering=False, num_devices=1)
    arrays, args = {}, []
    for name, a in data:
        a = np.ascontiguousarray(a)
        arrays[f"in_{name}"] = a
        args.append(nc.dram_tensor(f"in_{name}", a.shape, _mybir.dt.from_np(a.dtype), kind="ExternalInput").ap())
    out = nc.dram_tensor("out", (P, CC, B, T), _mybir.dt.float32, kind="ExternalOutput").ap()
    deformable_then_attention(nc, *args, out)
    r = run_bass_kernel_spmd(nc, [arrays], core_ids=[0])
    got = r.results[0]["out"]
    return np.ascontiguousarray(got.transpose(2, 1, 0, 3)).reshape(B, C, HH, WW)
```
